# Optimizing a Trainium2 kernel written in Bass

```python
import numpy as np
import jax
import jax.numpy as jnp

def _softmax(x, axis=-1):
    return jax.nn.softmax(x, axis=axis)

def _gelu(x):
    return jax.nn.gelu(x, approximate=True)

def _silu(x):
    return jax.nn.silu(x)

def _sigmoid(x):
    return jax.nn.sigmoid(x)

def _layernorm(x, axis=-1, eps=1e-05):
    m = jnp.mean(x, axis=axis, keepdims=True)
    v = jnp.var(x, axis=axis, keepdims=True)
    return (x - m) / jnp.sqrt(v + eps)

def _scatter_add(tgt, idx, src, axis=0):
    return tgt.at[idx].add(src)

def _segment_sum(src, seg, n):
    return jax.ops.segment_sum(src, seg, n)
kernel_name = 'mk_gnn_resnorm_d4_gnn_r16_fbf783'

def setup_inputs(seed: int=0):
    np.random.seed(seed)
    _w = jnp.asarray

    def _rec_inputs():
        import jax
        import jax.numpy as jnp
        _gk = jax.random.key(seed)
        x = -0.0001538 + 1 * jax.random.normal(jax.random.fold_in(_gk, 1), (512, 768), jnp.float32)
        _s = jax.random.randint(jax.random.fold_in(_gk, 2), (4096,), 0, 512, jnp.int32)
        _d = jax.random.randint(jax.random.fold_in(_gk, 3), (4096,), 0, 512, jnp.int32)
        _loop = jnp.arange(512, dtype=jnp.int32)
        src = jnp.concatenate([_s, _d, _loop])
        dst = jnp.concatenate([_d, _s, _loop])
        _o = jnp.argsort(dst, stable=True)
        src = src[_o]
        dst = dst[_o]
        edge_type_3 = jax.random.randint(jax.random.fold_in(_gk, 12), (8704,), 0, 3, jnp.int32)
        edge_type_4 = jax.random.randint(jax.random.fold_in(_gk, 13), (8704,), 0, 4, jnp.int32)
        return (x, src, dst, edge_type_3, edge_type_4)
    x, src, dst, edge_type_3, edge_type_4 = _rec_inputs()

    def _L0_gnn_setup():
        import jax, jax.numpy as jnp
        import numpy as np
        NEG_SLOPE = 0.2
        EPS = 1e-16
        N_NODES = 512
        N_EDGES = 4096
        D_IN = 768
        D_HID = 768
        H1 = 8
        H2 = 1

        def gat_layer(x, W, a_s, a_d, b, edge_index, concat):
            n = x.shape[0]
            H, C = a_s.shape
            h = (x @ W).reshape(n, H, C)
            src, dst = (edge_index[0], edge_index[1])
            alpha_s = jnp.einsum('nhc,hc->nh', h, a_s)
            alpha_d = jnp.einsum('nhc,hc->nh', h, a_d)
            e = jax.nn.leaky_relu(alpha_s[src] + alpha_d[dst], NEG_SLOPE)
            m = jax.ops.segment_max(e, dst, num_segments=n)
            e = jnp.exp(e - m[dst])
            denom = jax.ops.segment_sum(e, dst, num_segments=n)
            alpha = e / (denom[dst] + EPS)
            msg = h[src] * alpha[:, :, None]
            out = jax.ops.segment_sum(msg, dst, num_segments=n)
            out = out.reshape(n, H * C) if concat else out.mean(axis=1)
            return out + b
        key = jax.random.key(seed)
        ks = jax.random.split(key, 10)
        x = jax.random.normal(ks[0], (N_NODES, D_IN), dtype=jnp.float32)
        edge_list = jax.random.randint(ks[1], (2, N_EDGES), 0, N_NODES, dtype=jnp.int32)
        s = 0.05
        W1 = jax.random.normal(ks[2], (D_IN, H1 * D_HID), dtype=jnp.float32) * s
        a_src1 = jax.random.normal(ks[3], (H1, D_HID), dtype=jnp.float32) * s
        a_dst1 = jax.random.normal(ks[4], (H1, D_HID), dtype=jnp.float32) * s
        b1 = jnp.zeros((H1 * D_HID,), dtype=jnp.float32)
        W2 = jax.random.normal(ks[5], (H1 * D_HID, H2 * D_HID), dtype=jnp.float32) * s
        a_src2 = jax.random.normal(ks[6], (H2, D_HID), dtype=jnp.float32) * s
        a_dst2 = jax.random.normal(ks[7], (H2, D_HID), dtype=jnp.float32) * s
        b2 = jnp.zeros((H2 * D_HID,), dtype=jnp.float32)
        return {'x': x, 'W1': W1, 'a_src1': a_src1, 'a_dst1': a_dst1, 'b1': b1, 'W2': W2, 'a_src2': a_src2, 'a_dst2': a_dst2, 'b2': b2, 'edge_list': edge_list}
    _L0_gnn_all = _L0_gnn_setup()
    _L0_gnn_in = {k: v for k, v in _L0_gnn_all.items() if k in ('W1', 'a_src1', 'a_dst1', 'b1', 'W2', 'a_src2', 'a_dst2', 'b2')}
    del _L0_gnn_all

    def _L1_gnn_setup():
        import jax, jax.numpy as jnp
        import numpy as np
        NEG_SLOPE = 0.2
        EPS = 1e-16
        N_NODES = 2048
        N_EDGES = 10000
        DIM = 768
        HEADS1 = 4
        OUT1 = DIM // HEADS1
        HEADS2 = 1
        OUT2 = DIM
        N_REL = 3

        def rgat_conv(x, W, q, k, b, src, dst, etype, heads, out_ch, n_nodes):
            xr = jnp.einsum('nd,rdf->rnf', x, W)
            oi = xr[etype, dst]
            oj = xr[etype, src]
            qi = oi @ q
            kj = oj @ k
            alpha = jax.nn.leaky_relu(qi + kj, NEG_SLOPE)
            m = jax.ops.segment_max(alpha, dst, num_segments=n_nodes)
            e = jnp.exp(alpha - m[dst])
            z = jax.ops.segment_sum(e, dst, num_segments=n_nodes)
            a = e / (z[dst] + EPS)
            msg = (a[:, :, None] * oj.reshape(-1, heads, out_ch)).reshape(-1, heads * out_ch)
            out = jax.ops.segment_sum(msg, dst, num_segments=n_nodes)
            return out + b
        key = jax.random.key(seed)
        ks = jax.random.split(key, 12)
        s = 0.02
        return {'x': jax.random.normal(ks[0], (N_NODES, DIM), dtype=jnp.float32), 'edge_index': jax.random.randint(ks[1], (2, N_EDGES), 0, N_NODES, dtype=jnp.int64), 'edge_type': jax.random.randint(ks[2], (N_EDGES,), 0, N_REL, dtype=jnp.int64), 'W1': jax.random.normal(ks[3], (N_REL, DIM, HEADS1 * OUT1), dtype=jnp.float32) * s, 'q1': jax.random.normal(ks[4], (HEADS1 * OUT1, HEADS1), dtype=jnp.float32) * s, 'k1': jax.random.normal(ks[5], (HEADS1 * OUT1, HEADS1), dtype=jnp.float32) * s, 'b1': jnp.zeros((HEADS1 * OUT1,), dtype=jnp.float32), 'W2': jax.random.normal(ks[6], (N_REL, DIM, HEADS2 * OUT2), dtype=jnp.float32) * s, 'q2': jax.random.normal(ks[7], (HEADS2 * OUT2, HEADS2), dtype=jnp.float32) * s, 'k2': jax.random.normal(ks[8], (HEADS2 * OUT2, HEADS2), dtype=jnp.float32) * s, 'b2': jnp.zeros((HEADS2 * OUT2,), dtype=jnp.float32)}
    _L1_gnn_all = _L1_gnn_setup()
    _L1_gnn_in = {k: v for k, v in _L1_gnn_all.items() if k in ('W1', 'q1', 'k1', 'b1', 'W2', 'q2', 'k2', 'b2')}
    del _L1_gnn_all

    def _L2_gnn_setup():
        import jax, jax.numpy as jnp
        import numpy as np
        N_NODES = 1250
        N_EDGES = 6250
        D = 768
        NUM_REL = 4

        def _rgcn_conv(x, weight, root, bias, src, dst, etype):
            n = x.shape[0]
            out = x @ root + bias
            for r in range(NUM_REL):
                sel = etype == r
                self_f = sel.astype(x.dtype)
                deg = jnp.zeros((n,), x.dtype).at[dst].add(self_f)
                norm = jnp.where(sel, 1.0 / jnp.maximum(deg[dst], 1.0), 0.0)
                h_r = x @ weight[r]
                msgs = h_r[src] * norm[:, None]
                out = out + jax.ops.segment_sum(msgs, dst, num_segments=n)
            return out
        key = jax.random.key(seed)
        ks = jax.random.split(key, 12)
        entity = jax.random.normal(ks[0], (N_NODES, D), dtype=jnp.float32)
        edge_index = jax.random.randint(ks[1], (2, N_EDGES), 0, N_NODES, dtype=jnp.int64)
        edge_type = jax.random.randint(ks[2], (N_EDGES,), 0, NUM_REL, dtype=jnp.int64)
        s = 0.02
        params = {}
        for i, layer in enumerate(['1', '2', '3']):
            params[f'W{layer}'] = jax.random.normal(ks[3 + 3 * i], (NUM_REL, D, D), dtype=jnp.float32) * s
            params[f'root{layer}'] = jax.random.normal(ks[4 + 3 * i], (D, D), dtype=jnp.float32) * s
            params[f'b{layer}'] = jnp.zeros((D,), dtype=jnp.float32)
        return {'entity': entity, 'edge_index': edge_index, 'edge_type': edge_type, **params}
    _L2_gnn_all = _L2_gnn_setup()
    _L2_gnn_in = {k: v for k, v in _L2_gnn_all.items() if k in ('W1', 'root1', 'b1', 'W2', 'root2', 'b2', 'W3', 'root3', 'b3')}
    del _L2_gnn_all

    def _L3_gnn_setup():
        import jax, jax.numpy as jnp
        import numpy as np
        N_NODES = 625
        D = 768
        N_EDGES = 10000

        def gcn_conv(x, W, b, src, dst, n_nodes):
            h = x @ W
            deg = jax.ops.segment_sum(jnp.ones_like(dst, dtype=h.dtype), dst, num_segments=n_nodes)
            dinv = jnp.where(deg > 0, jax.lax.rsqrt(deg), 0.0)
            norm = dinv[src] * dinv[dst]
            msgs = h[src] * norm[:, None]
            out = jax.ops.segment_sum(msgs, dst, num_segments=n_nodes)
            return out + b

        def add_self_loops(edge_index, n_nodes):
            loop = jnp.arange(n_nodes, dtype=edge_index.dtype)
            src = jnp.concatenate([edge_index[0], loop])
            dst = jnp.concatenate([edge_index[1], loop])
            return (src, dst)
        key = jax.random.key(seed)
        k1, k2, k3, k4 = jax.random.split(key, 4)
        x = jax.random.normal(k1, (N_NODES, D), dtype=jnp.float32)
        edge_index = jax.random.randint(k2, (2, N_EDGES), 0, N_NODES, dtype=jnp.int32)
        glorot = float(np.sqrt(6.0 / (D + D)))
        W1 = jax.random.uniform(k3, (D, D), jnp.float32, -glorot, glorot)
        W2 = jax.random.uniform(k4, (D, D), jnp.float32, -glorot, glorot)
        b1 = jnp.zeros((D,), jnp.float32)
        b2 = jnp.zeros((D,), jnp.float32)
        return {'x': x, 'W1': W1, 'b1': b1, 'W2': W2, 'b2': b2, 'edge_index': edge_index}
    _L3_gnn_all = _L3_gnn_setup()
    _L3_gnn_in = {k: v for k, v in _L3_gnn_all.items() if k in ('W1', 'b1', 'W2', 'b2')}
    del _L3_gnn_all
    return {'x': x, 'src': src, 'dst': dst, 'edge_type_3': edge_type_3, 'edge_type_4': edge_type_4, 'L0_gnn_W1': _L0_gnn_in['W1'], 'L0_gnn_a_src1': _L0_gnn_in['a_src1'], 'L0_gnn_a_dst1': _L0_gnn_in['a_dst1'], 'L0_gnn_b1': _L0_gnn_in['b1'], 'L0_gnn_W2': _L0_gnn_in['W2'], 'L0_gnn_a_src2': _L0_gnn_in['a_src2'], 'L0_gnn_a_dst2': _L0_gnn_in['a_dst2'], 'L0_gnn_b2': _L0_gnn_in['b2'], 'L1_gnn_W1': _L1_gnn_in['W1'], 'L1_gnn_q1': _L1_gnn_in['q1'], 'L1_gnn_k1': _L1_gnn_in['k1'], 'L1_gnn_b1': _L1_gnn_in['b1'], 'L1_gnn_W2': _L1_gnn_in['W2'], 'L1_gnn_q2': _L1_gnn_in['q2'], 'L1_gnn_k2': _L1_gnn_in['k2'], 'L1_gnn_b2': _L1_gnn_in['b2'], 'L2_gnn_W1': _L2_gnn_in['W1'], 'L2_gnn_root1': _L2_gnn_in['root1'], 'L2_gnn_b1': _L2_gnn_in['b1'], 'L2_gnn_W2': _L2_gnn_in['W2'], 'L2_gnn_root2': _L2_gnn_in['root2'], 'L2_gnn_b2': _L2_gnn_in['b2'], 'L2_gnn_W3': _L2_gnn_in['W3'], 'L2_gnn_root3': _L2_gnn_in['root3'], 'L2_gnn_b3': _L2_gnn_in['b3'], 'L3_gnn_W1': _L3_gnn_in['W1'], 'L3_gnn_b1': _L3_gnn_in['b1'], 'L3_gnn_W2': _L3_gnn_in['W2'], 'L3_gnn_b2': _L3_gnn_in['b2']}

def reference(x, src, dst, edge_type_3, edge_type_4, L0_gnn_W1, L0_gnn_a_src1, L0_gnn_a_dst1, L0_gnn_b1, L0_gnn_W2, L0_gnn_a_src2, L0_gnn_a_dst2, L0_gnn_b2, L1_gnn_W1, L1_gnn_q1, L1_gnn_k1, L1_gnn_b1, L1_gnn_W2, L1_gnn_q2, L1_gnn_k2, L1_gnn_b2, L2_gnn_W1, L2_gnn_root1, L2_gnn_b1, L2_gnn_W2, L2_gnn_root2, L2_gnn_b2, L2_gnn_W3, L2_gnn_root3, L2_gnn_b3, L3_gnn_W1, L3_gnn_b1, L3_gnn_W2, L3_gnn_b2):
    import jax
    import jax.numpy as jnp

    def _L0_gnn_ref(x, W1, a_src1, a_dst1, b1, W2, a_src2, a_dst2, b2, edge_list):
        import jax, jax.numpy as jnp
        import numpy as np
        NEG_SLOPE = 0.2
        EPS = 1e-16
        N_NODES = 512
        N_EDGES = 4096
        D_IN = 768
        D_HID = 768
        H1 = 8
        H2 = 1

        def gat_layer(x, W, a_s, a_d, b, edge_index, concat):
            n = x.shape[0]
            H, C = a_s.shape
            h = (x @ W).reshape(n, H, C)
            src, dst = (edge_index[0], edge_index[1])
            alpha_s = jnp.einsum('nhc,hc->nh', h, a_s)
            alpha_d = jnp.einsum('nhc,hc->nh', h, a_d)
            e = jax.nn.leaky_relu(alpha_s[src] + alpha_d[dst], NEG_SLOPE)
            m = jax.ops.segment_max(e, dst, num_segments=n)
            e = jnp.exp(e - m[dst])
            denom = jax.ops.segment_sum(e, dst, num_segments=n)
            alpha = e / (denom[dst] + EPS)
            msg = h[src] * alpha[:, :, None]
            out = jax.ops.segment_sum(msg, dst, num_segments=n)
            out = out.reshape(n, H * C) if concat else out.mean(axis=1)
            return out + b
        h = gat_layer(x, W1, a_src1, a_dst1, b1, edge_list, concat=True)
        h = jax.nn.elu(h)
        out = gat_layer(h, W2, a_src2, a_dst2, b2, edge_list, concat=True)
        return out

    def _L1_gnn_ref(x, edge_index, edge_type, W1, q1, k1, b1, W2, q2, k2, b2):
        import jax, jax.numpy as jnp
        import numpy as np
        NEG_SLOPE = 0.2
        EPS = 1e-16
        N_NODES = 2048
        N_EDGES = 10000
        DIM = 768
        HEADS1 = 4
        OUT1 = DIM // HEADS1
        HEADS2 = 1
        OUT2 = DIM
        N_REL = 3

        def rgat_conv(x, W, q, k, b, src, dst, etype, heads, out_ch, n_nodes):
            xr = jnp.einsum('nd,rdf->rnf', x, W)
            oi = xr[etype, dst]
            oj = xr[etype, src]
            qi = oi @ q
            kj = oj @ k
            alpha = jax.nn.leaky_relu(qi + kj, NEG_SLOPE)
            m = jax.ops.segment_max(alpha, dst, num_segments=n_nodes)
            e = jnp.exp(alpha - m[dst])
            z = jax.ops.segment_sum(e, dst, num_segments=n_nodes)
            a = e / (z[dst] + EPS)
            msg = (a[:, :, None] * oj.reshape(-1, heads, out_ch)).reshape(-1, heads * out_ch)
            out = jax.ops.segment_sum(msg, dst, num_segments=n_nodes)
            return out + b
        src, dst = (edge_index[0], edge_index[1])
        n = x.shape[0]
        h = rgat_conv(x, W1, q1, k1, b1, src, dst, edge_type, HEADS1, OUT1, n)
        h = jax.nn.elu(h)
        out = rgat_conv(h, W2, q2, k2, b2, src, dst, edge_type, HEADS2, OUT2, n)
        return out

    def _L2_gnn_ref(entity, edge_index, edge_type, W1, root1, b1, W2, root2, b2, W3, root3, b3):
        import jax, jax.numpy as jnp
        import numpy as np
        N_NODES = 1250
        N_EDGES = 6250
        D = 768
        NUM_REL = 4

        def _rgcn_conv(x, weight, root, bias, src, dst, etype):
            n = x.shape[0]
            out = x @ root + bias
            for r in range(NUM_REL):
                sel = etype == r
                self_f = sel.astype(x.dtype)
                deg = jnp.zeros((n,), x.dtype).at[dst].add(self_f)
                norm = jnp.where(sel, 1.0 / jnp.maximum(deg[dst], 1.0), 0.0)
                h_r = x @ weight[r]
                msgs = h_r[src] * norm[:, None]
                out = out + jax.ops.segment_sum(msgs, dst, num_segments=n)
            return out
        src, dst = (edge_index[0], edge_index[1])
        x = jax.nn.relu(_rgcn_conv(entity, W1, root1, b1, src, dst, edge_type))
        x = jax.nn.relu(_rgcn_conv(x, W2, root2, b2, src, dst, edge_type))
        x = _rgcn_conv(x, W3, root3, b3, src, dst, edge_type)
        return x

    def _L3_gnn_ref(x, W1, b1, W2, b2, edge_index):
        import jax, jax.numpy as jnp
        import numpy as np
        N_NODES = 625
        D = 768
        N_EDGES = 10000

        def gcn_conv(x, W, b, src, dst, n_nodes):
            h = x @ W
            deg = jax.ops.segment_sum(jnp.ones_like(dst, dtype=h.dtype), dst, num_segments=n_nodes)
            dinv = jnp.where(deg > 0, jax.lax.rsqrt(deg), 0.0)
            norm = dinv[src] * dinv[dst]
            msgs = h[src] * norm[:, None]
            out = jax.ops.segment_sum(msgs, dst, num_segments=n_nodes)
            return out + b

        def add_self_loops(edge_index, n_nodes):
            loop = jnp.arange(n_nodes, dtype=edge_index.dtype)
            src = jnp.concatenate([edge_index[0], loop])
            dst = jnp.concatenate([edge_index[1], loop])
            return (src, dst)
        n = x.shape[0]
        src, dst = add_self_loops(edge_index, n)
        h = gcn_conv(x, W1, b1, src, dst, n)
        h = jax.nn.relu(h)
        out = gcn_conv(h, W2, b2, src, dst, n)
        return out
    edge_index = jnp.stack([src, dst])
    x = _layernorm(x + _L0_gnn_ref(x, L0_gnn_W1, L0_gnn_a_src1, L0_gnn_a_dst1, L0_gnn_b1, L0_gnn_W2, L0_gnn_a_src2, L0_gnn_a_dst2, L0_gnn_b2, edge_index), axis=-1)
    x = _layernorm(x + _L1_gnn_ref(x, edge_index, edge_type_3, L1_gnn_W1, L1_gnn_q1, L1_gnn_k1, L1_gnn_b1, L1_gnn_W2, L1_gnn_q2, L1_gnn_k2, L1_gnn_b2), axis=-1)
    x = _layernorm(x + _L2_gnn_ref(x, edge_index, edge_type_4, L2_gnn_W1, L2_gnn_root1, L2_gnn_b1, L2_gnn_W2, L2_gnn_root2, L2_gnn_b2, L2_gnn_W3, L2_gnn_root3, L2_gnn_b3), axis=-1)
    x = _layernorm(x + _L3_gnn_ref(x, L3_gnn_W1, L3_gnn_b1, L3_gnn_W2, L3_gnn_b2, edge_index), axis=-1)
    return x

_drawn_inputs = setup_inputs


def setup_inputs(seed=0):
    import zlib

    import numpy as np

    out = dict(_drawn_inputs(seed))
    spreads = {'L0_gnn_b1': (0.0, 0.1),
     'L0_gnn_b2': (0.0, 0.1),
     'L1_gnn_b1': (0.0, 0.1),
     'L1_gnn_b2': (0.0, 0.1),
     'L2_gnn_b1': (0.0, 0.1),
     'L2_gnn_b2': (0.0, 0.1),
     'L2_gnn_b3': (0.0, 0.1),
     'L3_gnn_b1': (0.0, 0.1),
     'L3_gnn_b2': (0.0, 0.1)}
    factors = {'L1_gnn_q1': 8.0, 'L1_gnn_k1': 8.0, 'L1_gnn_q2': 8.0, 'L1_gnn_k2': 8.0}
    for name, (base, spread) in spreads.items():
        noise = np.random.default_rng([zlib.crc32(name.encode()), seed]).standard_normal(out[name].shape)
        drawn = base * np.exp(spread * noise) if base else spread * noise
        out[name] = jnp.asarray(drawn.astype(out[name].dtype))
    for name, factor in factors.items():
        out[name] = (out[name] * factor).astype(out[name].dtype)
    return out
```

```python
from contextlib import ExitStack

import concourse.bass as bass
import numpy as np
from concourse import mybir

F32 = mybir.dt.float32
F32R = mybir.dt.float32r
BF16 = mybir.dt.bfloat16
F16 = mybir.dt.float16
I16 = mybir.dt.int16
I32 = mybir.dt.int32
ALU = mybir.AluOpType
ACT = mybir.ActivationFunctionType

P = 128
N = 512
D = 768
E = 8704
NB = N // P
KB = D // P
HW = D // 2
HEADS0 = 8
HEADS1 = 4
REL3 = 3
REL4 = 4
CH = E // P
NEG = -1.0e30
EPS_SOFTMAX = 1e-16
EPS_NORM = 1e-5
SLOPE = 0.2

GROUPS = [(0, 24), (24, 46), (46, CH)]
PACK = 2.0 ** -12
SHIFT = -0.375
ROUND = 1.5 * 2.0 ** 23
PAIRS = [(1, 0, 1, 0, 1), (1, 2, 3, 2, 3), (0, 0, 1, 4, 5)]
SLOT3 = 4
TOTAL = 7
BIG = 4096.0


def count_edges(nc, edges, counts, masks, flag):
    with ExitStack() as ctx:
        def sb(name, shape, dt):
            return ctx.enter_context(nc.sbuf_tensor(name, shape, dt))

        def sem(name):
            return ctx.enter_context(nc.semaphore(name))

        edge_i = sb("edge_i", [P, 4, CH], I32)
        edge_f = sb("edge_f", [P, 4, CH], F32)
        first = sb("first", [P, CH], F32)
        weight = sb("weight", [P, len(PAIRS), CH], F32)
        node_i = sb("node_i", [P, N], I32)
        node_f = sb("node_f", [P, N], F16)
        src_hot = sb("src_hot", [P, 2, N], BF16)
        dst_hot = sb("dst_hot", [P, 2, N], BF16)
        packed = sb("packed", [P, NB, N], F32)
        whole = sb("whole", [P, NB, N], F32)
        sum_a = sb("sum_a", [P, NB, N], F32)
        sum_b = sb("sum_b", [P, NB, N], F32)
        total = sb("total", [P, NB, N], F32)
        rel_a = sb("rel_a", [P, NB, N], F32)
        rel_b = sb("rel_b", [P, NB, N], F32)
        rel_c = sb("rel_c", [P, NB, N], F32)
        out16 = sb("out16", [P, 2, NB, N], I16)
        mask = sb("mask", [P, 4, NB, N], BF16)
        most = sb("most", [P, 1], F32)
        most_row = sb("most_row", [1, 1], F32)
        flag_i = sb("flag_i", [1, 1], I32)
        ident = sb("ident_c", [P, P], F32)
        ps = ctx.enter_context(nc.psum_tensor("count_ps", [P, 2, NB, N], F32))

        edges_in = sem("edges_in")
        setup = sem("setup")
        iota_done = sem("iota_done")
        ident_done = sem("ident_done")
        hot_ready = sem("hot_ready")
        hot_used = sem("hot_used")
        tile_read = sem("tile_read")
        unpack = sem("unpack")
        unpacked = sem("unpacked")
        out16_ready = sem("out16_ready")
        stored = sem("stored")
        all_done = sem("all_done")
        turned = sem("turned")
        mask_read = sem("mask_read")
        most_ready = sem("most_ready")
        flag_ready = sem("flag_ready")

        chunk_end = []
        for pair in range(len(PAIRS)):
            for lo, hi in GROUPS:
                chunk_end.append(CH * pair + hi)
        block = ctx.enter_context(nc.Block())

        @block.sync
        def _(sp):
            sp.dma_start(edge_i[:], edges).then_inc(edges_in, 16)
            done = 0
            for pair, (_, _, _, slot_a, slot_b) in enumerate(PAIRS):
                for half, slot in enumerate((slot_a, slot_b)):
                    done += 1
                    sp.wait_ge(out16_ready, done)
                    sp.dma_start(counts[slot], out16[:, half]).then_inc(stored, 16)
            for half, slot in enumerate((SLOT3 + 2, TOTAL)):
                done += 1
                sp.wait_ge(out16_ready, done)
                sp.dma_start(counts[slot], out16[:, half]).then_inc(stored, 16)
            for r in range(4):
                sp.wait_ge(mask_read, NB * (r + 1))
                sp.dma_start(masks[r], mask[:, r]).then_inc(stored, 16)
            sp.wait_ge(flag_ready, 1)
            sp.dma_start(flag, flag_i[:]).then_inc(stored, 16)
            sp.wait_ge(stored, 16 * (done + 5))

        @block.gpsimd
        def _(pool):
            nc.gpsimd.iota(node_i[:], pattern=[[1, N]], base=0, channel_multiplier=0).then_inc(iota_done, 1)
            nc.gpsimd.memset(ident[:], 0.0).then_inc(unpack, 1)
            pool.wait_ge(unpack, 1)
            nc.gpsimd.affine_select(out=ident[:], in_=ident[:], compare_op=ALU.not_equal, fill=1.0, base=0,
                                    pattern=[[-1, P]], channel_multiplier=1).then_inc(ident_done, 1)
            steps = [1]

            def step(ins):
                steps[0] += 1
                ins.then_inc(unpack, 1)
                pool.wait_ge(unpack, steps[0])

            group = 0
            for pair in range(len(PAIRS)):
                for g in range(len(GROUPS)):
                    group += 1
                    pool.wait_ge(tile_read, NB * group)
                    step(nc.gpsimd.tensor_scalar(whole[:], packed[:], ROUND, -ROUND, ALU.add, ALU.add))
                    if g == 0:
                        step(nc.gpsimd.tensor_tensor(sum_a[:], packed[:], whole[:], ALU.subtract))

                        nc.gpsimd.tensor_copy(sum_b[:], whole[:]).then_inc(unpacked, 1)
                        pool.wait_ge(unpacked, group)
                    else:
                        step(nc.gpsimd.tensor_tensor(packed[:], packed[:], whole[:], ALU.subtract))
                        step(nc.gpsimd.tensor_tensor(sum_b[:], sum_b[:], whole[:], ALU.add))
                        nc.gpsimd.tensor_tensor(sum_a[:], sum_a[:], packed[:], ALU.add).then_inc(unpacked, 1)
                        pool.wait_ge(unpacked, group)
                keep_a, keep_b = (rel_a, rel_b) if pair == 2 else (sum_a, sum_b)
                step(nc.gpsimd.tensor_scalar(keep_a[:], sum_a[:], -SHIFT * len(GROUPS), 1.0 / PACK, ALU.add, ALU.mult))
                if pair == 2:
                    step(nc.gpsimd.tensor_copy(rel_b[:], sum_b[:]))
                if pair:
                    pool.wait_ge(stored, 32 * pair)
                nc.gpsimd.tensor_copy(out16[:, 0], keep_a[:]).then_inc(out16_ready, 1)
                nc.gpsimd.tensor_copy(out16[:, 1], keep_b[:]).then_inc(out16_ready, 1)
                if pair == 0:
                    step(nc.gpsimd.tensor_tensor(total[:], sum_a[:], sum_b[:], ALU.add))
                elif pair == 1:
                    step(nc.gpsimd.tensor_tensor(total[:], total[:], sum_a[:], ALU.add))
                    step(nc.gpsimd.tensor_tensor(total[:], total[:], sum_b[:], ALU.add))
            step(nc.gpsimd.tensor_tensor(rel_c[:], total[:], rel_a[:], ALU.subtract))
            step(nc.gpsimd.tensor_tensor(rel_c[:], rel_c[:], rel_b[:], ALU.subtract))
            pool.wait_ge(stored, 32 * len(PAIRS))
            nc.gpsimd.tensor_copy(out16[:, 0], rel_c[:]).then_inc(out16_ready, 1)
            nc.gpsimd.tensor_copy(out16[:, 1], total[:]).then_inc(out16_ready, 1)

        @block.scalar
        def _(act):
            for group, end in enumerate(chunk_end):
                act.wait_ge(hot_used, end)
                if group:
                    act.wait_ge(unpacked, group)
                for m in range(NB):
                    nc.scalar.activation(packed[:, m], ps[:, group % 2, m], ACT.Copy, bias=SHIFT).then_inc(tile_read, 1)

        @block.vector
        def _(dve):
            n = [0]

            def step(ins):
                n[0] += 1
                ins.then_inc(setup, 1)
                dve.wait_ge(setup, n[0])

            dve.wait_ge(iota_done, 1)
            nc.vector.tensor_copy(node_f[:], node_i[:]).then_inc(setup, 1)
            n[0] += 1
            dve.wait_ge(edges_in, 16)
            step(nc.vector.tensor_copy(edge_f[:], edge_i[:]))
            for pair, (kinds, type_a, type_b, _, _) in enumerate(PAIRS):
                kind = edge_f[:, 2 + kinds, :]
                step(nc.vector.tensor_scalar(first[:], kind, float(type_a), PACK, ALU.is_equal, ALU.mult))
                step(nc.vector.scalar_tensor_tensor(weight[:, pair, :], kind, float(type_b), first[:],
                                                    ALU.is_equal, ALU.add))

            def one_hot(chunk, pair, c, half):
                nc.vector.tensor_scalar(src_hot[:, half], node_f[:], edge_f[:, 0, bass.ds(c, 1)], None, ALU.is_equal)
                nc.vector.tensor_scalar(dst_hot[:, half], node_f[:], edge_f[:, 1, bass.ds(c, 1)],
                                        weight[:, pair, bass.ds(c, 1)], ALU.is_equal, ALU.mult).then_inc(hot_ready, 1)

            for pair in range(len(PAIRS)):
                for g, (lo, hi) in enumerate(GROUPS):
                    start = lo
                    if pair == 0 and g == 0:
                        one_hot(0, pair, 0, 0)
                        one_hot(1, pair, 1, 1)
                        start = 2
                    with dve.Fori(0, (hi - start) // 2) as i:
                        c = i * 2 + start
                        for half in range(2):
                            dve.wait_ge(hot_used, c + (CH * pair + half - 1))
                            one_hot(c, pair, c + half, half)
            dve.wait_ge(out16_ready, 8)
            nc.vector.tensor_reduce(most[:], total[:], mybir.AxisListType.XY, ALU.max).then_inc(most_ready, 1)
            for t in range(4 * NB):
                dve.wait_ge(turned, t + 1)
                nc.vector.tensor_scalar(mask[:, t // NB, t % NB], ps[:, 0, t % NB], 0.0, NEG,
                                        ALU.is_equal, ALU.mult).then_inc(mask_read, 1)
            dve.wait_ge(turned, 4 * NB + 1)
            step(nc.vector.tensor_reduce(most_row[:], ps[0:1, 1, 0, 0:P], mybir.AxisListType.X, ALU.max))
            nc.vector.tensor_scalar(flag_i[:], most_row[:], BIG, None, ALU.is_ge).then_inc(flag_ready, 1)

        @block.tensor
        def _(pe):
            group = 0
            for pair in range(len(PAIRS)):
                for lo, hi in GROUPS:
                    bank = group % 2
                    if group >= 2:
                        pe.wait_ge(tile_read, NB * (group - 1))

                    def chunk(number, half, first, last):
                        pe.wait_ge(hot_ready, number + 1)
                        for m in range(NB):
                            mm = nc.tensor.matmul(ps[:, bank, m], src_hot[:, half, m * P:(m + 1) * P],
                                                  dst_hot[:, half], start=first, stop=last, skip_group_check=True)
                        mm.then_inc(hot_used, 1)

                    base = CH * pair
                    chunk(base + lo, 0, True, False)
                    chunk(base + lo + 1, 1, False, False)
                    with pe.Fori(0, (hi - lo - 4) // 2) as i:
                        c = i * 2 + (lo + 2)
                        chunk(c + base, 0, False, False)
                        chunk(c + (base + 1), 1, False, False)
                    chunk(base + hi - 2, 0, False, False)
                    chunk(base + hi - 1, 1, False, True)
                    group += 1
            pe.wait_ge(out16_ready, 8)
            pe.wait_ge(ident_done, 1)
            pe.wait_ge(tile_read, NB * group)
            for t, table in enumerate((total, rel_a, rel_b, rel_c)):
                for m in range(NB):
                    if t:
                        pe.wait_ge(mask_read, NB * (t - 1) + m + 1)
                    for s in range(NB):
                        mm = nc.tensor.transpose(ps[:, 0, m, s * P:(s + 1) * P], table[:, s, m * P:(m + 1) * P], ident[:])
                    mm.then_inc(turned, 1)
            pe.wait_ge(most_ready, 1)
            nc.tensor.transpose(ps[0:1, 1, 0, 0:P], most[:], ident[:]).then_inc(turned, 1)

WEIGHT_BLOCKS = 2 * HEADS0 + 2 * REL3 + 3 * (REL4 + 1) + 2
NORM_AT = (1, 2, 5, 7)
B_ROW_AT = (1, 2, 5, 7)
SD_AT = (1, 2, 3, 5)
HEAD_STEPS = 39
PIECES = [(0, slice(0, P)), (1, slice(0, 64)), (1, slice(64, P)), (2, slice(0, P)),
          (3, slice(0, P)), (4, slice(0, 64)), (4, slice(64, P)), (5, slice(0, P))]


def graph_layers(nc, x, weights, attn0, attn1, attn2, bias_cols, bias_rows, counts, masks, flag, kept, out):
    PASSES = 2 * WEIGHT_BLOCKS
    with ExitStack() as ctx:
        def sb(name, shape, dt):
            return ctx.enter_context(nc.sbuf_tensor(name, shape, dt))

        def sem(name):
            return ctx.enter_context(nc.semaphore(name))

        cols_x = sb("cols_x", [P, 2, KB, N], F32R)
        wide = [sb(f"wide{i}", [P, 2, KB * N], F32R) for i in range(3)]
        prob = sb("prob", [P, 2, NB, N], F32R)
        w_pair = sb("w_pair", [P, 2, 2, KB, HW], F32R)
        w_raw = sb("w_raw", [P, 3, 2, HW], F32)
        acc = sb("acc", [P, NB, D], F32)
        multi = sb("multi", [P, NB * D], F32)
        mask = sb("edge_mask", [P, NB, N], BF16)
        xt = sb("xt", [P, 2, N], F32)
        yt = sb("yt", [P, 2, N], F32)
        hv = sb("hv", [P, 2, HW], F32)
        v_bc = sb("v_bc", [P, N], F32)
        r_den = sb("r_den", [P, N], F32)
        q_rows = sb("q_rows", [4, N], F32R)
        ident = sb("ident", [P, P], F32)
        ones = sb("ones", [P, P], F32R)
        pick = sb("pick", [4, 2, P], F32R)
        b_cols = sb("b_cols", [P, HEADS0 * KB + KB], F32)
        al_part = sb("al_part", [P, 8, NB], F32)
        al = sb("al", [P, 2, 2, NB], F32)
        al1 = sb("al1", [P, 2, REL3, HEADS1, NB], F32)
        kc = sb("kc", [P, NB, 2], F32)
        ks = sb("ks", [P, 2, 2, NB], F32)
        ks1 = sb("ks1", [P, 2, REL3, HEADS1, NB], F32)
        mx = sb("mx", [P, NB], F32)
        mx1 = sb("mx1", [P, REL3, HEADS1, NB], F32)
        uv = sb("uv", [P, 2, NB], F32)
        uv1 = sb("uv1", [P, 2, REL3, HEADS1, NB], F32)
        uvc = sb("uvc", [P, REL3, HEADS1, NB, 4], F32)
        zc = sb("zc", [P, 2, NB], F32)
        bn = sb("bn", [P, NB, 2, 6], F32)
        stat = sb("stat", [P, NB, 2], F32)
        sd = sb("sd", [P, 2, NB], F32)
        waited = sb("waited", [P, 1], F32)
        flag_sb = sb("flag_sb", [1, 1], I32)
        rows = [wide[i][:].rearrange("p a (m f) -> p a m f", m=NB) for i in range(3)]
        cols_y = [wide[i][:].rearrange("p a (k n) -> p a k n", k=KB) for i in (2, 1)]
        prob_sets = [prob, cols_x]
        count16 = [multi[:, 1024 * r:1024 * (r + 1)].bitcast(I16).rearrange("p (m n) -> p m n", m=NB) for r in range(3)]
        vec = multi[:, 1024:1024 + 2 * D].rearrange("p (a f) -> p a f", a=2)
        vec4 = multi[:].rearrange("p (a f) -> p a f", a=NB)
        resid = multi[:].rearrange("p (m f) -> p m f", m=NB)
        scale_bc = multi[:, 1024:].rearrange("p (r n) -> p r n", r=REL4)
        ones_f = xt[:, 0, 0:P]
        pick_f = yt[0:4, :, 0:P]
        b_row = yt[:].rearrange("p a n -> p (a n)")[:, 0:D]
        xt_row = xt[:].rearrange("p a n -> p (a n)")[:, 0:D]
        ps = ctx.enter_context(nc.psum_tensor("ps", [P, 8, N], F32))

        raw_in = [sem(f"raw_in{p}") for p in range(3)]
        consts = sem("consts")
        w_high = sem("w_high")
        w_low = sem("w_low")
        prod_done = sem("prod_done")
        tile_copied = sem("tile_copied")
        rows_ready = sem("rows_ready")
        rows_split = sem("rows_split")
        acc_added = sem("acc_added")
        agg_done = sem("agg_done")
        agg_read = sem("agg_read")
        misc_done = sem("misc_done")
        kc_ready = sem("kc_ready")
        uv_ready = sem("uv_ready")
        q_ready = sem("q_ready")
        vb_ready = sem("vb_ready")
        rd_done = sem("rd_done")
        max_done = sem("max_done")
        b_used = sem("b_used")
        diag_added = sem("diag_added")
        out_done = sem("out_done")
        den_read = sem("den_read")
        x_pre = sem("x_pre")
        x_exp = sem("x_exp")
        x_mid = sem("x_mid")
        x_hi = sem("x_hi")
        x_lo = sem("x_lo")
        p_used = sem("p_used")
        row_done = sem("row_done")
        row_read = sem("row_read")
        turn_done = sem("turn_done")
        turn_hi = sem("turn_hi")
        turn_lo = sem("turn_lo")
        cnt_hi = sem("cnt_hi")
        cnt_lo = sem("cnt_lo")
        edge_done = sem("edge_done")
        y_done = sem("y_done")
        y_hi = sem("y_hi")
        y_lo = sem("y_lo")
        scale_ready = sem("scale_ready")
        var_ready = sem("var_ready")
        sd_ready = sem("sd_ready")
        acc_ready = sem("acc_ready")
        step = sem("step")
        vec_in = sem("vec_in")
        cnt_in = sem("cnt_in")
        mask_in = sem("mask_in")
        res_in = sem("res_in")
        b_in = sem("b_in")
        small_in = sem("small_in")
        kept_out = sem("kept_out")

        block = ctx.enter_context(nc.Block())

        @block.sync
        def _(sp):
            for p in range(3):
                sp.dma_start(w_raw[:, p], weights[0, p]).then_inc(raw_in[p], 16)
            with sp.Fori(1, PASSES) as j:
                for p in range(3):
                    sp.wait_ge(w_low, j * 3 + (p - 2))
                    sp.dma_start(w_raw[:, p], weights[bass.ds(j, 1), p]).then_inc(raw_in[p], 16)

        @block.gpsimd
        def _(pool):
            nc.gpsimd.memset(ident[:], 0.0).then_inc(consts, 1)
            nc.gpsimd.memset(ones_f, 1.0).then_inc(consts, 1)
            pool.wait_ge(consts, 2)
            nc.gpsimd.affine_select(out=ident[:], in_=ident[:], compare_op=ALU.not_equal, fill=1.0, base=0,
                                    pattern=[[-1, P]], channel_multiplier=1).then_inc(consts, 1)
            with pool.Fori(0, PASSES // 2) as i:
                for slot in range(2):
                    for p in range(3):
                        pool.wait_ge(w_high, i * 6 + (3 * slot + p + 1))
                        nc.gpsimd.tensor_tensor(w_pair[:, slot, 1, 2 * p:2 * p + 2, :], w_raw[:, p],
                                                w_pair[:, slot, 0, 2 * p:2 * p + 2, :].bitcast(F32),
                                                ALU.subtract).then_inc(w_low, 1)

        @block.tensor
        def _(pe):
            def product(j, m, left, free, value):
                pe.wait_ge(free, value)
                for k in range(KB):
                    if m == 0 and k % 2 == 0:
                        pe.wait_ge(w_low, j * 3 + (k // 2 + 1))
                    for a, b in ((0, 0), (0, 1), (1, 0)):
                        mm = nc.tensor.matmul(ps[:, m, 0:HW], left[:, a, k, m * P:(m + 1) * P], w_pair[:, slot_of[0], b, k, :],
                                              start=(k == 0 and a + b == 0), stop=(k == KB - 1 and a == 1))
                mm.then_inc(prod_done, 1)

            slot_of = [0]

            def turn_small(table, width):
                for m in range(NB):
                    mm = nc.tensor.transpose(ps[0:width, 6, m * P:(m + 1) * P], table[:, m, :], ident[:])
                mm.then_inc(misc_done, 1)

            def spread_source():
                nc.tensor.matmul(ps[:, 7, :], ones[0:2, :], q_rows[0:2, :], start=True, stop=True).then_inc(misc_done, 1)

            def spread_uv():
                nc.tensor.matmul(ps[:, 7, :], pick[:, 0, :], q_rows[:], start=True, stop=True)
                nc.tensor.matmul(ps[:, 6, :], pick[:, 1, :], q_rows[:], start=True, stop=True).then_inc(misc_done, 1)

            def turn(count):
                for f in range(KB):
                    if f >= 2:
                        pe.wait_ge(turn_lo, count + f - 1)
                    for m in range(NB):
                        mm = nc.tensor.transpose(ps[:, 4 + f % 2, m * P:(m + 1) * P], acc[:, m, f * P:(f + 1) * P], ident[:])
                    mm.then_inc(turn_done, 1)

            pe.wait_ge(consts, 5)
            pe.wait_ge(small_in, 32)
            many = pe.value_load(flag_sb[0:1, 0:1], min_val=0, max_val=1)
            pe.wait_ge(res_in, 16)
            turn(0)

            def head(h, parity, j_rows, j_out, with_next, with_last):
                if with_next:
                    for u in range(8):
                        n, m = u // 4, u % 4
                        slot_of[0] = n
                        if n == 0:
                            if with_last:
                                pe.wait_ge(acc_added, h * 8 + (m - 3))
                            product(j_rows, m, cols_x, tile_copied, h * 8 + (4 + m + 1))
                        else:
                            product(j_rows + 1, m, cols_x, tile_copied, h * 8 + (8 + m + 1))
                        if u == 0:
                            pe.wait_ge(kc_ready, h + 1)
                            if with_last:
                                pe.wait_ge(rd_done, h)
                            turn_small(kc, 2)
                        elif u == 1:
                            pe.wait_ge(q_ready, h * 2 + 1)
                            if with_last:
                                pe.wait_ge(x_pre, h * 10)
                            spread_source()
                        elif u == 3:
                            pe.wait_ge(uv_ready, h + 1)
                            turn_small(uvc[:, 0, 0], 4)
                        elif u == 5:
                            pe.wait_ge(q_ready, h * 2 + 2)
                            spread_uv()
                else:
                    pe.wait_ge(kc_ready, h + 1)
                    pe.wait_ge(rd_done, h)
                    turn_small(kc, 2)
                    pe.wait_ge(q_ready, h * 2 + 1)
                    spread_source()
                    pe.wait_ge(uv_ready, h + 1)
                    turn_small(uvc[:, 0, 0], 4)
                    pe.wait_ge(q_ready, h * 2 + 2)
                    spread_uv()
                if with_last:
                    out_product(h - 1, j_out, tile_copied if with_next else None)
                pe.wait_ge(x_lo, h * 10 + 4)
                pe.wait_ge(vb_ready, h + 1)
                for s in range(NB):
                    for a in range(2):
                        mm = nc.tensor.matmul(ps[:, 6, :], ones[:], prob[:, a, s, :], start=(s + a == 0), stop=(s + a == NB))
                mm.then_inc(misc_done, 1)
                pe.wait_ge(rows_ready, h * 8 + 8)
                for f in range(KB):
                    if with_last or f >= 2:
                        pe.wait_ge(agg_read, h * 6 + (f - 1))
                    for s in range(NB):
                        for a, b in ((0, 0), (0, 1), (1, 0)):
                            mm = nc.tensor.matmul(ps[:, 4 + f % 2, :], rows[parity][:, a, s, f * P:(f + 1) * P], prob[:, b, s, :],
                                                  start=(s + a + b == 0), stop=(s == NB - 1 and a == 1))
                    mm.then_inc(agg_done, 1)

            def out_product(x_head, j, before):
                pe.wait_ge(x_lo, x_head * 10 + 10)
                for u in range(8):
                    n, m = u // 4, u % 4
                    slot_of[0] = n
                    if n == 0 and before is tile_copied:
                        product(j, m, cols_y[0], tile_copied, x_head * 8 + (16 + 4 + m + 1))
                    else:
                        product(j + n, m, cols_y[0], acc_added, x_head * 8 + (4 + m + 1 if n == 0 else 8 + m + 1))

            pe.wait_ge(turn_lo, KB)
            for u in range(8):
                slot_of[0] = u // 4
                if u < 4:
                    product(0, u % 4, cols_x, turn_lo, KB)
                else:
                    product(1, u % 4, cols_x, tile_copied, u % 4 + 1)
            head(0, 0, 2, None, True, False)
            with pe.Fori(0, 3) as i:
                for odd in range(2):
                    h = i * 2 + (1 + odd)
                    head(h, 1 - odd, h * 4, h * 4 + 2, True, True)
            head(7, 1, None, 28, False, True)
            out_product(7, 30, acc_added)

            pe.wait_ge(kc_ready, 9)
            turn_small(kc, 2)
            pe.wait_ge(q_ready, 17)
            spread_source()
            pe.wait_ge(uv_ready, 9)
            turn_small(uvc[:, 0, 0], 4)
            pe.wait_ge(q_ready, 18)
            spread_uv()

            def row_sums(source, weights_of, first_sem, first_value, units):
                for m in range(NB):
                    for s in range(NB):
                        for a in range(2):
                            mm = nc.tensor.matmul(ps[:, 5, 2 * m:2 * m + 2], weights_of[:, a, s, m * P:(m + 1) * P], ones[:, 0:2],
                                                  start=(s + a == 0), stop=(s + a == NB))
                mm.then_inc(misc_done, 1)
                for u in range(8):
                    n, m = u // 4, u % 4
                    if n == 0:
                        pe.wait_ge(first_sem, first_value + m)
                    else:
                        pe.wait_ge(row_read, units + m + 1)
                    for s in range(NB):
                        for a, b in ((0, 0), (0, 1), (1, 0)):
                            mm = nc.tensor.matmul(ps[:, m, 0:HW], weights_of[:, a, s, m * P:(m + 1) * P],
                                                  source[:, b, s, n * HW:(n + 1) * HW],
                                                  start=(s + a + b == 0), stop=(s == NB - 1 and a == 1))
                    mm.then_inc(row_done, 1)

            pe.wait_ge(x_lo, 84)
            pe.wait_ge(rows_split, NB)
            row_sums(rows[0], prob, acc_added, 69, 0)
            pe.wait_ge(acc_ready, 1)
            turn(KB)

            def max_round(kc_count, q_count, part):
                if part == 0:
                    pe.wait_ge(kc_ready, kc_count)
                    turn_small(kc, 2)
                else:
                    pe.wait_ge(q_ready, q_count)
                    spread_source()

            pe.wait_ge(turn_lo, 2 * KB)
            for r in range(REL3):
                for u in range(8):
                    n, m = u // 4, u % 4
                    slot_of[0] = n
                    if r == 0 and n == 0:
                        product(32, m, cols_x, row_read, 4 + m + 1)
                    else:
                        product(32 + 2 * r + n, m, cols_x, tile_copied, 64 + 8 * r + 4 * n - 4 + m + 1)
                    if r:
                        max_round(9 + 4 * (r - 1) + u // 2 + 1, 18 + 4 * (r - 1) + u // 2 + 1, u % 2)
            for h in range(HEADS1):
                for part in range(2):
                    max_round(18 + h, 27 + h, part)
            pe.wait_ge(uv_ready, 10)
            turn_small(uvc[:, 0, 0], 4)
            pe.wait_ge(q_ready, 31)
            spread_uv()
            pe.wait_ge(tile_copied, 88)
            pe.wait_ge(rows_ready, 88)
            for g in range(REL3 * HEADS1):
                h, r = g // REL3, g % REL3
                if g + 1 < REL3 * HEADS1:
                    pe.wait_ge(vb_ready, 10 + g)
                    turn_small(uvc[:, (g + 1) % REL3, (g + 1) // REL3], 4)
                if r == 0 and h >= 2:
                    pe.wait_ge(agg_read, 48 + 2 * (h - 1))
                    pe.wait_ge(rd_done, 8 + h - 1)
                chunk0 = (0, 1, 3, 4)[h]
                w0 = 84 + 14 * h + 4 * r
                for s in range(NB):
                    if s == 2 and g + 1 < REL3 * HEADS1:
                        pe.wait_ge(q_ready, 32 + g)
                        pe.wait_ge(x_pre, w0 + 4)
                        spread_uv()
                    pe.wait_ge(x_lo, w0 + s + 1)
                    begin, end = r == 0 and s == 0, r == REL3 - 1 and s == NB - 1
                    for a in range(2):
                        nc.tensor.matmul(ps[:, 4 + h % 2, :], ones[:], prob[:, a, s, :], start=(begin and a == 0), stop=(end and a == 1))
                    for c in range(2):
                        f = chunk0 + c
                        for a, b in ((0, 0), (0, 1), (1, 0)):
                            mm = nc.tensor.matmul(ps[:, 2 * (h % 2) + c, :], rows[r][:, a, s, f * P:(f + 1) * P], prob[:, b, s, :],
                                                  start=(begin and a + b == 0), stop=(end and a == 1))
                    mm.then_inc(p_used, 1)

            pe.wait_ge(x_lo, 140)
            for r in range(REL3):
                for u in range(8):
                    n, m = u // 4, u % 4
                    slot_of[0] = n
                    if r == 0 and n == 0:
                        product(38, m, cols_x, agg_read, 56)
                    else:
                        product(38 + 2 * r + n, m, cols_x, tile_copied, 88 + 8 * r + 4 * n - 4 + m + 1)
                    if r and u < 2:
                        max_round(21 + r, 42 + r, u)
            for part in range(2):
                max_round(24, 45, part)

            def uv_round(r, x_count):
                pe.wait_ge(uv_ready, 11)
                pe.wait_ge(vb_ready, 21 + r)
                turn_small(uvc[:, r, 0], 4)
                pe.wait_ge(q_ready, 46 + r)
                pe.wait_ge(x_pre, x_count)
                spread_uv()

            uv_round(0, 140)
            uv_round(1, 144)
            pe.wait_ge(x_lo, 144)
            pe.wait_ge(rows_ready, 112)
            row_sums(rows[0], prob_sets[0], tile_copied, 109, 8)
            uv_round(2, 148)
            pe.wait_ge(x_lo, 148)
            pe.wait_ge(den_read, 2)
            row_sums(rows[1], prob_sets[1], row_read, 13, 16)
            pe.wait_ge(x_lo, 152)
            pe.wait_ge(den_read, 3)
            row_sums(rows[2], prob_sets[0], row_read, 21, 24)
            pe.wait_ge(acc_ready, 2)
            turn(2 * KB)

            def edge_sums(number, cnt):
                pe.wait_ge(cnt_lo, cnt)
                for f in range(KB):
                    t = number * KB + f
                    if t >= 2:
                        pe.wait_ge(y_done, t - 1)
                    bank = ps[:, 4 + f % 2, :]
                    nc.tensor.matmul(bank, rows[0][:, 0, 0, f * P:(f + 1) * P], prob[:, 0, 0, :], start=True, stop=False)
                    with pe.If(many > 0):
                        for s in range(NB):
                            for a in range(2):
                                nc.tensor.matmul(bank, rows[0][:, a, s, f * P:(f + 1) * P], prob[:, 1, s, :], start=False, stop=False)
                    for s in range(NB):
                        for a in range(2):
                            if s + a:
                                mm = nc.tensor.matmul(bank, rows[0][:, a, s, f * P:(f + 1) * P], prob[:, 0, s, :],
                                                      start=False, stop=(s + a == NB))
                    mm.then_inc(edge_done, 1)

            def degrees(spread_only):
                for s in range(NB):
                    for a in range(2):
                        mm = nc.tensor.matmul(ps[:, 6, :], ones[:], prob[:, a, s, :], start=(s + a == 0), stop=(s + a == NB))
                if not spread_only:
                    for m in range(NB):
                        for s in range(NB):
                            for a in range(2):
                                mm = nc.tensor.matmul(ps[:, 7, 2 * m:2 * m + 2], prob[:, a, s, m * P:(m + 1) * P], ones[:, 0:2],
                                                      start=(s + a == 0), stop=(s + a == NB))
                mm.then_inc(misc_done, 1)

            def layer_product(j, left, added):
                for u in range(8):
                    n, m = u // 4, u % 4
                    slot_of[0] = n
                    product(j + n, m, left, acc_added, added + 4 * n - 4 + m + 1)

            added = 72
            pe.wait_ge(row_read, 32)
            for layer in range(3):
                pe.wait_ge(rows_split, NB * (2 + layer))
                for r in range(REL4):
                    if layer == 0:
                        pe.wait_ge(cnt_lo, r + 1)
                        if r:
                            pe.wait_ge(scale_ready, r)
                        degrees(True)
                    edge_sums(4 * layer + r, 4 * layer + r + 1)
                    if r == 0:
                        pe.wait_ge(turn_lo, KB * (3 + layer))
                        layer_product(44 + 10 * layer, cols_x, added)
                    else:
                        pe.wait_ge(y_lo, KB * (4 * layer + r))
                        layer_product(44 + 10 * layer + 2 * r, cols_y[(r - 1) % 2], added)
                    added += 8
                pe.wait_ge(y_lo, KB * (4 * layer + 4))
                layer_product(52 + 10 * layer, cols_y[1], added)
                added += 8
                pe.wait_ge(acc_ready, 3 + layer)
                if layer < 2:
                    turn(KB * (3 + layer))
            pe.wait_ge(cnt_lo, 13)
            pe.wait_ge(scale_ready, REL4)
            degrees(False)
            for layer in range(2):
                pe.wait_ge(rows_split, NB * (5 + layer))
                edge_sums(12 + layer, 13)
                pe.wait_ge(y_lo, KB * (13 + layer))
                layer_product(74 + 2 * layer, cols_y[0], added)
                added += 8

        @block.scalar
        def _(act):
            def copy(dst, src):
                return nc.scalar.activation(dst, src, ACT.Copy)

            def split_high(j, slot, wait=True):
                for p in range(3):
                    act.wait_ge(raw_in[p], j * 16 + 16)
                    if p == 0 and wait:
                        act.wait_ge(prod_done, j * 4 - 4)
                    copy(w_pair[:, slot, 0, 2 * p:2 * p + 2, :], w_raw[:, p]).then_inc(w_high, 1)

            def copy_tile(j, m, q, first=False):
                act.wait_ge(prod_done, j * 4 + (m + 1))
                if not first:
                    act.wait_ge(rows_ready, q - 1)
                copy(hv[:, m % 2], ps[:, m, 0:HW]).then_inc(tile_copied, 1)

            def copy_rows(count, width):
                act.wait_ge(misc_done, count)
                copy(q_rows[0:width, :], ps[0:width, 6, :]).then_inc(q_ready, 1)

            def copy_v(count):
                act.wait_ge(misc_done, count)
                copy(v_bc[:], ps[:, 6, :]).then_inc(vb_ready, 1)

            def exponential(w, slot, bias):
                act.wait_ge(x_pre, w + 1)
                nc.scalar.activation(xt[:, slot], xt[:, slot], ACT.Exp, bias=bias).then_inc(x_exp, 1)

            def high(w, slot, dst, part=slice(0, P)):
                act.wait_ge(x_mid, w + 1)
                copy(dst, xt[part, slot]).then_inc(x_hi, 1)

            def turn(count):
                for f in range(KB):
                    act.wait_ge(turn_done, count + f + 1)
                    copy(cols_x[:, 0, f, :], ps[:, 4 + f % 2, :]).then_inc(turn_hi, 1)

            act.dma_start(acc[:], x).then_inc(res_in, 16)
            act.dma_start(b_cols[:], bias_cols).then_inc(small_in, 16)
            act.dma_start(flag_sb[:], flag).then_inc(small_in, 16)
            act.dma_start(vec, attn0[0:1].partition_broadcast(P)).then_inc(vec_in, 16)
            act.dma_start(count16[0], counts[TOTAL]).then_inc(cnt_in, 16)
            act.dma_start(mask[:], masks[0]).then_inc(mask_in, 16)
            split_high(0, 0, wait=False)
            split_high(1, 1, wait=False)
            turn(0)

            def head(h, parity, j_rows, j_out, with_next, with_last):
                if with_next:
                    for u in range(8):
                        n, m = u // 4, u % 4
                        copy_tile(j_rows + n, m, h * 8 + (8 + u))
                        if u == 0:
                            copy_rows(h * 5 + 1, 2)
                        elif u == 3:
                            split_high(j_rows + 2, 0)
                            copy_rows(h * 5 + 3, 4)
                        elif u == 5:
                            copy_v(h * 5 + 4)
                    split_high(j_rows + 3, 1)
                    act.wait_ge(rows_ready, h * 8 + 16)
                    act.dma_start(vec, attn0[bass.ds(h + 2, 1)].partition_broadcast(P)).then_inc(vec_in, 16)
                else:
                    copy_rows(h * 5 + 1, 2)
                    copy_rows(h * 5 + 3, 4)
                    copy_v(h * 5 + 4)
                for s in range(NB + 1):
                    if s < NB:
                        exponential(h * 10 + s, s % 2, ks[:, parity, 1, s:s + 1])
                    if s >= 1:
                        high(h * 10 + (s - 1), (s - 1) % 2, prob[:, 0, s - 1, :])
                    if s == 3 and with_last:
                        split_high(j_out + 2, 0)
                if with_last:
                    split_high(j_out + 3, 1)
                for f in range(KB + 1):
                    if f < KB:
                        exponential(h * 10 + (4 + f), f % 2, 0.0)
                    if f >= 1:
                        high(h * 10 + (4 + f - 1), (f - 1) % 2, cols_y[0][:, 0, f - 1, :])

            for u in range(8):
                copy_tile(u // 4, u % 4, u, first=u < 2)
                if u == 3:
                    split_high(2, 0)
            split_high(3, 1)
            act.wait_ge(rows_ready, 8)
            act.dma_start(vec, attn0[1:2].partition_broadcast(P)).then_inc(vec_in, 16)
            head(0, 0, 2, None, True, False)
            with act.Fori(0, 3) as i:
                for odd in range(2):
                    h = i * 2 + (1 + odd)
                    head(h, 1 - odd, h * 4, h * 4 + 2, True, True)
            head(7, 1, None, 28, False, True)
            split_high(32, 0)
            split_high(33, 1)

            copy_rows(41, 2)
            copy_rows(43, 4)
            copy_v(44)
            for s in range(NB + 1):
                if s < NB:
                    exponential(80 + s, s % 2, ks[:, 0, 1, s:s + 1])
                if s >= 1:
                    high(80 + s - 1, (s - 1) % 2, prob[:, 0, s - 1, :])

            def norm(layer, residual):
                if layer > 1:
                    act.wait_ge(kept_out, 16 * layer)
                act.dma_start(resid, residual).then_inc(res_in, 16)
                act.wait_ge(var_ready, layer + 1)
                nc.scalar.activation(sd[:, 0], stat[:, :, 1], ACT.Sqrt).then_inc(sd_ready, 1)
                act.wait_ge(acc_ready, NORM_AT[layer])
                if layer < 3:
                    act.dma_start(kept, acc[:]).then_inc(kept_out, 16)

            act.wait_ge(x_lo, 84)
            act.dma_start(b_row, bias_rows[0:1].partition_broadcast(P)).then_inc(b_in, 16)
            norm(0, x)
            turn(KB)
            act.wait_ge(kept_out, 16)

            act.dma_start(acc[:], attn1[0:1].partition_broadcast(P)).then_inc(vec_in, 16)
            act.dma_start(vec4, attn1[1:2].partition_broadcast(P)).then_inc(vec_in, 16)
            act.dma_start(mask[:], masks[1]).then_inc(mask_in, 16)
            for r in range(REL3):
                for u in range(8):
                    n, m = u // 4, u % 4
                    copy_tile(32 + 2 * r + n, m, 64 + 8 * r + u)
                    if m == 3:
                        split_high(34 + 2 * r + n, n)
                    if r and u % 2 == 0:
                        copy_rows(45 + 8 * (r - 1) + u + 1, 2)
                if r:
                    act.wait_ge(max_done, 9 + 4 * r)
                    act.dma_start(mask[:], masks[1 + r]).then_inc(mask_in, 16)
            act.wait_ge(rows_ready, 88)
            for r in range(REL3):
                act.dma_start(count16[r], counts[SLOT3 + r]).then_inc(cnt_in, 16)
            for h in range(HEADS1):
                copy_rows(61 + 2 * h + 1, 2)
            copy_rows(70, 4)
            copy_v(71)
            for h in range(HEADS1):
                w0 = 84 + 14 * h
                for s in range(REL3 * NB + 1):
                    g = 3 * h + s // 4
                    if s < REL3 * NB:
                        exponential(w0 + s, s % 2, ks1[:, 1, s // 4, h, s % 4:s % 4 + 1])
                    if s >= 1:
                        tile = 12 * h + s - 1
                        if tile >= NB:
                            act.wait_ge(p_used, tile - NB + 1)
                        high(w0 + s - 1, (s - 1) % 2, prob[:, 0, (s - 1) % 4, :])
                    if s < 12 and g < 11:
                        if s % 4 == 1:
                            copy_rows(72 + 2 * g, 4)
                        elif s % 4 == 3:
                            copy_v(73 + 2 * g)
                for c in range(3):
                    if c < 2:
                        exponential(w0 + 12 + c, c, 0.0)
                    if c >= 1:
                        f, part = PIECES[2 * h + c - 1]
                        high(w0 + 12 + c - 1, c - 1, cols_x[part, 0, f, :], part)

            act.dma_start(acc[:, 0:2], attn2.partition_broadcast(P)).then_inc(vec_in, 16)
            act.dma_start(mask[:], masks[1]).then_inc(mask_in, 16)
            for r in range(REL3):
                for u in range(8):
                    n, m = u // 4, u % 4
                    copy_tile(38 + 2 * r + n, m, 88 + 8 * r + u)
                    if m == 3:
                        split_high(40 + 2 * r + n, n)
                    if r and u == 0:
                        copy_rows(93 + 2 * r - 1, 2)
                    if r and u == 7:
                        act.wait_ge(max_done, 21 + r)
                        act.dma_start(mask[:], masks[1 + r]).then_inc(mask_in, 16)
            copy_rows(98, 2)
            for r in range(REL3):
                copy_rows((100, 102, 105)[r], 4)
                copy_v((101, 103, 106)[r])
                if r == 2:
                    act.wait_ge(row_done, 16)
                for s in range(NB + 1):
                    if s < NB:
                        exponential(140 + 4 * r + s, s % 2, ks1[:, 1, r, 0, s:s + 1])
                    if s >= 1:
                        high(140 + 4 * r + s - 1, (s - 1) % 2, prob_sets[r % 2][:, 0, s - 1, :])
            act.wait_ge(x_lo, 152)
            act.dma_start(b_row, bias_rows[1:2].partition_broadcast(P)).then_inc(b_in, 16)
            norm(1, kept)
            turn(2 * KB)

            def count_high(number, after):
                act.wait_ge(cnt_in, 16 * (4 + number))
                if number > 1:
                    act.wait_ge(edge_done, KB * (number - 1))
                copy(prob[:, 0], count16[0]).then_inc(cnt_hi, 1)
                if after is not None:
                    act.wait_ge(cnt_lo, number)
                    act.dma_start(count16[0], after).then_inc(cnt_in, 16)

            def edge_high(number, dst):
                for f in range(KB):
                    t = number * KB + f
                    act.wait_ge(y_done, t + 1)
                    copy(dst[:, 0, f, :], xt[:, f % 2]).then_inc(y_hi, 1)

            act.dma_start(count16[0], counts[0]).then_inc(cnt_in, 16)
            for layer in range(3):
                j = 44 + 10 * layer
                act.wait_ge(b_used, 2 + layer)
                act.dma_start(b_row, bias_rows[2 + layer:3 + layer].partition_broadcast(P)).then_inc(b_in, 16)
                count_high(4 * layer + 1, counts[1])
                for r in range(REL4):
                    edge_high(4 * layer + r, cols_y[r % 2])
                    if r + 1 < REL4:
                        count_high(4 * layer + r + 2, None if layer == 2 and r == 2 else counts[(r + 2) % REL4])
                    for n in range(2):
                        split_high(j + 2 * r + n + 2, n)
                for n in range(2):
                    split_high(j + 10 + n, n)
                if layer < 2:
                    act.wait_ge(acc_ready, 3 + layer)
                    turn(KB * (3 + layer))
            norm(2, kept)
            act.dma_start(count16[0], counts[TOTAL]).then_inc(cnt_in, 16)
            act.wait_ge(diag_added, 1)
            act.wait_ge(edge_done, KB * 12)
            copy(prob[:, 0], count16[0]).then_inc(cnt_hi, 1)
            act.wait_ge(misc_done, 113)
            nc.scalar.activation(scale_bc[:, 0], ps[:, 6, :], ACT.Sqrt)
            nc.scalar.activation(zc[:, 0], ps[:, 7, 0:2 * NB:2], ACT.Sqrt).then_inc(sd_ready, 1)
            for layer in range(2):
                act.wait_ge(b_used, 5 + layer)
                act.dma_start(b_row, bias_rows[5 + layer:6 + layer].partition_broadcast(P)).then_inc(b_in, 16)
                edge_high(12 + layer, cols_y[0])
                if layer == 0:
                    for n in range(2):
                        split_high(76 + n, n)
            act.wait_ge(y_lo, KB * 14)
            norm(3, kept)
            act.dma_start(out, acc[:]).then_inc(out_done, 16)
            act.wait_ge(out_done, 16)

        @block.vector
        def _(dve):
            base, local = [0], [0]

            def mark(ins):
                local[0] += 1
                ins.then_inc(step, 1)

            def wait_steps():
                dve.wait_ge(step, base[0] + local[0])

            def wait_all_but_one():
                dve.wait_ge(step, base[0] + (local[0] - 1))

            def sub(dst, a, b):
                return nc.vector.tensor_tensor(dst, a, b, ALU.subtract)

            def add(dst, a, b):
                return nc.vector.tensor_tensor(dst, a, b, ALU.add)

            def copy(dst, src):
                return nc.vector.tensor_copy(dst, src)

            def dot(scratch, a, b, start, total):
                return nc.vector.tensor_tensor_reduce(out=scratch, in0=a, in1=b, scale=1.0, scalar=start,
                                                      op0=ALU.mult, op1=ALU.add, accum_out=total)

            def f32(ap):
                return ap.bitcast(F32)

            def turn(count):
                for f in range(KB):
                    dve.wait_ge(turn_hi, count + f + 1)
                    sub(cols_x[:, 1, f, :], ps[:, 4 + f % 2, :], f32(cols_x[:, 0, f, :])).then_inc(turn_lo, 1)

            def split_tile(q, m, n, dst, dots):
                dve.wait_ge(tile_copied, q + 1)
                tile = hv[:, m % 2]
                part = slice(n * HW, (n + 1) * HW)
                mark(copy(dst[:, 0, m, part], tile))
                for v, (vector, total) in enumerate(dots):
                    if v >= 2:
                        wait_all_but_one()
                    if n == 0:
                        mark(dot(yt[:, v % 2, 0:HW], tile, vector[:, part], 0.0, al_part[:, v, m:m + 1]))
                    else:
                        mark(dot(yt[:, v % 2, 0:HW], tile, vector[:, part], al_part[:, v, m:m + 1], total[:, m:m + 1]))
                wait_steps()
                sub(dst[:, 1, m, part], tile, f32(dst[:, 0, m, part])).then_inc(rows_ready, 1)

            def source_columns(term, scaled):
                mark(nc.vector.tensor_copy(kc[:, :, 0].bitcast(F32R), term))
                if scaled is not None:
                    nc.vector.tensor_scalar(scaled[0], term, 1.0 - SLOPE, None, ALU.mult)
                    nc.vector.tensor_scalar(scaled[1], term, SLOPE, None, ALU.mult)
                wait_steps()
                sub(kc[:, :, 1], term, kc[:, :, 0]).then_inc(kc_ready, 1)

            def maxima(misc, total, done, tiles=None):
                if tiles is not None:
                    dve.wait_ge(x_lo, tiles)
                dve.wait_ge(misc_done, misc)
                nc.vector.memset(waited[:], 0.0)
                for m in range(NB):
                    ins = nc.vector.tensor_tensor_reduce(out=(xt, yt)[m // 2][:, m % 2], in0=ps[:, 7, :], in1=mask[:, m, :], scale=1.0,
                                                         scalar=-3.0e38, op0=ALU.add, op1=ALU.max, accum_out=total[:, m:m + 1])
                ins.then_inc(max_done, 1)
                dve.wait_ge(max_done, done)

            def leaky(z):
                wait_steps()
                mark(nc.vector.scalar_tensor_tensor(z, z, SLOPE, z, ALU.mult, ALU.max))
                wait_steps()

            def u_and_v(target, largest, u, v, parts):
                mark(sub(u, target, largest))
                mark(nc.vector.scalar_tensor_tensor(v, target, SLOPE, largest, ALU.mult, ALU.subtract))
                wait_steps()
                mark(nc.vector.tensor_copy(parts[0].bitcast(F32R), u))
                mark(nc.vector.tensor_copy(parts[2].bitcast(F32R), v))
                wait_steps()
                mark(sub(parts[1], u, parts[0]))
                return sub(parts[3], v, parts[2])

            def exponent(w, slot, source, first=False):
                if not first:
                    dve.wait_ge(x_lo, w - 1)
                nc.vector.scalar_tensor_tensor(xt[:, slot], ps[:, 7, :], source, v_bc[:], ALU.add, ALU.max).then_inc(x_pre, 1)

            def weigh(w, slot, count):
                dve.wait_ge(x_exp, w + 1)
                nc.vector.scalar_tensor_tensor(xt[:, slot], xt[:, slot], 1.0, count, ALU.min, ALU.mult).then_inc(x_mid, 1)

            def low(w, slot, dst, high, part=slice(0, P)):
                dve.wait_ge(x_hi, w + 1)
                sub(dst, xt[part, slot], f32(high)).then_inc(x_lo, 1)

            def elu_start(w, read, slot, bank, bias, part=slice(0, P)):
                dve.wait_ge(x_lo, w - 1)
                nc.vector.tensor_tensor(yt[part, slot], bank[part], r_den[part], ALU.mult).then_inc(agg_read, 1)
                dve.wait_ge(agg_read, read + 1)
                nc.vector.tensor_scalar(xt[part, slot], yt[part, slot], bias, 0.0, ALU.add, ALU.min).then_inc(x_pre, 1)

            def elu_end(w, slot, bias, part=slice(0, P)):
                mark(nc.vector.tensor_scalar(yt[part, slot], yt[part, slot], bias, 0.0, ALU.add, ALU.max))
                wait_steps()
                dve.wait_ge(x_exp, w + 1)
                nc.vector.scalar_tensor_tensor(xt[part, slot], xt[part, slot], -1.0, yt[part, slot],
                                               ALU.add, ALU.add).then_inc(x_mid, 1)

            def denominators(bank):
                mark(nc.vector.tensor_scalar(r_den[:], bank, EPS_SOFTMAX, None, ALU.add))
                wait_steps()
                nc.vector.reciprocal(r_den[:], r_den[:]).then_inc(rd_done, 1)

            dve.wait_ge(consts, 3)
            nc.vector.memset(pick_f, 0.0).then_inc(consts, 1)
            dve.wait_ge(consts, 4)
            mark(nc.vector.memset(pick_f[0:2, 0, :], 1.0))
            wait_steps()
            mark(nc.vector.tensor_scalar(pick_f[:, 1, :], pick_f[:, 0, :], -1.0, 1.0, ALU.mult, ALU.add))
            wait_steps()
            mark(copy(ones[:], ones_f))
            copy(pick[:], pick_f).then_inc(consts, 1)
            turn(0)
            nc.vector.memset(acc[:], 0.0).then_inc(acc_added, 8)
            dve.wait_ge(small_in, 32)
            dve.wait_ge(mask_in, 16)
            dve.wait_ge(cnt_in, 16)

            def rows_tile(x_head, parity, u):
                split_tile(x_head * 8 + u, u % 4, u // 4, rows[parity],
                           [(vec[:, v], al[:, parity, v]) for v in range(2)])

            def product_tile(j, u, into_first=False):
                n, m = u // 4, u % 4
                part = slice(n * HW, (n + 1) * HW)
                dve.wait_ge(prod_done, j * 4 + (u + 1))
                if into_first:
                    copy(acc[:, m, part], ps[:, m, 0:HW]).then_inc(acc_added, 1)
                else:
                    add(acc[:, m, part], acc[:, m, part], ps[:, m, 0:HW]).then_inc(acc_added, 1)

            def prob_slot(h, parity, s, with_last=True):
                if s >= 2:
                    low(h * 10 + (s - 2), s % 2, prob[:, 1, s - 2, :], prob[:, 0, s - 2, :])
                if s < NB:
                    exponent(h * 10 + s, s % 2, ks[:, parity, 0, s:s + 1], first=not with_last and s < 2)
                if 1 <= s <= NB:
                    weigh(h * 10 + (s - 1), (s - 1) % 2, count16[0][:, s - 1, :])

            def small_uv(h, parity, first=False):
                target = al[:, parity, 1]
                maxima(h * 5 + 2, mx, h + 1, None if first else h * 10)
                mark(add(mx[:], mx[:], target))
                leaky(mx[:])
                u_and_v(target, mx[:], uv[:, 0], uv[:, 1], [uvc[:, 0, 0, :, i] for i in range(4)]).then_inc(uv_ready, 1)

            def head(h, parity, j_rows, j_out, with_next, with_last):
                if with_next:
                    dve.wait_ge(vec_in, h * 16 + 32)
                    for u in range(8):
                        rows_tile(h + 1, 1 - parity, u)
                        if u == 2:
                            small_uv(h, parity, first=not with_last)
                    source_columns(al[:, 1 - parity, 0], (ks[:, 1 - parity, 0], ks[:, 1 - parity, 1]))
                else:
                    small_uv(h, parity)
                dve.wait_ge(misc_done, h * 5 + 4)
                dve.wait_ge(vb_ready, h + 1)
                for u in range(8):
                    if with_last:
                        product_tile(j_out, u)
                    if u < NB + 2:
                        prob_slot(h, parity, u, with_last)
                dve.wait_ge(misc_done, h * 5 + 5)
                denominators(ps[:, 6, :])
                dve.wait_ge(rd_done, h + 1)
                for s in range(KB + 2):
                    if s >= 2:
                        low(h * 10 + (4 + s - 2), s % 2, cols_y[0][:, 1, s - 2, :], cols_y[0][:, 0, s - 2, :])
                    if s < KB:
                        dve.wait_ge(agg_done, h * 6 + (s + 1))
                        elu_start(h * 10 + (4 + s), h * 6 + s, s % 2, ps[:, 4 + s % 2, :], b_cols[:, bass.ds(h * KB + s, 1)])
                    if 1 <= s <= KB:
                        elu_end(h * 10 + (4 + s - 1), (s - 1) % 2, b_cols[:, bass.ds(h * KB + (s - 1), 1)])

            dve.wait_ge(vec_in, 16)
            for u in range(8):
                rows_tile(0, 0, u)
            source_columns(al[:, 0, 0], (ks[:, 0, 0], ks[:, 0, 1]))
            head(0, 0, 2, None, True, False)
            base[0], local[0] = local[0], 0
            first_steps = base[0]
            with dve.Fori(0, 3) as i:
                for odd in range(2):
                    base[0], local[0] = i * (2 * HEAD_STEPS) + (first_steps + odd * HEAD_STEPS), 0
                    h = i * 2 + (1 + odd)
                    head(h, 1 - odd, h * 4, h * 4 + 2, True, True)
                    assert local[0] == HEAD_STEPS, local
            base[0], local[0] = first_steps + 6 * HEAD_STEPS, 0
            head(7, 1, None, 28, False, True)
            for u in range(8):
                product_tile(30, u)

            def split_rows(last_added=None):
                for m in range(NB):
                    mark(copy(rows[0][:, 0, m, :], acc[:, m, :]))
                wait_steps()
                for m in range(NB):
                    sub(rows[0][:, 1, m, :], acc[:, m, :], f32(rows[0][:, 0, m, :])).then_inc(rows_split, 1)

            dve.wait_ge(acc_added, 72)
            dve.wait_ge(vec_in, 144)
            split_rows()
            for m in range(NB):
                for v in range(2):
                    mark(dot(xt_row, acc[:, m, :], vec[:, v], 0.0, al[:, 0, v, m:m + 1]))
                    wait_steps()
            source_columns(al[:, 0, 0], (ks[:, 0, 0], ks[:, 0, 1]))
            small_uv(8, 0)
            dve.wait_ge(misc_done, 44)
            dve.wait_ge(vb_ready, 9)
            for s in range(NB + 2):
                prob_slot(8, 0, s)

            def read_denominators(misc, first):
                dve.wait_ge(misc_done, misc)
                bank = ps[:, 5, 0:2 * NB:2]
                if first:
                    copy(zc[:, 0], bank).then_inc(den_read, 1)
                else:
                    add(zc[:, 0], zc[:, 0], bank).then_inc(den_read, 1)

            def read_rows(done, first):
                for u in range(8):
                    n, m = u // 4, u % 4
                    part = slice(n * HW, (n + 1) * HW)
                    dve.wait_ge(row_done, done + u + 1)
                    if first:
                        copy(acc[:, m, part], ps[:, m, 0:HW]).then_inc(row_read, 1)
                    else:
                        add(acc[:, m, part], acc[:, m, part], ps[:, m, 0:HW]).then_inc(row_read, 1)

            def norm(layer, reads):
                dve.wait_ge(res_in, 16 * (2 + layer))
                dve.wait_ge(b_in, 16 * B_ROW_AT[layer])
                if layer < 2:
                    dve.wait_ge(row_read, reads)
                    dve.wait_ge(den_read, 1 + 3 * layer)
                    mark(nc.vector.tensor_scalar(zc[:, 0], zc[:, 0], EPS_SOFTMAX, None, ALU.add))
                    wait_steps()
                    mark(nc.vector.reciprocal(zc[:, 1], zc[:, 0]))
                    wait_steps()
                else:
                    dve.wait_ge(acc_added, reads)
                for m in range(NB):
                    if layer < 2:
                        mark(nc.vector.scalar_tensor_tensor(acc[:, m, :], acc[:, m, :], zc[:, 1, m:m + 1], resid[:, m, :],
                                                            ALU.mult, ALU.add))
                    else:
                        mark(add(acc[:, m, :], acc[:, m, :], resid[:, m, :]))
                wait_steps()
                for m in range(NB):
                    ins = add(acc[:, m, :], acc[:, m, :], b_row)
                    ins.then_inc(b_used, 1) if m == NB - 1 else mark(ins)
                dve.wait_ge(b_used, B_ROW_AT[layer])
                for m in range(NB):
                    for n in range(2):
                        ins = nc.vector.bn_stats(bn[:, m, n], acc[:, m, n * HW:(n + 1) * HW])
                mark(ins)
                wait_steps()
                for m in range(NB):
                    ins = nc.vector.bn_aggr(stat[:, m, :], bn[:, m].rearrange("p n s -> p (n s)"))
                mark(ins)
                wait_steps()
                nc.vector.tensor_scalar(stat[:, :, 1], stat[:, :, 1], EPS_NORM, None, ALU.add).then_inc(var_ready, 1)
                dve.wait_ge(sd_ready, SD_AT[layer])
                mark(nc.vector.reciprocal(sd[:, 1], sd[:, 0]))
                wait_steps()
                for m in range(NB):
                    ins = nc.vector.tensor_scalar(acc[:, m, :], acc[:, m, :], stat[:, m, 0:1], sd[:, 1, m:m + 1],
                                                  ALU.subtract, ALU.mult)
                ins.then_inc(acc_ready, 1)

            read_denominators(45, True)
            read_rows(0, True)
            norm(0, 8)
            turn(KB)

            def relation_uv(heads):
                span = slice(0, heads)
                z, target = mx1[:, :, span], al1[:, 1, :, span]
                mark(add(z, z, target))
                leaky(z)
                mark(nc.vector.tensor_tensor(mx1[:, 0, span], mx1[:, 0, span], mx1[:, 1, span], ALU.max))
                wait_steps()
                mark(nc.vector.tensor_tensor(mx1[:, 0, span], mx1[:, 0, span], mx1[:, 2, span], ALU.max))
                wait_steps()
                for r in range(REL3):
                    ins = u_and_v(target[:, r], mx1[:, 0, span], uv1[:, 0, r, span], uv1[:, 1, r, span],
                                  [uvc[:, r, span, :, i] for i in range(4)])
                    ins.then_inc(uv_ready, 1) if r == REL3 - 1 else mark(ins)

            def scale_sources(r, heads):
                span = slice(0, heads)
                for i, by in enumerate((1.0 - SLOPE, SLOPE)):
                    nc.vector.tensor_scalar(ks1[:, i, r, span], al1[:, 0, r, span], by, None, ALU.mult)

            dve.wait_ge(vec_in, 176)
            dots = [None] * REL3
            for r in range(REL3):
                for u in range(8):
                    if r and u % 2 == 0:
                        if u == 0:
                            dve.wait_ge(mask_in, 16 * (1 + r))
                        source_columns(al1[:, 0, r - 1, u // 2], None)
                    split_tile(64 + 8 * r + u, u % 4, u // 4, rows[r],
                               [((acc if v < 4 else vec4)[:, v % 4], al1[:, v // 4, r, v % 4]) for v in range(8)])
                    if r and u % 2 == 1:
                        maxima(45 + 8 * (r - 1) + u + 1, mx1[:, r - 1, u // 2], 9 + 4 * (r - 1) + u // 2 + 1, 84)
                scale_sources(r, HEADS1)
            dve.wait_ge(mask_in, 64)
            for h in range(HEADS1):
                source_columns(al1[:, 0, 2, h], None)
                maxima(61 + 2 * h + 2, mx1[:, 2, h], 18 + h, 84)
            relation_uv(HEADS1)
            dve.wait_ge(cnt_in, 64)
            for h in range(HEADS1):
                w0 = 84 + 14 * h
                for s in range(REL3 * NB + 2):
                    g = 3 * h + s // 4
                    if s >= 2:
                        low(w0 + s - 2, s % 2, prob[:, 1, (s - 2) % 4, :], prob[:, 0, (s - 2) % 4, :])
                    if s < REL3 * NB:
                        if s % 4 == 0:
                            dve.wait_ge(misc_done, 71 + 2 * g)
                            dve.wait_ge(vb_ready, 10 + g)
                        exponent(w0 + s, s % 2, ks1[:, 0, s // 4, h, s % 4:s % 4 + 1])
                    if 1 <= s <= REL3 * NB:
                        weigh(w0 + s - 1, (s - 1) % 2, count16[(s - 1) // 4][:, (s - 1) % 4, :])
                dve.wait_ge(p_used, 12 * (h + 1))
                denominators(ps[:, 4 + h % 2, :])
                dve.wait_ge(rd_done, 8 + h + 1)
                for c in range(4):
                    if c >= 2:
                        f, part = PIECES[2 * h + c - 2]
                        low(w0 + 12 + c - 2, c - 2, cols_x[part, 1, f, :], cols_x[part, 0, f, :], part)
                    if c < 2:
                        f, part = PIECES[2 * h + c]
                        elu_start(w0 + 12 + c, 48 + 2 * h + c, c, ps[:, 2 * (h % 2) + c, :], b_cols[part, HEADS0 * KB + f:HEADS0 * KB + f + 1], part)
                    if 1 <= c <= 2:
                        f, part = PIECES[2 * h + c - 1]
                        elu_end(w0 + 12 + c - 1, c - 1, b_cols[part, HEADS0 * KB + f:HEADS0 * KB + f + 1], part)

            dve.wait_ge(vec_in, 192)
            for r in range(REL3):
                for u in range(8):
                    if r and u == 0:
                        dve.wait_ge(mask_in, 16 * (4 + r))
                        source_columns(al1[:, 0, r - 1, 0], None)
                    split_tile(88 + 8 * r + u, u % 4, u // 4, rows[r], [(acc[:, v], al1[:, v, r, 0]) for v in range(2)])
                    if r and u == 1:
                        maxima(94 + 2 * (r - 1) + 1, mx1[:, r - 1, 0], 21 + r, 140)
                scale_sources(r, 1)
            dve.wait_ge(mask_in, 16 * 7)
            source_columns(al1[:, 0, 2, 0], None)
            maxima(99, mx1[:, 2, 0], 24, 140)
            relation_uv(1)
            for r in range(REL3):
                dve.wait_ge(misc_done, (101, 103, 106)[r])
                dve.wait_ge(vb_ready, 22 + r)
                w0 = 140 + 4 * r
                held = prob_sets[r % 2]
                for s in range(NB + 2):
                    if s >= 2:
                        low(w0 + s - 2, s % 2, held[:, 1, s - 2, :], held[:, 0, s - 2, :])
                    if s < NB:
                        exponent(w0 + s, s % 2, ks1[:, 0, r, 0, s:s + 1])
                    if 1 <= s <= NB:
                        weigh(w0 + s - 1, (s - 1) % 2, count16[r][:, s - 1, :])
                if r:
                    read_denominators((104, 107)[r - 1], r == 1)
                    if r == 2:
                        dve.wait_ge(row_read, 16)
                    read_rows(8 * r, r == 1)
            read_denominators(108, False)
            dve.wait_ge(row_read, 24)
            read_rows(24, False)
            norm(1, 32)
            dve.wait_ge(kept_out, 32)
            split_rows()
            turn(2 * KB)

            def count_low(number, src):
                dve.wait_ge(cnt_hi, number)
                sub(prob[:, 1], src, f32(prob[:, 0])).then_inc(cnt_lo, 1)

            def edge_tiles(number, scale, dst):
                for f in range(KB + 1):
                    t = number * KB + f
                    if f < KB:
                        dve.wait_ge(edge_done, t + 1)
                        if t >= 2:
                            dve.wait_ge(y_lo, t - 1)
                        nc.vector.tensor_tensor(xt[:, f % 2], ps[:, 4 + f % 2, :], scale, ALU.mult).then_inc(y_done, 1)
                    if f >= 1:
                        dve.wait_ge(y_hi, t)
                        sub(dst[:, 1, f - 1, :], xt[:, (f - 1) % 2], f32(dst[:, 0, f - 1, :])).then_inc(y_lo, 1)

            def add_bias(count, relu_too):
                dve.wait_ge(b_in, 16 * count)
                for m in range(NB):
                    ins = add(acc[:, m, :], acc[:, m, :], b_row)
                    ins.then_inc(b_used, 1) if m == NB - 1 else mark(ins)
                dve.wait_ge(b_used, count)
                for m in range(NB):
                    ins = nc.vector.tensor_scalar(acc[:, m, :], acc[:, m, :], 0.0, None, ALU.max)
                ins.then_inc(acc_ready, 1)

            added = 72
            for layer in range(3):
                for r in range(REL4):
                    number = 4 * layer + r
                    if r == 0:
                        count_low(number + 1, count16[0])
                    if layer == 0:
                        dve.wait_ge(misc_done, 108 + r + 1)
                        mark(nc.vector.tensor_scalar(scale_bc[:, r], ps[:, 6, :], 1.0, None, ALU.max))
                        wait_steps()
                        nc.vector.reciprocal(scale_bc[:, r], scale_bc[:, r]).then_inc(scale_ready, 1)
                        dve.wait_ge(scale_ready, r + 1)
                    edge_tiles(number, scale_bc[:, r], cols_y[r % 2])
                    if r + 1 < REL4:
                        count_low(number + 2, count16[0])
                    for u in range(8):
                        if r:
                            dve.wait_ge(acc_added, added)
                        product_tile(44 + 10 * layer + 2 * r, u, into_first=r == 0)
                    added += 8
                dve.wait_ge(acc_added, added)
                for u in range(8):
                    product_tile(52 + 10 * layer, u)
                added += 8
                dve.wait_ge(acc_added, added)
                if layer < 2:
                    add_bias(3 + layer, True)
                    dve.wait_ge(acc_ready, 3 + layer)
                    split_rows()
                    turn(KB * (3 + layer))
            norm(2, added)

            def split_scaled():
                for m in range(NB):
                    mark(nc.vector.tensor_scalar(acc[:, m, :], acc[:, m, :], zc[:, 1, m:m + 1], None, ALU.mult))
                wait_steps()
                split_rows()

            dve.wait_ge(cnt_in, 16 * 17)
            for m in range(NB):
                ins = add(count16[0][:, m, m * P:(m + 1) * P], count16[0][:, m, m * P:(m + 1) * P], ident[:])
            ins.then_inc(diag_added, 1)
            count_low(13, count16[0])
            dve.wait_ge(sd_ready, 4)
            mark(nc.vector.reciprocal(zc[:, 1], zc[:, 0]))
            nc.vector.reciprocal(scale_bc[:, 0], scale_bc[:, 0]).then_inc(scale_ready, 1)
            wait_steps()
            dve.wait_ge(scale_ready, 5)
            dve.wait_ge(kept_out, 48)
            for layer in range(2):
                split_scaled()
                edge_tiles(12 + layer, scale_bc[:, 0], cols_y[0])
                for u in range(8):
                    product_tile(74 + 2 * layer, u, into_first=True)
                added += 8
                dve.wait_ge(acc_added, added)
                if layer == 0:
                    add_bias(6, True)
                    dve.wait_ge(acc_ready, 6)
            norm(3, added)


def kernel(**inputs):
    import concourse.bacc as bacc
    from concourse.bass_utils import run_bass_kernel_spmd

    a = {name: np.ascontiguousarray(value) for name, value in inputs.items()}
    blocks = {}
    first0 = a["L0_gnn_W1"].reshape(D, HEADS0, D)
    second0 = a["L0_gnn_W2"].reshape(HEADS0, D, D)
    order = [first0[:, 0], first0[:, 1]]
    for h in range(HEADS0 - 2):
        order += [first0[:, h + 2], second0[h]]
    order += [second0[6], second0[7], *a["L1_gnn_W1"], *a["L1_gnn_W2"]]
    for i in "123":
        order += [a["L2_gnn_root" + i], *a["L2_gnn_W" + i]]
    order += [a["L3_gnn_W1"], a["L3_gnn_W2"]]
    weights = np.stack(order).reshape(WEIGHT_BLOCKS, 3, 2, P, 2, HW).transpose(0, 4, 1, 3, 2, 5)
    arrays = {
        "edges": np.stack([a["src"], a["dst"], a["edge_type_3"], a["edge_type_4"]]).reshape(4, P, CH).transpose(1, 0, 2),
        "x_rows": a["x"].reshape(NB, P, D).transpose(1, 0, 2),
        "weights": weights.reshape(2 * WEIGHT_BLOCKS, 3, P, 2 * HW),
        "attn0": np.stack([np.concatenate([a["L0_gnn_a_src1"], a["L0_gnn_a_src2"]]),
                           np.concatenate([a["L0_gnn_a_dst1"], a["L0_gnn_a_dst2"]])], 1),
        "attn1": np.stack([a["L1_gnn_k1"].T, a["L1_gnn_q1"].T]),
        "attn2": np.stack([a["L1_gnn_k2"].T, a["L1_gnn_q2"].T], 1),
        "bias_cols": np.concatenate([a["L0_gnn_b1"], a["L1_gnn_b1"]]).reshape(HEADS0 * KB + KB, P).T,
        "bias_rows": np.stack([a[n] for n in ("L0_gnn_b2", "L1_gnn_b2", "L2_gnn_b1", "L2_gnn_b2", "L2_gnn_b3",
                                              "L3_gnn_b1", "L3_gnn_b2")]),
    }
    arrays = {name: np.ascontiguousarray(value) for name, value in arrays.items()}

    nc = bacc.Bacc("TRN2", target_bir_lowering=False, num_devices=1)
    dram = {name: nc.dram_tensor(name, v.shape, mybir.dt.from_np(v.dtype), kind="ExternalInput").ap()
            for name, v in arrays.items()}
    out = nc.dram_tensor("out", [P, NB, D], F32, kind="ExternalOutput").ap()
    counts = nc.dram_tensor("counts", [8, P, NB, N], I16).ap()
    masks = nc.dram_tensor("masks", [4, P, NB, N], BF16).ap()
    flag = nc.dram_tensor("flag", [1, 1], I32).ap()
    kept = nc.dram_tensor("kept", [P, NB, D], F32).ap()
    count_edges(nc, dram["edges"], counts, masks, flag)
    graph_layers(nc, dram["x_rows"], dram["weights"], dram["attn0"], dram["attn1"], dram["attn2"],
                 dram["bias_cols"], dram["bias_rows"], counts, masks, flag, kept, out)
    got = run_bass_kernel_spmd(nc, [arrays], core_ids=[0]).results[0]["out"]
    return got.reshape(P, NB, D).transpose(1, 0, 2).reshape(N, D)
```

```python
from contextlib import ExitStack

import concourse.bass as bass
import numpy as np
from concourse import mybir

F32 = mybir.dt.float32
F32R = mybir.dt.float32r
BF16 = mybir.dt.bfloat16
F16 = mybir.dt.float16
I16 = mybir.dt.int16
I32 = mybir.dt.int32
ALU = mybir.AluOpType
ACT = mybir.ActivationFunctionType

P = 128
N = 512
D = 768
E = 8704
NB = N // P
KB = D // P
HW = D // 2
HEADS0 = 8
HEADS1 = 4
REL3 = 3
REL4 = 4
CH = E // P
NEG = -1.0e30
EPS_SOFTMAX = 1e-16
EPS_NORM = 1e-5
SLOPE = 0.2

GROUPS = [(0, 24), (24, 48), (48, CH)]
PACK = 2.0 ** -12
SHIFT = -0.375
ROUND = 1.5 * 2.0 ** 23
PAIRS = [(1, 0, 1, 0, 1), (1, 2, 3, 2, 3), (0, 0, 1, 4, 5)]
SLOT3 = 4
TOTAL = 7
BIG = 4096.0


def count_edges(nc, edges, counts, masks, flag):
    with ExitStack() as ctx:
        def sb(name, shape, dt):
            return ctx.enter_context(nc.sbuf_tensor(name, shape, dt))

        def sem(name):
            return ctx.enter_context(nc.semaphore(name))

        most_chunks = max(hi - lo for lo, hi in GROUPS)
        edge_i = sb("edge_i", [P, 4, CH], I32)
        edge_f = sb("edge_f", [P, 4, CH], F32)
        first = sb("first", [P, CH], F32)
        weight = sb("weight", [P, len(PAIRS), CH], F32)
        node_i = sb("node_i", [P, N], I32)
        node_f = sb("node_f", [P, N], F16)
        src_hot = sb("src_hot", [P, CH, N], BF16)
        dst_hot = sb("dst_hot", [P, most_chunks, N], BF16)
        packed = sb("packed", [P, 2, NB, N], F32)
        whole = sb("whole", [P, 2, NB, N], F32)
        sum_a = sb("sum_a", [P, 2, NB, N], F32)
        sum_b = sb("sum_b", [P, 2, NB, N], F32)
        total = sb("total", [P, NB, N], F32)
        rel_c = sb("rel_c", [P, NB, N], F32)
        out16 = sb("out16", [P, 4, NB, N], I16)
        most = sb("most", [P, 1], F32)
        most_row = sb("most_row", [1, 1], F32)
        flag_i = sb("flag_i", [1, 1], I32)
        ident_f = sb("ident_f", [P, P], F32)
        ident_b = sb("ident_b", [P, P], BF16)
        has_edge = src_hot[:, 0:4 * NB]
        mask = src_hot[:, 4 * NB:8 * NB]
        ps = ctx.enter_context(nc.psum_tensor("count_ps", [P, 2, NB, N], F32))

        def turned_tile(t, m):
            return ps[:, (t + 1) % 2, m].bitcast(BF16)[:, 0:N]

        edges_in = sem("edges_in")
        setup = sem("setup")
        iota_done = sem("iota_done")
        ident_done = sem("ident_done")
        hot_ready = sem("hot_ready")
        hot_used = sem("hot_used")
        tile_read = sem("tile_read")
        rounded = sem("rounded")
        summed = sem("summed")
        unpacked = sem("unpacked")
        scaled = sem("scaled")
        total_done = sem("total_done")
        out16_ready = sem("out16_ready")
        pairs_stored = sem("pairs_stored")
        stored = sem("stored")
        last_whole = sem("last_whole")
        last_part = sem("last_part")
        last_b = sem("last_b")
        last_a = sem("last_a")
        c_part = sem("c_part")
        c_ready = sem("c_ready")
        has_ready = sem("has_ready")
        turned = sem("turned")
        mask_act = sem("mask_act")
        mask_dve = sem("mask_dve")
        most_ready = sem("most_ready")
        flag_ready = sem("flag_ready")

        spans = [(CH * pair + lo, CH * pair + hi) for pair in range(len(PAIRS)) for lo, hi in GROUPS]
        per_pair = len(GROUPS)
        last = len(spans) - 1
        block = ctx.enter_context(nc.Block())

        @block.sync
        def _(sp):
            sp.dma_start(edge_i[:], edges).then_inc(edges_in, 16)
            order = [(PAIRS[0][4], 1), (PAIRS[0][3], 0), (PAIRS[1][4], 1), (PAIRS[1][3], 0), (TOTAL, 3),
                     (PAIRS[2][4], 1), (PAIRS[2][3], 0), (SLOT3 + 2, 2)]
            for done, (slot, half) in enumerate(order):
                sp.wait_ge(out16_ready, done + 1)
                sp.dma_start(counts[slot], out16[:, half]).then_inc(pairs_stored if done < 4 else stored, 16)
            for r, (ready, value) in enumerate(((mask_act, NB), (mask_dve, NB), (mask_act, 2 * NB), (mask_dve, 2 * NB))):
                sp.wait_ge(ready, value)
                sp.dma_start(masks[r], mask[:, r * NB:(r + 1) * NB]).then_inc(stored, 16)
            sp.wait_ge(flag_ready, 1)
            sp.dma_start(flag, flag_i[:]).then_inc(stored, 16)
            sp.wait_ge(pairs_stored, 16 * 4)
            sp.wait_ge(stored, 16 * (len(order) - 4 + 5))

        @block.gpsimd
        def _(pool):
            nc.gpsimd.iota(node_i[:], pattern=[[1, N]], base=0, channel_multiplier=0).then_inc(iota_done, 1)
            nc.gpsimd.memset(ident_f[:], 0.0).then_inc(summed, 1)
            pool.wait_ge(summed, 1)
            nc.gpsimd.affine_select(out=ident_f[:], in_=ident_f[:], compare_op=ALU.not_equal, fill=1.0, base=0,
                                    pattern=[[-1, P]], channel_multiplier=1).then_inc(ident_done, 1)
            steps = 1
            for group in range(last):
                pair, g = divmod(group, per_pair)
                slot = group % 2
                pool.wait_ge(rounded, group + 1)
                if g == 0:
                    if pair == 2:
                        pool.wait_ge(total_done, 1)
                    nc.gpsimd.tensor_tensor(sum_a[:, pair % 2], packed[:, slot], sum_b[:, pair % 2],
                                            ALU.subtract).then_inc(unpacked, 1)
                else:
                    nc.gpsimd.tensor_tensor(packed[:, slot], packed[:, slot], whole[:, slot], ALU.subtract).then_inc(summed, 1)
                    pool.wait_ge(unpacked, group)
                    nc.gpsimd.tensor_tensor(sum_b[:, pair % 2], sum_b[:, pair % 2], whole[:, slot], ALU.add).then_inc(summed, 1)
                    steps += 2
                    pool.wait_ge(summed, steps)
                    nc.gpsimd.tensor_tensor(sum_a[:, pair % 2], sum_a[:, pair % 2], packed[:, slot],
                                            ALU.add).then_inc(unpacked, 1)
                if g == per_pair - 1:
                    pool.wait_ge(scaled, pair + 1)
                    if pair == 0:
                        nc.gpsimd.tensor_tensor(total[:], sum_a[:, 0], sum_b[:, 0], ALU.add).then_inc(total_done, 1)
                    else:
                        pool.wait_ge(total_done, 1)
                        nc.gpsimd.tensor_tensor(total[:], total[:], sum_a[:, 1], ALU.add).then_inc(summed, 1)
                        steps += 1
                        pool.wait_ge(summed, steps)
                        nc.gpsimd.tensor_tensor(total[:], total[:], sum_b[:, 1], ALU.add).then_inc(total_done, 1)
            pool.wait_ge(total_done, 2)
            for m in range(NB):
                pool.wait_ge(last_b, m + 1)
                nc.gpsimd.tensor_tensor(rel_c[:, m], total[:, m], sum_b[:, 0, m], ALU.subtract).then_inc(c_part, 1)
            for m in range(NB):
                pool.wait_ge(c_part, m + 1)
                pool.wait_ge(scaled, 2 + m + 1)
                nc.gpsimd.tensor_tensor(rel_c[:, m], rel_c[:, m], sum_a[:, 0, m], ALU.subtract).then_inc(c_ready, 1)

        @block.scalar
        def _(act):
            def copy(dst, src, bias=0.0, scale=1.0):
                return nc.scalar.activation(dst, src, ACT.Copy, bias=bias, scale=scale)

            to_count = dict(scale=1.0 / PACK, bias=-SHIFT * per_pair / PACK)
            for group, (_, end) in enumerate(spans):
                act.wait_ge(hot_used, end)
                if group >= 2:
                    act.wait_ge(unpacked, group - 1)
                for m in range(NB):
                    copy(packed[:, group % 2, m], ps[:, group % 2, m], bias=SHIFT).then_inc(tile_read, 1)
                pair = group // per_pair - 1
                if pair >= 0 and group % per_pair == 0:
                    act.wait_ge(unpacked, group)
                    copy(sum_a[:, pair], sum_a[:, pair], **to_count).then_inc(scaled, 1)
                    if pair:
                        act.wait_ge(pairs_stored, 32)
                    copy(out16[:, 1], sum_b[:, pair]).then_inc(out16_ready, 1)
                    act.wait_ge(scaled, pair + 1)
                    copy(out16[:, 0], sum_a[:, pair]).then_inc(out16_ready, 1)
                if group == last - 1:
                    act.wait_ge(total_done, 2)
                    copy(out16[:, 3], total[:]).then_inc(out16_ready, 1)
            for m in range(NB):
                act.wait_ge(turned, m + 1)
                copy(mask[:, m], turned_tile(0, m), scale=-NEG, bias=NEG).then_inc(mask_act, 1)
            act.wait_ge(pairs_stored, 64)
            for m in range(NB):
                act.wait_ge(last_a, m + 1)
                copy(sum_a[:, 0, m], sum_a[:, 0, m], **to_count).then_inc(scaled, 1)
            act.wait_ge(last_b, NB)
            copy(out16[:, 1], sum_b[:, 0]).then_inc(out16_ready, 1)
            act.wait_ge(scaled, 2 + NB)
            copy(out16[:, 0], sum_a[:, 0]).then_inc(out16_ready, 1)
            for m in range(NB):
                act.wait_ge(turned, NB + m + 1)
                copy(mask[:, 2 * NB + m], turned_tile(1, m), scale=-NEG, bias=NEG).then_inc(mask_act, 1)
            act.wait_ge(c_ready, NB)
            copy(out16[:, 2], rel_c[:]).then_inc(out16_ready, 1)

        @block.vector
        def _(dve):
            n = [0]

            def step(ins):
                n[0] += 1
                ins.then_inc(setup, 1)
                dve.wait_ge(setup, n[0])

            dve.wait_ge(ident_done, 1)
            nc.vector.tensor_copy(ident_b[:], ident_f[:]).then_inc(ident_done, 1)
            dve.wait_ge(iota_done, 1)
            step(nc.vector.tensor_copy(node_f[:], node_i[:]))
            dve.wait_ge(edges_in, 16)
            step(nc.vector.tensor_copy(edge_f[:], edge_i[:]))
            for pair, (kinds, type_a, type_b, _, _) in enumerate(PAIRS):
                kind = edge_f[:, 2 + kinds, :]
                step(nc.vector.tensor_scalar(first[:], kind, float(type_a), PACK, ALU.is_equal, ALU.mult))
                step(nc.vector.scalar_tensor_tensor(weight[:, pair, :], kind, float(type_b), first[:],
                                                    ALU.is_equal, ALU.add))

            def one_hot(pair, c, slot):
                if pair == 0:
                    nc.vector.tensor_scalar(src_hot[:, bass.ds(c, 1)], node_f[:], edge_f[:, 0, bass.ds(c, 1)], None, ALU.is_equal)
                nc.vector.tensor_scalar(dst_hot[:, bass.ds(slot, 1)], node_f[:], edge_f[:, 1, bass.ds(c, 1)],
                                        weight[:, pair, bass.ds(c, 1)], ALU.is_equal, ALU.mult).then_inc(hot_ready, 1)

            def round_group(group):
                pair, g = divmod(group, per_pair)
                dve.wait_ge(tile_read, NB * (group + 1))
                if g == 0 and pair == 2:
                    dve.wait_ge(total_done, 1)
                    dve.wait_ge(out16_ready, 2)
                nc.vector.tensor_scalar(sum_b[:, pair % 2] if g == 0 else whole[:, group % 2], packed[:, group % 2],
                                        ROUND, -ROUND, ALU.add, ALU.add).then_inc(rounded, 1)

            for group, (begin, end) in enumerate(spans):
                pair = group // per_pair
                lo = begin - CH * pair
                with dve.Fori(0, (end - begin) // 2) as i:
                    for half in range(2):
                        if group:
                            dve.wait_ge(hot_used, i * 2 + (spans[group - 1][0] + half + 1))
                        one_hot(pair, i * 2 + (lo + half), i * 2 + half)
                if group:
                    round_group(group - 1)
            dve.wait_ge(hot_used, spans[last][0])
            dve.wait_ge(total_done, 2)
            for m in range(NB):
                nc.vector.tensor_scalar(has_edge[:, m], total[:, m], 1.0, None, ALU.min).then_inc(has_ready, 1)
            nc.vector.tensor_reduce(most[:], total[:], mybir.AxisListType.XY, ALU.max).then_inc(most_ready, 1)
            slot = last % 2
            for m in range(NB):
                dve.wait_ge(tile_read, NB * last + m + 1)
                nc.vector.tensor_scalar(whole[:, slot, m], packed[:, slot, m], ROUND, -ROUND, ALU.add, ALU.add).then_inc(last_whole, 1)
            dve.wait_ge(unpacked, last)
            for m in range(NB):
                dve.wait_ge(last_whole, m + 1)
                nc.vector.tensor_tensor(packed[:, slot, m], packed[:, slot, m], whole[:, slot, m], ALU.subtract).then_inc(last_part, 1)
            for m in range(NB):
                dve.wait_ge(last_part, m + 1)
                nc.vector.tensor_tensor(sum_a[:, 0, m], sum_a[:, 0, m], packed[:, slot, m], ALU.add).then_inc(last_a, 1)
            for m in range(NB):
                nc.vector.tensor_tensor(sum_b[:, 0, m], sum_b[:, 0, m], whole[:, slot, m], ALU.add).then_inc(last_b, 1)
            for m in range(NB):
                dve.wait_ge(last_b, m + 1)
                nc.vector.tensor_scalar(has_edge[:, NB + m], sum_b[:, 0, m], 1.0, None, ALU.min).then_inc(has_ready, 1)
            for m in range(NB):
                dve.wait_ge(scaled, 2 + m + 1)
                nc.vector.tensor_scalar(has_edge[:, 2 * NB + m], sum_a[:, 0, m], 1.0, None, ALU.min).then_inc(has_ready, 1)
            for m in range(NB):
                dve.wait_ge(c_ready, m + 1)
                nc.vector.tensor_scalar(has_edge[:, 3 * NB + m], rel_c[:, m], 1.0, None, ALU.min).then_inc(has_ready, 1)
            for t, row in ((2, 1), (3, 3)):
                for m in range(NB):
                    dve.wait_ge(turned, NB * t + m + 1)
                    nc.vector.tensor_scalar(mask[:, NB * row + m], turned_tile(t, m), 1.0, -NEG,
                                            ALU.subtract, ALU.mult).then_inc(mask_dve, 1)
            dve.wait_ge(turned, 4 * NB + 1)
            step(nc.vector.tensor_reduce(most_row[:], ps[0:1, 1, 0, 0:P], mybir.AxisListType.X, ALU.max))
            nc.vector.tensor_scalar(flag_i[:], most_row[:], BIG, None, ALU.is_ge).then_inc(flag_ready, 1)

        @block.tensor
        def _(pe):
            for group, (begin, end) in enumerate(spans):
                bank = group % 2
                lo = begin % CH
                if group >= 2:
                    pe.wait_ge(tile_read, NB * (group - 1))

                def chunk(index, start, stop):
                    pe.wait_ge(hot_ready, index + (begin + 1))
                    for m in range(NB):
                        mm = nc.tensor.matmul(ps[:, bank, m], src_hot[:, bass.ds(index + lo, 1), m * P:(m + 1) * P],
                                              dst_hot[:, bass.ds(index, 1)], start=start, stop=stop, skip_group_check=True)
                    mm.then_inc(hot_used, 1)

                chunk(0, True, False)
                with pe.Fori(0, (end - begin - 2) // 2) as i:
                    chunk(i * 2 + 1, False, False)
                    chunk(i * 2 + 2, False, False)
                chunk(end - begin - 1, False, True)
            pe.wait_ge(ident_done, 2)
            for t in range(4):
                for m in range(NB):
                    if t == 0:
                        pe.wait_ge(tile_read, NB * last)
                    elif t == 1:
                        pe.wait_ge(tile_read, NB * (last + 1))
                    else:
                        pe.wait_ge(mask_act, NB * (t - 2) + m + 1)
                    pe.wait_ge(has_ready, NB * (t + 1))
                    for s in range(NB):
                        mm = nc.tensor.transpose(turned_tile(t, m)[:, s * P:(s + 1) * P],
                                                 has_edge[:, NB * t + s, m * P:(m + 1) * P], ident_b[:])
                    mm.then_inc(turned, 1)
            pe.wait_ge(most_ready, 1)
            pe.wait_ge(mask_dve, 1)
            nc.tensor.transpose(ps[0:1, 1, 0, 0:P], most[:], ident_f[:]).then_inc(turned, 1)


WEIGHT_BLOCKS = 2 * HEADS0 + 2 * REL3 + 3 * (REL4 + 1) + 2
NORM_AT = (1, 2, 5, 7)
B_ROW_AT = (1, 2, 5, 7)
SD_AT = (1, 2, 3, 5)
HEAD_STEPS = 33
PIECES = [(0, slice(0, P)), (1, slice(0, 64)), (1, slice(64, P)), (2, slice(0, P)),
          (3, slice(0, P)), (4, slice(0, 64)), (4, slice(64, P)), (5, slice(0, P))]


def graph_layers(nc, x, weights, attn0, attn1, attn2, bias_cols, bias_rows, counts, masks, flag, kept, out):
    PASSES = 2 * WEIGHT_BLOCKS
    with ExitStack() as ctx:
        def sb(name, shape, dt):
            return ctx.enter_context(nc.sbuf_tensor(name, shape, dt))

        def sem(name):
            return ctx.enter_context(nc.semaphore(name))

        cols_x = sb("cols_x", [P, 2, KB, N], F32R)
        wide = [sb(f"wide{i}", [P, 2, KB * N], F32R) for i in range(3)]
        prob = sb("prob", [P, 2, NB, N], F32R)
        w_pair = sb("w_pair", [P, 2, 2, KB, HW], F32R)
        w_raw = sb("w_raw", [P, 3, 2, HW], F32)
        acc = sb("acc", [P, NB, D], F32)
        multi = sb("multi", [P, NB * D], F32)
        mask = sb("edge_mask", [P, NB, N], BF16)
        xt = sb("xt", [P, 2, N], F32)
        yt = sb("yt", [P, 2, N], F32)
        hv = sb("hv", [P, 2, HW], F32)
        v_bc = sb("v_bc", [P, N], F32)
        r_den = sb("r_den", [P, N], F32)
        q_rows = sb("q_rows", [4, N], F32R)
        ident = sb("ident", [P, P], F32)
        ones = sb("ones", [P, P], F32R)
        pick = sb("pick", [4, 2, P], F32R)
        b_cols = sb("b_cols", [P, HEADS0 * KB + KB], F32)
        al_part = sb("al_part", [P, 8, NB], F32)
        al = sb("al", [P, 2, 2, NB], F32)
        al1 = sb("al1", [P, 2, REL3, HEADS1, NB], F32)
        kc = sb("kc", [P, NB, 2], F32)
        ks = sb("ks", [P, 2, 2, NB], F32)
        ks1 = sb("ks1", [P, 2, REL3, HEADS1, NB], F32)
        mx = sb("mx", [P, NB], F32)
        mx1 = sb("mx1", [P, REL3, HEADS1, NB], F32)
        uv = sb("uv", [P, 2, NB], F32)
        uv1 = sb("uv1", [P, 2, REL3, HEADS1, NB], F32)
        uvc = sb("uvc", [P, REL3, HEADS1, NB, 4], F32)
        zc = sb("zc", [P, 2, NB], F32)
        bn = sb("bn", [P, NB, 2, 6], F32)
        stat = sb("stat", [P, NB, 2], F32)
        sd = sb("sd", [P, 2, NB], F32)
        waited = sb("waited", [P, 1], F32)
        flag_sb = sb("flag_sb", [1, 1], I32)
        rows = [wide[i][:].rearrange("p a (m f) -> p a m f", m=NB) for i in range(3)]
        cols_y = [wide[i][:].rearrange("p a (k n) -> p a k n", k=KB) for i in (2, 1)]
        prob_sets = [prob, cols_x]
        count16 = [multi[:, 1024 * r:1024 * (r + 1)].bitcast(I16).rearrange("p (m n) -> p m n", m=NB) for r in range(3)]
        vec = multi[:, 1024:1024 + 2 * D].rearrange("p (a f) -> p a f", a=2)
        vec4 = multi[:].rearrange("p (a f) -> p a f", a=NB)
        resid = multi[:].rearrange("p (m f) -> p m f", m=NB)
        scale_bc = multi[:, 1024:].rearrange("p (r n) -> p r n", r=REL4)
        y_tiles = [yt[:, 0], yt[:, 1], multi[:, 2560:2560 + N]]
        ones_f = xt[:, 0, 0:P]
        pick_f = yt[0:4, :, 0:P]
        b_row = yt[:].rearrange("p a n -> p (a n)")[:, 0:D]
        xt_row = xt[:].rearrange("p a n -> p (a n)")[:, 0:D]
        ps = ctx.enter_context(nc.psum_tensor("ps", [P, 8, N], F32))

        raw_in = [sem(f"raw_in{p}") for p in range(3)]
        consts = sem("consts")
        w_high = sem("w_high")
        w_low = sem("w_low")
        prod_done = sem("prod_done")
        tile_copied = sem("tile_copied")
        rows_ready = sem("rows_ready")
        rows_split = sem("rows_split")
        acc_added = sem("acc_added")
        agg_done = sem("agg_done")
        agg_read = sem("agg_read")
        misc_done = sem("misc_done")
        kc_ready = sem("kc_ready")
        uv_ready = sem("uv_ready")
        q_ready = sem("q_ready")
        vb_ready = sem("vb_ready")
        rd_done = sem("rd_done")
        max_done = sem("max_done")
        b_used = sem("b_used")
        diag_added = sem("diag_added")
        out_done = sem("out_done")
        den_read = sem("den_read")
        x_pre = sem("x_pre")
        x_exp = sem("x_exp")
        x_mid = sem("x_mid")
        x_hi = sem("x_hi")
        x_lo = sem("x_lo")
        p_used = sem("p_used")
        row_done = sem("row_done")
        row_read = sem("row_read")
        turn_done = sem("turn_done")
        turn_hi = sem("turn_hi")
        turn_lo = sem("turn_lo")
        cnt_hi = sem("cnt_hi")
        cnt_lo = sem("cnt_lo")
        edge_done = sem("edge_done")
        y_done = sem("y_done")
        y_hi = sem("y_hi")
        y_lo = sem("y_lo")
        scale_ready = sem("scale_ready")
        var_ready = sem("var_ready")
        sd_ready = sem("sd_ready")
        acc_ready = sem("acc_ready")
        step = sem("step")
        vec_in = sem("vec_in")
        cnt_in = sem("cnt_in")
        mask_in = sem("mask_in")
        res_in = sem("res_in")
        b_in = sem("b_in")
        small_in = sem("small_in")
        kept_out = sem("kept_out")

        block = ctx.enter_context(nc.Block())

        @block.sync
        def _(sp):
            for p in range(3):
                sp.dma_start(w_raw[:, p], weights[0, p]).then_inc(raw_in[p], 16)
            with sp.Fori(1, PASSES) as j:
                for p in range(3):
                    sp.wait_ge(w_low, j * 3 + (p - 2))
                    sp.dma_start(w_raw[:, p], weights[bass.ds(j, 1), p]).then_inc(raw_in[p], 16)

        @block.gpsimd
        def _(pool):
            nc.gpsimd.memset(ident[:], 0.0).then_inc(consts, 1)
            nc.gpsimd.memset(ones_f, 1.0).then_inc(consts, 1)
            pool.wait_ge(consts, 2)
            nc.gpsimd.affine_select(out=ident[:], in_=ident[:], compare_op=ALU.not_equal, fill=1.0, base=0,
                                    pattern=[[-1, P]], channel_multiplier=1).then_inc(consts, 1)
            with pool.Fori(0, PASSES // 2) as i:
                for slot in range(2):
                    for p in range(3):
                        pool.wait_ge(w_high, i * 6 + (3 * slot + p + 1))
                        nc.gpsimd.tensor_tensor(w_pair[:, slot, 1, 2 * p:2 * p + 2, :], w_raw[:, p],
                                                w_pair[:, slot, 0, 2 * p:2 * p + 2, :].bitcast(F32),
                                                ALU.subtract).then_inc(w_low, 1)

        @block.tensor
        def _(pe):
            def product(j, m, left, free, value):
                pe.wait_ge(free, value)
                for k in range(KB):
                    if m == 0 and k % 2 == 0:
                        pe.wait_ge(w_low, j * 3 + (k // 2 + 1))
                    for a, b in ((0, 0), (0, 1), (1, 0)):
                        mm = nc.tensor.matmul(ps[:, m, 0:HW], left[:, a, k, m * P:(m + 1) * P], w_pair[:, slot_of[0], b, k, :],
                                              start=(k == 0 and a + b == 0), stop=(k == KB - 1 and a == 1))
                mm.then_inc(prod_done, 1)

            slot_of = [0]

            def turn_small(table, width):
                for m in range(NB):
                    mm = nc.tensor.transpose(ps[0:width, 6, m * P:(m + 1) * P], table[:, m, :], ident[:])
                mm.then_inc(misc_done, 1)

            def spread_source():
                nc.tensor.matmul(ps[:, 7, :], ones[0:2, :], q_rows[0:2, :], start=True, stop=True).then_inc(misc_done, 1)

            def spread_uv():
                nc.tensor.matmul(ps[:, 7, :], pick[:, 0, :], q_rows[:], start=True, stop=True)
                nc.tensor.matmul(ps[:, 6, :], pick[:, 1, :], q_rows[:], start=True, stop=True).then_inc(misc_done, 1)

            def turn(count):
                for f in range(KB):
                    if f >= 2:
                        pe.wait_ge(turn_lo, count + f - 1)
                    for m in range(NB):
                        mm = nc.tensor.transpose(ps[:, 4 + f % 2, m * P:(m + 1) * P], acc[:, m, f * P:(f + 1) * P], ident[:])
                    mm.then_inc(turn_done, 1)

            pe.wait_ge(consts, 5)
            pe.wait_ge(small_in, 32)
            many = pe.value_load(flag_sb[0:1, 0:1], min_val=0, max_val=1)
            pe.wait_ge(res_in, 16)
            turn(0)

            def head(h, parity, j_rows, j_out, with_next, with_last):
                if with_next:
                    for u in range(8):
                        n, m = u // 4, u % 4
                        slot_of[0] = n
                        if n == 0:
                            if with_last:
                                pe.wait_ge(acc_added, h * 8 + (m - 3))
                            product(j_rows, m, cols_x, tile_copied, h * 8 + (4 + m + 1))
                        else:
                            product(j_rows + 1, m, cols_x, tile_copied, h * 8 + (8 + m + 1))
                        if u == 0:
                            pe.wait_ge(kc_ready, h + 1)
                            if with_last:
                                pe.wait_ge(rd_done, h)
                            turn_small(kc, 2)
                        elif u == 1:
                            pe.wait_ge(q_ready, h * 2 + 1)
                            if with_last:
                                pe.wait_ge(x_pre, h * 10)
                            spread_source()
                        elif u == 3:
                            pe.wait_ge(uv_ready, h + 1)
                            turn_small(uvc[:, 0, 0], 4)
                        elif u == 5:
                            pe.wait_ge(q_ready, h * 2 + 2)
                            spread_uv()
                else:
                    pe.wait_ge(kc_ready, h + 1)
                    pe.wait_ge(rd_done, h)
                    turn_small(kc, 2)
                    pe.wait_ge(q_ready, h * 2 + 1)
                    spread_source()
                    pe.wait_ge(uv_ready, h + 1)
                    turn_small(uvc[:, 0, 0], 4)
                    pe.wait_ge(q_ready, h * 2 + 2)
                    spread_uv()
                if with_last:
                    out_product(h - 1, j_out, tile_copied if with_next else None)
                pe.wait_ge(x_lo, h * 10 + 4)
                pe.wait_ge(vb_ready, h + 1)
                for s in range(NB):
                    for a in range(2):
                        mm = nc.tensor.matmul(ps[:, 6, :], ones[:], prob[:, a, s, :], start=(s + a == 0), stop=(s + a == NB))
                mm.then_inc(misc_done, 1)
                pe.wait_ge(rows_ready, h * 8 + 8)
                for f in range(KB):
                    if with_last or f >= 2:
                        pe.wait_ge(agg_read, h * 6 + (f - 1))
                    for s in range(NB):
                        for a, b in ((0, 0), (0, 1), (1, 0)):
                            mm = nc.tensor.matmul(ps[:, 4 + f % 2, :], rows[parity][:, a, s, f * P:(f + 1) * P], prob[:, b, s, :],
                                                  start=(s + a + b == 0), stop=(s == NB - 1 and a == 1))
                    mm.then_inc(agg_done, 1)

            def out_product(x_head, j, before):
                pe.wait_ge(x_lo, x_head * 10 + 10)
                for u in range(8):
                    n, m = u // 4, u % 4
                    slot_of[0] = n
                    if n == 0 and before is tile_copied:
                        product(j, m, cols_y[0], tile_copied, x_head * 8 + (16 + 4 + m + 1))
                    else:
                        product(j + n, m, cols_y[0], acc_added, x_head * 8 + (4 + m + 1 if n == 0 else 8 + m + 1))

            pe.wait_ge(turn_lo, KB)
            for u in range(8):
                slot_of[0] = u // 4
                if u < 4:
                    product(0, u % 4, cols_x, turn_lo, KB)
                else:
                    product(1, u % 4, cols_x, tile_copied, u % 4 + 1)
            head(0, 0, 2, None, True, False)
            with pe.Fori(0, 3) as i:
                for odd in range(2):
                    h = i * 2 + (1 + odd)
                    head(h, 1 - odd, h * 4, h * 4 + 2, True, True)
            head(7, 1, None, 28, False, True)
            out_product(7, 30, acc_added)

            pe.wait_ge(kc_ready, 9)
            turn_small(kc, 2)
            pe.wait_ge(q_ready, 17)
            spread_source()
            pe.wait_ge(uv_ready, 9)
            turn_small(uvc[:, 0, 0], 4)
            pe.wait_ge(q_ready, 18)
            spread_uv()

            def row_sums(source, weights_of, first_sem, first_value, units):
                for m in range(NB):
                    for s in range(NB):
                        for a in range(2):
                            mm = nc.tensor.matmul(ps[:, 5, 2 * m:2 * m + 2], weights_of[:, a, s, m * P:(m + 1) * P], ones[:, 0:2],
                                                  start=(s + a == 0), stop=(s + a == NB))
                mm.then_inc(misc_done, 1)
                for u in range(8):
                    n, m = u // 4, u % 4
                    if n == 0:
                        pe.wait_ge(first_sem, first_value + m)
                    else:
                        pe.wait_ge(row_read, units + m + 1)
                    for s in range(NB):
                        for a, b in ((0, 0), (0, 1), (1, 0)):
                            mm = nc.tensor.matmul(ps[:, m, 0:HW], weights_of[:, a, s, m * P:(m + 1) * P],
                                                  source[:, b, s, n * HW:(n + 1) * HW],
                                                  start=(s + a + b == 0), stop=(s == NB - 1 and a == 1))
                    mm.then_inc(row_done, 1)

            pe.wait_ge(x_lo, 84)
            pe.wait_ge(rows_split, NB)
            row_sums(rows[0], prob, acc_added, 69, 0)
            pe.wait_ge(acc_ready, 1)
            turn(KB)

            def max_round(kc_count, q_count, part):
                if part == 0:
                    pe.wait_ge(kc_ready, kc_count)
                    turn_small(kc, 2)
                else:
                    pe.wait_ge(q_ready, q_count)
                    spread_source()

            pe.wait_ge(turn_lo, 2 * KB)
            for r in range(REL3):
                for u in range(8):
                    n, m = u // 4, u % 4
                    slot_of[0] = n
                    if r == 0 and n == 0:
                        product(32, m, cols_x, row_read, 4 + m + 1)
                    else:
                        product(32 + 2 * r + n, m, cols_x, tile_copied, 64 + 8 * r + 4 * n - 4 + m + 1)
                    if r:
                        max_round(9 + 4 * (r - 1) + u // 2 + 1, 18 + 4 * (r - 1) + u // 2 + 1, u % 2)
            for h in range(HEADS1):
                for part in range(2):
                    max_round(18 + h, 27 + h, part)
            pe.wait_ge(uv_ready, 10)
            turn_small(uvc[:, 0, 0], 4)
            pe.wait_ge(q_ready, 31)
            spread_uv()
            pe.wait_ge(tile_copied, 88)
            pe.wait_ge(rows_ready, 88)
            for g in range(REL3 * HEADS1):
                h, r = g // REL3, g % REL3
                if g + 1 < REL3 * HEADS1:
                    pe.wait_ge(vb_ready, 10 + g)
                    turn_small(uvc[:, (g + 1) % REL3, (g + 1) // REL3], 4)
                if r == 0 and h >= 2:
                    pe.wait_ge(agg_read, 48 + 2 * (h - 1))
                    pe.wait_ge(rd_done, 8 + h - 1)
                chunk0 = (0, 1, 3, 4)[h]
                w0 = 84 + 14 * h + 4 * r
                for s in range(NB):
                    if s == 2 and g + 1 < REL3 * HEADS1:
                        pe.wait_ge(q_ready, 32 + g)
                        pe.wait_ge(x_pre, w0 + 4)
                        spread_uv()
                    pe.wait_ge(x_lo, w0 + s + 1)
                    begin, end = r == 0 and s == 0, r == REL3 - 1 and s == NB - 1
                    for a in range(2):
                        nc.tensor.matmul(ps[:, 4 + h % 2, :], ones[:], prob[:, a, s, :], start=(begin and a == 0), stop=(end and a == 1))
                    for c in range(2):
                        f = chunk0 + c
                        for a, b in ((0, 0), (0, 1), (1, 0)):
                            mm = nc.tensor.matmul(ps[:, 2 * (h % 2) + c, :], rows[r][:, a, s, f * P:(f + 1) * P], prob[:, b, s, :],
                                                  start=(begin and a + b == 0), stop=(end and a == 1))
                    mm.then_inc(p_used, 1)

            pe.wait_ge(x_lo, 140)
            for r in range(REL3):
                for u in range(8):
                    n, m = u // 4, u % 4
                    slot_of[0] = n
                    if r == 0 and n == 0:
                        product(38, m, cols_x, agg_read, 56)
                    else:
                        product(38 + 2 * r + n, m, cols_x, tile_copied, 88 + 8 * r + 4 * n - 4 + m + 1)
                    if r and u < 2:
                        max_round(21 + r, 42 + r, u)
            for part in range(2):
                max_round(24, 45, part)

            def uv_round(r, x_count):
                pe.wait_ge(uv_ready, 11)
                pe.wait_ge(vb_ready, 21 + r)
                turn_small(uvc[:, r, 0], 4)
                pe.wait_ge(q_ready, 46 + r)
                pe.wait_ge(x_pre, x_count)
                spread_uv()

            uv_round(0, 140)
            uv_round(1, 144)
            pe.wait_ge(x_lo, 144)
            pe.wait_ge(rows_ready, 112)
            row_sums(rows[0], prob_sets[0], tile_copied, 109, 8)
            uv_round(2, 148)
            pe.wait_ge(x_lo, 148)
            pe.wait_ge(den_read, 2)
            row_sums(rows[1], prob_sets[1], row_read, 13, 16)
            pe.wait_ge(x_lo, 152)
            pe.wait_ge(den_read, 3)
            row_sums(rows[2], prob_sets[0], row_read, 21, 24)
            pe.wait_ge(acc_ready, 2)
            turn(2 * KB)

            def edge_sums(number, cnt):
                pe.wait_ge(cnt_lo, cnt)
                for f in range(KB):
                    t = number * KB + f
                    if t >= 2:
                        pe.wait_ge(y_done, t - 1)
                    bank = ps[:, 4 + f % 2, :]
                    nc.tensor.matmul(bank, rows[0][:, 0, 0, f * P:(f + 1) * P], prob[:, 0, 0, :], start=True, stop=False)
                    with pe.If(many > 0):
                        for s in range(NB):
                            for a in range(2):
                                nc.tensor.matmul(bank, rows[0][:, a, s, f * P:(f + 1) * P], prob[:, 1, s, :], start=False, stop=False)
                    for s in range(NB):
                        for a in range(2):
                            if s + a:
                                mm = nc.tensor.matmul(bank, rows[0][:, a, s, f * P:(f + 1) * P], prob[:, 0, s, :],
                                                      start=False, stop=(s + a == NB))
                    mm.then_inc(edge_done, 1)

            def degrees(spread_only):
                for s in range(NB):
                    for a in range(2):
                        mm = nc.tensor.matmul(ps[:, 6, :], ones[:], prob[:, a, s, :], start=(s + a == 0), stop=(s + a == NB))
                if not spread_only:
                    for m in range(NB):
                        for s in range(NB):
                            for a in range(2):
                                mm = nc.tensor.matmul(ps[:, 7, 2 * m:2 * m + 2], prob[:, a, s, m * P:(m + 1) * P], ones[:, 0:2],
                                                      start=(s + a == 0), stop=(s + a == NB))
                mm.then_inc(misc_done, 1)

            def layer_product(j, left, added):
                for u in range(8):
                    n, m = u // 4, u % 4
                    slot_of[0] = n
                    product(j + n, m, left, acc_added, added + 4 * n - 4 + m + 1)

            added = 72
            pe.wait_ge(row_read, 32)
            for layer in range(3):
                pe.wait_ge(rows_split, NB * (2 + layer))
                for r in range(REL4):
                    if layer == 0:
                        pe.wait_ge(cnt_lo, r + 1)
                        if r:
                            pe.wait_ge(scale_ready, r)
                        degrees(True)
                    edge_sums(4 * layer + r, 4 * layer + r + 1)
                    if r == 0:
                        pe.wait_ge(turn_lo, KB * (3 + layer))
                        layer_product(44 + 10 * layer, cols_x, added)
                    else:
                        pe.wait_ge(y_lo, KB * (4 * layer + r))
                        layer_product(44 + 10 * layer + 2 * r, cols_y[(r - 1) % 2], added)
                    added += 8
                pe.wait_ge(y_lo, KB * (4 * layer + 4))
                layer_product(52 + 10 * layer, cols_y[1], added)
                added += 8
                pe.wait_ge(acc_ready, 3 + layer)
                if layer < 2:
                    turn(KB * (3 + layer))
            pe.wait_ge(cnt_lo, 13)
            pe.wait_ge(scale_ready, REL4)
            degrees(False)
            for layer in range(2):
                pe.wait_ge(rows_split, NB * (5 + layer))
                edge_sums(12 + layer, 13)
                pe.wait_ge(y_lo, KB * (13 + layer))
                layer_product(74 + 2 * layer, cols_y[0], added)
                added += 8

        @block.scalar
        def _(act):
            def copy(dst, src):
                return nc.scalar.activation(dst, src, ACT.Copy)

            def split_high(j, slot, wait=True):
                for p in range(3):
                    act.wait_ge(raw_in[p], j * 16 + 16)
                    if p == 0 and wait:
                        act.wait_ge(prod_done, j * 4 - 4)
                    copy(w_pair[:, slot, 0, 2 * p:2 * p + 2, :], w_raw[:, p]).then_inc(w_high, 1)

            def copy_tile(j, m, q, first=False):
                act.wait_ge(prod_done, j * 4 + (m + 1))
                if not first:
                    act.wait_ge(rows_ready, q - 1)
                copy(hv[:, m % 2], ps[:, m, 0:HW]).then_inc(tile_copied, 1)

            def copy_rows(count, width):
                act.wait_ge(misc_done, count)
                copy(q_rows[0:width, :], ps[0:width, 6, :]).then_inc(q_ready, 1)

            def copy_v(count):
                act.wait_ge(misc_done, count)
                copy(v_bc[:], ps[:, 6, :]).then_inc(vb_ready, 1)

            def exponential(w, slot, bias):
                act.wait_ge(x_pre, w + 1)
                nc.scalar.activation(xt[:, slot], xt[:, slot], ACT.Exp, bias=bias).then_inc(x_exp, 1)

            def elu_exponential(w, slot, y, bias, part=slice(0, P)):
                act.wait_ge(x_pre, w + 1)
                nc.scalar.activation(xt[part, slot], xt[part, slot], ACT.Exp)
                nc.scalar.activation(y[part], y[part], ACT.Identity, bias=bias).then_inc(x_exp, 1)

            def high(w, y, dst, part=slice(0, P)):
                act.wait_ge(x_mid, w + 1)
                copy(dst, y[part]).then_inc(x_hi, 1)

            def turn(count):
                for f in range(KB):
                    act.wait_ge(turn_done, count + f + 1)
                    copy(cols_x[:, 0, f, :], ps[:, 4 + f % 2, :]).then_inc(turn_hi, 1)

            act.dma_start(acc[:], x).then_inc(res_in, 16)
            act.dma_start(b_cols[:], bias_cols).then_inc(small_in, 16)
            act.dma_start(flag_sb[:], flag).then_inc(small_in, 16)
            act.dma_start(vec, attn0[0:1].partition_broadcast(P)).then_inc(vec_in, 16)
            act.dma_start(count16[0], counts[TOTAL]).then_inc(cnt_in, 16)
            act.dma_start(mask[:], masks[0]).then_inc(mask_in, 16)
            split_high(0, 0, wait=False)
            split_high(1, 1, wait=False)
            turn(0)

            def head(h, parity, j_rows, j_out, with_next, with_last):
                if with_next:
                    for u in range(8):
                        n, m = u // 4, u % 4
                        copy_tile(j_rows + n, m, h * 8 + (8 + u))
                        if u == 0:
                            copy_rows(h * 5 + 1, 2)
                        elif u == 3:
                            split_high(j_rows + 2, 0)
                            copy_rows(h * 5 + 3, 4)
                        elif u == 5:
                            copy_v(h * 5 + 4)
                    split_high(j_rows + 3, 1)
                    act.wait_ge(rows_ready, h * 8 + 16)
                    act.dma_start(vec, attn0[bass.ds(h + 2, 1)].partition_broadcast(P)).then_inc(vec_in, 16)
                else:
                    copy_rows(h * 5 + 1, 2)
                    copy_rows(h * 5 + 3, 4)
                    copy_v(h * 5 + 4)
                for s in range(NB + 1):
                    if s < NB:
                        exponential(h * 10 + s, s % 2, ks[:, parity, 1, s:s + 1])
                    if s >= 1:
                        high(h * 10 + (s - 1), y_tiles[(s - 1) % 2], prob[:, 0, s - 1, :])
                    if s == 3 and with_last:
                        split_high(j_out + 2, 0)
                if with_last:
                    split_high(j_out + 3, 1)
                for f in range(KB + 1):
                    if f < KB:
                        elu_exponential(h * 10 + (4 + f), f % 2, y_tiles[f % 3], b_cols[:, bass.ds(h * KB + f, 1)])
                    if f >= 1:
                        high(h * 10 + (4 + f - 1), y_tiles[(f - 1) % 3], cols_y[0][:, 0, f - 1, :])

            for u in range(8):
                copy_tile(u // 4, u % 4, u, first=u < 2)
                if u == 3:
                    split_high(2, 0)
            split_high(3, 1)
            act.wait_ge(rows_ready, 8)
            act.dma_start(vec, attn0[1:2].partition_broadcast(P)).then_inc(vec_in, 16)
            head(0, 0, 2, None, True, False)
            with act.Fori(0, 3) as i:
                for odd in range(2):
                    h = i * 2 + (1 + odd)
                    head(h, 1 - odd, h * 4, h * 4 + 2, True, True)
            head(7, 1, None, 28, False, True)
            split_high(32, 0)
            split_high(33, 1)

            copy_rows(41, 2)
            copy_rows(43, 4)
            copy_v(44)
            for s in range(NB + 1):
                if s < NB:
                    exponential(80 + s, s % 2, ks[:, 0, 1, s:s + 1])
                if s >= 1:
                    high(80 + s - 1, y_tiles[(s - 1) % 2], prob[:, 0, s - 1, :])

            def norm(layer, residual):
                if layer > 1:
                    act.wait_ge(kept_out, 16 * layer)
                act.dma_start(resid, residual).then_inc(res_in, 16)
                act.wait_ge(var_ready, layer + 1)
                nc.scalar.activation(sd[:, 0], stat[:, :, 1], ACT.Sqrt).then_inc(sd_ready, 1)
                act.wait_ge(acc_ready, NORM_AT[layer])
                if layer < 3:
                    act.dma_start(kept, acc[:]).then_inc(kept_out, 16)

            act.wait_ge(x_lo, 84)
            act.dma_start(b_row, bias_rows[0:1].partition_broadcast(P)).then_inc(b_in, 16)
            norm(0, x)
            turn(KB)
            act.wait_ge(kept_out, 16)

            act.dma_start(acc[:], attn1[0:1].partition_broadcast(P)).then_inc(vec_in, 16)
            act.dma_start(vec4, attn1[1:2].partition_broadcast(P)).then_inc(vec_in, 16)
            act.dma_start(mask[:], masks[1]).then_inc(mask_in, 16)
            for r in range(REL3):
                for u in range(8):
                    n, m = u // 4, u % 4
                    copy_tile(32 + 2 * r + n, m, 64 + 8 * r + u)
                    if m == 3:
                        split_high(34 + 2 * r + n, n)
                    if r and u % 2 == 0:
                        copy_rows(45 + 8 * (r - 1) + u + 1, 2)
                if r:
                    act.wait_ge(max_done, 9 + 4 * r)
                    act.dma_start(mask[:], masks[1 + r]).then_inc(mask_in, 16)
            act.wait_ge(rows_ready, 88)
            for r in range(REL3):
                act.dma_start(count16[r], counts[SLOT3 + r]).then_inc(cnt_in, 16)
            for h in range(HEADS1):
                copy_rows(61 + 2 * h + 1, 2)
            copy_rows(70, 4)
            copy_v(71)
            for h in range(HEADS1):
                w0 = 84 + 14 * h
                for s in range(REL3 * NB + 1):
                    g = 3 * h + s // 4
                    if s < REL3 * NB:
                        exponential(w0 + s, s % 2, ks1[:, 1, s // 4, h, s % 4:s % 4 + 1])
                    if s >= 1:
                        tile = 12 * h + s - 1
                        if tile >= NB:
                            act.wait_ge(p_used, tile - NB + 1)
                        high(w0 + s - 1, y_tiles[(s - 1) % 2], prob[:, 0, (s - 1) % 4, :])
                    if s < 12 and g < 11:
                        if s % 4 == 1:
                            copy_rows(72 + 2 * g, 4)
                        elif s % 4 == 3:
                            copy_v(73 + 2 * g)
                for c in range(3):
                    if c < 2:
                        f, part = PIECES[2 * h + c]
                        elu_exponential(w0 + 12 + c, c, y_tiles[c], b_cols[part, HEADS0 * KB + f:HEADS0 * KB + f + 1], part)
                    if c >= 1:
                        f, part = PIECES[2 * h + c - 1]
                        high(w0 + 12 + c - 1, y_tiles[c - 1], cols_x[part, 0, f, :], part)

            act.dma_start(acc[:, 0:2], attn2.partition_broadcast(P)).then_inc(vec_in, 16)
            act.dma_start(mask[:], masks[1]).then_inc(mask_in, 16)
            for r in range(REL3):
                for u in range(8):
                    n, m = u // 4, u % 4
                    copy_tile(38 + 2 * r + n, m, 88 + 8 * r + u)
                    if m == 3:
                        split_high(40 + 2 * r + n, n)
                    if r and u == 0:
                        copy_rows(93 + 2 * r - 1, 2)
                    if r and u == 7:
                        act.wait_ge(max_done, 21 + r)
                        act.dma_start(mask[:], masks[1 + r]).then_inc(mask_in, 16)
            copy_rows(98, 2)
            for r in range(REL3):
                copy_rows((100, 102, 105)[r], 4)
                copy_v((101, 103, 106)[r])
                if r == 2:
                    act.wait_ge(row_done, 16)
                for s in range(NB + 1):
                    if s < NB:
                        exponential(140 + 4 * r + s, s % 2, ks1[:, 1, r, 0, s:s + 1])
                    if s >= 1:
                        high(140 + 4 * r + s - 1, y_tiles[(s - 1) % 2], prob_sets[r % 2][:, 0, s - 1, :])
            act.wait_ge(x_lo, 152)
            act.dma_start(b_row, bias_rows[1:2].partition_broadcast(P)).then_inc(b_in, 16)
            norm(1, kept)
            turn(2 * KB)

            def count_high(number, after):
                act.wait_ge(cnt_in, 16 * (4 + number))
                if number > 1:
                    act.wait_ge(edge_done, KB * (number - 1))
                copy(prob[:, 0], count16[0]).then_inc(cnt_hi, 1)
                if after is not None:
                    act.wait_ge(cnt_lo, number)
                    act.dma_start(count16[0], after).then_inc(cnt_in, 16)

            def edge_high(number, dst):
                for f in range(KB):
                    t = number * KB + f
                    act.wait_ge(y_done, t + 1)
                    copy(dst[:, 0, f, :], xt[:, f % 2]).then_inc(y_hi, 1)

            act.dma_start(count16[0], counts[0]).then_inc(cnt_in, 16)
            for layer in range(3):
                j = 44 + 10 * layer
                act.wait_ge(b_used, 2 + layer)
                act.dma_start(b_row, bias_rows[2 + layer:3 + layer].partition_broadcast(P)).then_inc(b_in, 16)
                count_high(4 * layer + 1, counts[1])
                for r in range(REL4):
                    edge_high(4 * layer + r, cols_y[r % 2])
                    if r + 1 < REL4:
                        count_high(4 * layer + r + 2, None if layer == 2 and r == 2 else counts[(r + 2) % REL4])
                    for n in range(2):
                        split_high(j + 2 * r + n + 2, n)
                for n in range(2):
                    split_high(j + 10 + n, n)
                if layer < 2:
                    act.wait_ge(acc_ready, 3 + layer)
                    turn(KB * (3 + layer))
            norm(2, kept)
            act.dma_start(count16[0], counts[TOTAL]).then_inc(cnt_in, 16)
            act.wait_ge(diag_added, 1)
            act.wait_ge(edge_done, KB * 12)
            copy(prob[:, 0], count16[0]).then_inc(cnt_hi, 1)
            act.wait_ge(misc_done, 113)
            nc.scalar.activation(scale_bc[:, 0], ps[:, 6, :], ACT.Sqrt)
            nc.scalar.activation(zc[:, 0], ps[:, 7, 0:2 * NB:2], ACT.Sqrt).then_inc(sd_ready, 1)
            for layer in range(2):
                act.wait_ge(b_used, 5 + layer)
                act.dma_start(b_row, bias_rows[5 + layer:6 + layer].partition_broadcast(P)).then_inc(b_in, 16)
                edge_high(12 + layer, cols_y[0])
                if layer == 0:
                    for n in range(2):
                        split_high(76 + n, n)
            act.wait_ge(y_lo, KB * 14)
            norm(3, kept)
            act.dma_start(out, acc[:]).then_inc(out_done, 16)
            act.wait_ge(out_done, 16)

        @block.vector
        def _(dve):
            base, local = [0], [0]

            def mark(ins):
                local[0] += 1
                ins.then_inc(step, 1)

            def wait_steps():
                dve.wait_ge(step, base[0] + local[0])

            def wait_all_but_one():
                dve.wait_ge(step, base[0] + (local[0] - 1))

            def sub(dst, a, b):
                return nc.vector.tensor_tensor(dst, a, b, ALU.subtract)

            def add(dst, a, b):
                return nc.vector.tensor_tensor(dst, a, b, ALU.add)

            def copy(dst, src):
                return nc.vector.tensor_copy(dst, src)

            def dot(scratch, a, b, start, total):
                return nc.vector.tensor_tensor_reduce(out=scratch, in0=a, in1=b, scale=1.0, scalar=start,
                                                      op0=ALU.mult, op1=ALU.add, accum_out=total)

            def f32(ap):
                return ap.bitcast(F32)

            def turn(count):
                for f in range(KB):
                    dve.wait_ge(turn_hi, count + f + 1)
                    sub(cols_x[:, 1, f, :], ps[:, 4 + f % 2, :], f32(cols_x[:, 0, f, :])).then_inc(turn_lo, 1)

            def split_tile(q, m, n, dst, dots):
                dve.wait_ge(tile_copied, q + 1)
                tile = hv[:, m % 2]
                part = slice(n * HW, (n + 1) * HW)
                mark(copy(dst[:, 0, m, part], tile))
                for v, (vector, total) in enumerate(dots):
                    if v >= 2:
                        wait_all_but_one()
                    if n == 0:
                        mark(dot(yt[:, v % 2, 0:HW], tile, vector[:, part], 0.0, al_part[:, v, m:m + 1]))
                    else:
                        mark(dot(yt[:, v % 2, 0:HW], tile, vector[:, part], al_part[:, v, m:m + 1], total[:, m:m + 1]))
                wait_steps()
                sub(dst[:, 1, m, part], tile, f32(dst[:, 0, m, part])).then_inc(rows_ready, 1)

            def source_columns(term, scaled):
                mark(nc.vector.tensor_copy(kc[:, :, 0].bitcast(F32R), term))
                if scaled is not None:
                    nc.vector.tensor_scalar(scaled[0], term, 1.0 - SLOPE, None, ALU.mult)
                    nc.vector.tensor_scalar(scaled[1], term, SLOPE, None, ALU.mult)
                wait_steps()
                sub(kc[:, :, 1], term, kc[:, :, 0]).then_inc(kc_ready, 1)

            def maxima(misc, total, done, tiles=None):
                if tiles is not None:
                    dve.wait_ge(x_lo, tiles)
                dve.wait_ge(misc_done, misc)
                nc.vector.memset(waited[:], 0.0)
                for m in range(NB):
                    ins = nc.vector.tensor_tensor_reduce(out=(xt, yt)[m // 2][:, m % 2], in0=ps[:, 7, :], in1=mask[:, m, :], scale=1.0,
                                                         scalar=-3.0e38, op0=ALU.add, op1=ALU.max, accum_out=total[:, m:m + 1])
                ins.then_inc(max_done, 1)
                dve.wait_ge(max_done, done)

            def leaky(z):
                wait_steps()
                mark(nc.vector.scalar_tensor_tensor(z, z, SLOPE, z, ALU.mult, ALU.max))
                wait_steps()

            def u_and_v(target, largest, u, v, parts):
                mark(sub(u, target, largest))
                mark(nc.vector.scalar_tensor_tensor(v, target, SLOPE, largest, ALU.mult, ALU.subtract))
                wait_steps()
                mark(nc.vector.tensor_copy(parts[0].bitcast(F32R), u))
                mark(nc.vector.tensor_copy(parts[2].bitcast(F32R), v))
                wait_steps()
                mark(sub(parts[1], u, parts[0]))
                return sub(parts[3], v, parts[2])

            def exponent(w, slot, source, first=False):
                if not first:
                    dve.wait_ge(x_mid, w - 1)
                nc.vector.scalar_tensor_tensor(xt[:, slot], ps[:, 7, :], source, v_bc[:], ALU.add, ALU.max).then_inc(x_pre, 1)

            def weigh(w, slot, count, first=False):
                dve.wait_ge(x_exp, w + 1)
                if not first:
                    dve.wait_ge(x_lo, w - 1)
                nc.vector.scalar_tensor_tensor(yt[:, slot], xt[:, slot], 1.0, count, ALU.min, ALU.mult).then_inc(x_mid, 1)

            def low(w, y, dst, high, part=slice(0, P)):
                dve.wait_ge(x_hi, w + 1)
                sub(dst, y[part], f32(high)).then_inc(x_lo, 1)

            def elu_start(w, read, slot, y, bank, bias, before, part=slice(0, P)):
                dve.wait_ge(x_lo, before)
                nc.vector.tensor_tensor(y[part], bank[part], r_den[part], ALU.mult).then_inc(agg_read, 1)
                dve.wait_ge(agg_read, read + 1)
                nc.vector.tensor_scalar(xt[part, slot], y[part], bias, 0.0, ALU.add, ALU.min).then_inc(x_pre, 1)

            def elu_end(w, slot, y, part=slice(0, P)):
                dve.wait_ge(x_exp, w + 1)
                nc.vector.scalar_tensor_tensor(y[part], xt[part, slot], -1.0, y[part],
                                               ALU.add, ALU.max).then_inc(x_mid, 1)

            def denominators(bank):
                mark(nc.vector.tensor_scalar(r_den[:], bank, EPS_SOFTMAX, None, ALU.add))
                wait_steps()
                nc.vector.reciprocal(r_den[:], r_den[:]).then_inc(rd_done, 1)

            dve.wait_ge(consts, 3)
            nc.vector.memset(pick_f, 0.0).then_inc(consts, 1)
            dve.wait_ge(consts, 4)
            mark(nc.vector.memset(pick_f[0:2, 0, :], 1.0))
            wait_steps()
            mark(nc.vector.tensor_scalar(pick_f[:, 1, :], pick_f[:, 0, :], -1.0, 1.0, ALU.mult, ALU.add))
            wait_steps()
            mark(copy(ones[:], ones_f))
            copy(pick[:], pick_f).then_inc(consts, 1)
            turn(0)
            nc.vector.memset(acc[:], 0.0).then_inc(acc_added, 8)
            dve.wait_ge(small_in, 32)
            dve.wait_ge(mask_in, 16)
            dve.wait_ge(cnt_in, 16)

            def rows_tile(x_head, parity, u):
                split_tile(x_head * 8 + u, u % 4, u // 4, rows[parity],
                           [(vec[:, v], al[:, parity, v]) for v in range(2)])

            def product_tile(j, u, into_first=False):
                n, m = u // 4, u % 4
                part = slice(n * HW, (n + 1) * HW)
                dve.wait_ge(prod_done, j * 4 + (u + 1))
                if into_first:
                    copy(acc[:, m, part], ps[:, m, 0:HW]).then_inc(acc_added, 1)
                else:
                    add(acc[:, m, part], acc[:, m, part], ps[:, m, 0:HW]).then_inc(acc_added, 1)

            def prob_slot(h, parity, s, with_last=True):
                if s < NB:
                    exponent(h * 10 + s, s % 2, ks[:, parity, 0, s:s + 1], first=not with_last and s < 2)
                if 1 <= s <= NB:
                    weigh(h * 10 + (s - 1), (s - 1) % 2, count16[0][:, s - 1, :], first=not with_last and s <= 2)
                if s >= 2:
                    low(h * 10 + (s - 2), y_tiles[s % 2], prob[:, 1, s - 2, :], prob[:, 0, s - 2, :])

            def small_uv(h, parity, first=False):
                target = al[:, parity, 1]
                maxima(h * 5 + 2, mx, h + 1, None if first else h * 10)
                mark(add(mx[:], mx[:], target))
                leaky(mx[:])
                u_and_v(target, mx[:], uv[:, 0], uv[:, 1], [uvc[:, 0, 0, :, i] for i in range(4)]).then_inc(uv_ready, 1)

            def head(h, parity, j_rows, j_out, with_next, with_last):
                if with_next:
                    dve.wait_ge(vec_in, h * 16 + 32)
                    if with_last:
                        dve.wait_ge(x_lo, h * 10)
                    for u in range(8):
                        rows_tile(h + 1, 1 - parity, u)
                        if u == 2:
                            small_uv(h, parity, first=not with_last)
                    source_columns(al[:, 1 - parity, 0], (ks[:, 1 - parity, 0], ks[:, 1 - parity, 1]))
                else:
                    small_uv(h, parity)
                dve.wait_ge(misc_done, h * 5 + 4)
                dve.wait_ge(vb_ready, h + 1)
                for u in range(8):
                    if with_last:
                        product_tile(j_out, u)
                    if u < NB + 2:
                        prob_slot(h, parity, u, with_last)
                dve.wait_ge(misc_done, h * 5 + 5)
                denominators(ps[:, 6, :])
                dve.wait_ge(rd_done, h + 1)
                for s in range(KB + 2):
                    if s < KB:
                        dve.wait_ge(agg_done, h * 6 + (s + 1))
                        elu_start(h * 10 + (4 + s), h * 6 + s, s % 2, y_tiles[s % 3], ps[:, 4 + s % 2, :],
                                  b_cols[:, bass.ds(h * KB + s, 1)], h * 10 + (4 + max(s - 2, 0)))
                    if 1 <= s <= KB:
                        elu_end(h * 10 + (4 + s - 1), (s - 1) % 2, y_tiles[(s - 1) % 3])
                    if s >= 2:
                        low(h * 10 + (4 + s - 2), y_tiles[(s - 2) % 3], cols_y[0][:, 1, s - 2, :], cols_y[0][:, 0, s - 2, :])

            dve.wait_ge(vec_in, 16)
            for u in range(8):
                rows_tile(0, 0, u)
            source_columns(al[:, 0, 0], (ks[:, 0, 0], ks[:, 0, 1]))
            head(0, 0, 2, None, True, False)
            base[0], local[0] = local[0], 0
            first_steps = base[0]
            with dve.Fori(0, 3) as i:
                for odd in range(2):
                    base[0], local[0] = i * (2 * HEAD_STEPS) + (first_steps + odd * HEAD_STEPS), 0
                    h = i * 2 + (1 + odd)
                    head(h, 1 - odd, h * 4, h * 4 + 2, True, True)
                    assert local[0] == HEAD_STEPS, local
            base[0], local[0] = first_steps + 6 * HEAD_STEPS, 0
            head(7, 1, None, 28, False, True)
            for u in range(8):
                product_tile(30, u)

            def split_rows(last_added=None):
                for m in range(NB):
                    mark(copy(rows[0][:, 0, m, :], acc[:, m, :]))
                wait_steps()
                for m in range(NB):
                    sub(rows[0][:, 1, m, :], acc[:, m, :], f32(rows[0][:, 0, m, :])).then_inc(rows_split, 1)

            dve.wait_ge(acc_added, 72)
            dve.wait_ge(vec_in, 144)
            split_rows()
            for m in range(NB):
                for v in range(2):
                    mark(dot(xt_row, acc[:, m, :], vec[:, v], 0.0, al[:, 0, v, m:m + 1]))
                    wait_steps()
            source_columns(al[:, 0, 0], (ks[:, 0, 0], ks[:, 0, 1]))
            small_uv(8, 0)
            dve.wait_ge(misc_done, 44)
            dve.wait_ge(vb_ready, 9)
            for s in range(NB + 2):
                prob_slot(8, 0, s)

            def read_denominators(misc, first):
                dve.wait_ge(misc_done, misc)
                bank = ps[:, 5, 0:2 * NB:2]
                if first:
                    copy(zc[:, 0], bank).then_inc(den_read, 1)
                else:
                    add(zc[:, 0], zc[:, 0], bank).then_inc(den_read, 1)

            def read_rows(done, first):
                for u in range(8):
                    n, m = u // 4, u % 4
                    part = slice(n * HW, (n + 1) * HW)
                    dve.wait_ge(row_done, done + u + 1)
                    if first:
                        copy(acc[:, m, part], ps[:, m, 0:HW]).then_inc(row_read, 1)
                    else:
                        add(acc[:, m, part], acc[:, m, part], ps[:, m, 0:HW]).then_inc(row_read, 1)

            def norm(layer, reads):
                dve.wait_ge(res_in, 16 * (2 + layer))
                dve.wait_ge(b_in, 16 * B_ROW_AT[layer])
                if layer < 2:
                    dve.wait_ge(row_read, reads)
                    dve.wait_ge(den_read, 1 + 3 * layer)
                    mark(nc.vector.tensor_scalar(zc[:, 0], zc[:, 0], EPS_SOFTMAX, None, ALU.add))
                    wait_steps()
                    mark(nc.vector.reciprocal(zc[:, 1], zc[:, 0]))
                    wait_steps()
                else:
                    dve.wait_ge(acc_added, reads)
                for m in range(NB):
                    if layer < 2:
                        mark(nc.vector.scalar_tensor_tensor(acc[:, m, :], acc[:, m, :], zc[:, 1, m:m + 1], resid[:, m, :],
                                                            ALU.mult, ALU.add))
                    else:
                        mark(add(acc[:, m, :], acc[:, m, :], resid[:, m, :]))
                wait_steps()
                for m in range(NB):
                    ins = add(acc[:, m, :], acc[:, m, :], b_row)
                    ins.then_inc(b_used, 1) if m == NB - 1 else mark(ins)
                dve.wait_ge(b_used, B_ROW_AT[layer])
                for m in range(NB):
                    for n in range(2):
                        ins = nc.vector.bn_stats(bn[:, m, n], acc[:, m, n * HW:(n + 1) * HW])
                mark(ins)
                wait_steps()
                for m in range(NB):
                    ins = nc.vector.bn_aggr(stat[:, m, :], bn[:, m].rearrange("p n s -> p (n s)"))
                mark(ins)
                wait_steps()
                nc.vector.tensor_scalar(stat[:, :, 1], stat[:, :, 1], EPS_NORM, None, ALU.add).then_inc(var_ready, 1)
                dve.wait_ge(sd_ready, SD_AT[layer])
                mark(nc.vector.reciprocal(sd[:, 1], sd[:, 0]))
                wait_steps()
                for m in range(NB):
                    ins = nc.vector.tensor_scalar(acc[:, m, :], acc[:, m, :], stat[:, m, 0:1], sd[:, 1, m:m + 1],
                                                  ALU.subtract, ALU.mult)
                ins.then_inc(acc_ready, 1)

            read_denominators(45, True)
            read_rows(0, True)
            norm(0, 8)
            turn(KB)

            def relation_uv(heads):
                span = slice(0, heads)
                z, target = mx1[:, :, span], al1[:, 1, :, span]
                mark(add(z, z, target))
                leaky(z)
                mark(nc.vector.tensor_tensor(mx1[:, 0, span], mx1[:, 0, span], mx1[:, 1, span], ALU.max))
                wait_steps()
                mark(nc.vector.tensor_tensor(mx1[:, 0, span], mx1[:, 0, span], mx1[:, 2, span], ALU.max))
                wait_steps()
                for r in range(REL3):
                    ins = u_and_v(target[:, r], mx1[:, 0, span], uv1[:, 0, r, span], uv1[:, 1, r, span],
                                  [uvc[:, r, span, :, i] for i in range(4)])
                    ins.then_inc(uv_ready, 1) if r == REL3 - 1 else mark(ins)

            def scale_sources(r, heads):
                span = slice(0, heads)
                for i, by in enumerate((1.0 - SLOPE, SLOPE)):
                    nc.vector.tensor_scalar(ks1[:, i, r, span], al1[:, 0, r, span], by, None, ALU.mult)

            dve.wait_ge(vec_in, 176)
            dots = [None] * REL3
            for r in range(REL3):
                for u in range(8):
                    if r and u % 2 == 0:
                        if u == 0:
                            dve.wait_ge(mask_in, 16 * (1 + r))
                        source_columns(al1[:, 0, r - 1, u // 2], None)
                    split_tile(64 + 8 * r + u, u % 4, u // 4, rows[r],
                               [((acc if v < 4 else vec4)[:, v % 4], al1[:, v // 4, r, v % 4]) for v in range(8)])
                    if r and u % 2 == 1:
                        maxima(45 + 8 * (r - 1) + u + 1, mx1[:, r - 1, u // 2], 9 + 4 * (r - 1) + u // 2 + 1, 84)
                scale_sources(r, HEADS1)
            dve.wait_ge(mask_in, 64)
            for h in range(HEADS1):
                source_columns(al1[:, 0, 2, h], None)
                maxima(61 + 2 * h + 2, mx1[:, 2, h], 18 + h, 84)
            relation_uv(HEADS1)
            dve.wait_ge(cnt_in, 64)
            for h in range(HEADS1):
                w0 = 84 + 14 * h
                for s in range(REL3 * NB + 2):
                    g = 3 * h + s // 4
                    if s < REL3 * NB:
                        if s % 4 == 0:
                            dve.wait_ge(misc_done, 71 + 2 * g)
                            dve.wait_ge(vb_ready, 10 + g)
                        exponent(w0 + s, s % 2, ks1[:, 0, s // 4, h, s % 4:s % 4 + 1])
                    if 1 <= s <= REL3 * NB:
                        weigh(w0 + s - 1, (s - 1) % 2, count16[(s - 1) // 4][:, (s - 1) % 4, :])
                    if s >= 2:
                        low(w0 + s - 2, y_tiles[s % 2], prob[:, 1, (s - 2) % 4, :], prob[:, 0, (s - 2) % 4, :])
                dve.wait_ge(p_used, 12 * (h + 1))
                denominators(ps[:, 4 + h % 2, :])
                dve.wait_ge(rd_done, 8 + h + 1)
                for c in range(4):
                    if c < 2:
                        f, part = PIECES[2 * h + c]
                        elu_start(w0 + 12 + c, 48 + 2 * h + c, c, y_tiles[c], ps[:, 2 * (h % 2) + c, :],
                                  b_cols[part, HEADS0 * KB + f:HEADS0 * KB + f + 1], w0 + 12, part)
                    if 1 <= c <= 2:
                        f, part = PIECES[2 * h + c - 1]
                        elu_end(w0 + 12 + c - 1, c - 1, y_tiles[c - 1], part)
                    if c >= 2:
                        f, part = PIECES[2 * h + c - 2]
                        low(w0 + 12 + c - 2, y_tiles[c - 2], cols_x[part, 1, f, :], cols_x[part, 0, f, :], part)

            dve.wait_ge(vec_in, 192)
            for r in range(REL3):
                for u in range(8):
                    if r and u == 0:
                        dve.wait_ge(mask_in, 16 * (4 + r))
                        source_columns(al1[:, 0, r - 1, 0], None)
                    split_tile(88 + 8 * r + u, u % 4, u // 4, rows[r], [(acc[:, v], al1[:, v, r, 0]) for v in range(2)])
                    if r and u == 1:
                        maxima(94 + 2 * (r - 1) + 1, mx1[:, r - 1, 0], 21 + r, 140)
                scale_sources(r, 1)
            dve.wait_ge(mask_in, 16 * 7)
            source_columns(al1[:, 0, 2, 0], None)
            maxima(99, mx1[:, 2, 0], 24, 140)
            relation_uv(1)
            for r in range(REL3):
                dve.wait_ge(misc_done, (101, 103, 106)[r])
                dve.wait_ge(vb_ready, 22 + r)
                w0 = 140 + 4 * r
                held = prob_sets[r % 2]
                for s in range(NB + 2):
                    if s < NB:
                        exponent(w0 + s, s % 2, ks1[:, 0, r, 0, s:s + 1])
                    if 1 <= s <= NB:
                        weigh(w0 + s - 1, (s - 1) % 2, count16[r][:, s - 1, :])
                    if s >= 2:
                        low(w0 + s - 2, y_tiles[s % 2], held[:, 1, s - 2, :], held[:, 0, s - 2, :])
                if r:
                    read_denominators((104, 107)[r - 1], r == 1)
                    if r == 2:
                        dve.wait_ge(row_read, 16)
                    read_rows(8 * r, r == 1)
            read_denominators(108, False)
            dve.wait_ge(row_read, 24)
            read_rows(24, False)
            norm(1, 32)
            dve.wait_ge(kept_out, 32)
            split_rows()
            turn(2 * KB)

            def count_low(number, src):
                dve.wait_ge(cnt_hi, number)
                sub(prob[:, 1], src, f32(prob[:, 0])).then_inc(cnt_lo, 1)

            def edge_tiles(number, scale, dst):
                for f in range(KB + 1):
                    t = number * KB + f
                    if f < KB:
                        dve.wait_ge(edge_done, t + 1)
                        if t >= 2:
                            dve.wait_ge(y_lo, t - 1)
                        nc.vector.tensor_tensor(xt[:, f % 2], ps[:, 4 + f % 2, :], scale, ALU.mult).then_inc(y_done, 1)
                    if f >= 1:
                        dve.wait_ge(y_hi, t)
                        sub(dst[:, 1, f - 1, :], xt[:, (f - 1) % 2], f32(dst[:, 0, f - 1, :])).then_inc(y_lo, 1)

            def add_bias(count, relu_too):
                dve.wait_ge(b_in, 16 * count)
                for m in range(NB):
                    ins = add(acc[:, m, :], acc[:, m, :], b_row)
                    ins.then_inc(b_used, 1) if m == NB - 1 else mark(ins)
                dve.wait_ge(b_used, count)
                for m in range(NB):
                    ins = nc.vector.tensor_scalar(acc[:, m, :], acc[:, m, :], 0.0, None, ALU.max)
                ins.then_inc(acc_ready, 1)

            added = 72
            for layer in range(3):
                for r in range(REL4):
                    number = 4 * layer + r
                    if r == 0:
                        count_low(number + 1, count16[0])
                    if layer == 0:
                        dve.wait_ge(misc_done, 108 + r + 1)
                        mark(nc.vector.tensor_scalar(scale_bc[:, r], ps[:, 6, :], 1.0, None, ALU.max))
                        wait_steps()
                        nc.vector.reciprocal(scale_bc[:, r], scale_bc[:, r]).then_inc(scale_ready, 1)
                        dve.wait_ge(scale_ready, r + 1)
                    edge_tiles(number, scale_bc[:, r], cols_y[r % 2])
                    if r + 1 < REL4:
                        count_low(number + 2, count16[0])
                    for u in range(8):
                        if r:
                            dve.wait_ge(acc_added, added)
                        product_tile(44 + 10 * layer + 2 * r, u, into_first=r == 0)
                    added += 8
                dve.wait_ge(acc_added, added)
                for u in range(8):
                    product_tile(52 + 10 * layer, u)
                added += 8
                dve.wait_ge(acc_added, added)
                if layer < 2:
                    add_bias(3 + layer, True)
                    dve.wait_ge(acc_ready, 3 + layer)
                    split_rows()
                    turn(KB * (3 + layer))
            norm(2, added)

            def split_scaled():
                for m in range(NB):
                    mark(nc.vector.tensor_scalar(acc[:, m, :], acc[:, m, :], zc[:, 1, m:m + 1], None, ALU.mult))
                wait_steps()
                split_rows()

            dve.wait_ge(cnt_in, 16 * 17)
            for m in range(NB):
                ins = add(count16[0][:, m, m * P:(m + 1) * P], count16[0][:, m, m * P:(m + 1) * P], ident[:])
            ins.then_inc(diag_added, 1)
            count_low(13, count16[0])
            dve.wait_ge(sd_ready, 4)
            mark(nc.vector.reciprocal(zc[:, 1], zc[:, 0]))
            nc.vector.reciprocal(scale_bc[:, 0], scale_bc[:, 0]).then_inc(scale_ready, 1)
            wait_steps()
            dve.wait_ge(scale_ready, 5)
            dve.wait_ge(kept_out, 48)
            for layer in range(2):
                split_scaled()
                edge_tiles(12 + layer, scale_bc[:, 0], cols_y[0])
                for u in range(8):
                    product_tile(74 + 2 * layer, u, into_first=True)
                added += 8
                dve.wait_ge(acc_added, added)
                if layer == 0:
                    add_bias(6, True)
                    dve.wait_ge(acc_ready, 6)
            norm(3, added)


def kernel(**inputs):
    import concourse.bacc as bacc
    from concourse.bass_utils import run_bass_kernel_spmd

    a = {name: np.ascontiguousarray(value) for name, value in inputs.items()}
    blocks = {}
    first0 = a["L0_gnn_W1"].reshape(D, HEADS0, D)
    second0 = a["L0_gnn_W2"].reshape(HEADS0, D, D)
    order = [first0[:, 0], first0[:, 1]]
    for h in range(HEADS0 - 2):
        order += [first0[:, h + 2], second0[h]]
    order += [second0[6], second0[7], *a["L1_gnn_W1"], *a["L1_gnn_W2"]]
    for i in "123":
        order += [a["L2_gnn_root" + i], *a["L2_gnn_W" + i]]
    order += [a["L3_gnn_W1"], a["L3_gnn_W2"]]
    weights = np.stack(order).reshape(WEIGHT_BLOCKS, 3, 2, P, 2, HW).transpose(0, 4, 1, 3, 2, 5)
    arrays = {
        "edges": np.stack([a["src"], a["dst"], a["edge_type_3"], a["edge_type_4"]]).reshape(4, P, CH).transpose(1, 0, 2),
        "x_rows": a["x"].reshape(NB, P, D).transpose(1, 0, 2),
        "weights": weights.reshape(2 * WEIGHT_BLOCKS, 3, P, 2 * HW),
        "attn0": np.stack([np.concatenate([a["L0_gnn_a_src1"], a["L0_gnn_a_src2"]]),
                           np.concatenate([a["L0_gnn_a_dst1"], a["L0_gnn_a_dst2"]])], 1),
        "attn1": np.stack([a["L1_gnn_k1"].T, a["L1_gnn_q1"].T]),
        "attn2": np.stack([a["L1_gnn_k2"].T, a["L1_gnn_q2"].T], 1),
        "bias_cols": np.concatenate([a["L0_gnn_b1"], a["L1_gnn_b1"]]).reshape(HEADS0 * KB + KB, P).T,
        "bias_rows": np.stack([a[n] for n in ("L0_gnn_b2", "L1_gnn_b2", "L2_gnn_b1", "L2_gnn_b2", "L2_gnn_b3",
                                              "L3_gnn_b1", "L3_gnn_b2")]),
    }
    arrays = {name: np.ascontiguousarray(value) for name, value in arrays.items()}

    nc = bacc.Bacc("TRN2", target_bir_lowering=False, num_devices=1)
    dram = {name: nc.dram_tensor(name, v.shape, mybir.dt.from_np(v.dtype), kind="ExternalInput").ap()
            for name, v in arrays.items()}
    out = nc.dram_tensor("out", [P, NB, D], F32, kind="ExternalOutput").ap()
    counts = nc.dram_tensor("counts", [8, P, NB, N], I16).ap()
    masks = nc.dram_tensor("masks", [4, P, NB, N], BF16).ap()
    flag = nc.dram_tensor("flag", [1, 1], I32).ap()
    kept = nc.dram_tensor("kept", [P, NB, D], F32).ap()
    count_edges(nc, dram["edges"], counts, masks, flag)
    graph_layers(nc, dram["x_rows"], dram["weights"], dram["attn0"], dram["attn1"], dram["attn2"],
                 dram["bias_cols"], dram["bias_rows"], counts, masks, flag, kept, out)
    got = run_bass_kernel_spmd(nc, [arrays], core_ids=[0]).results[0]["out"]
    return got.reshape(P, NB, D).transpose(1, 0, 2).reshape(N, D)
```

```python
from contextlib import ExitStack

import concourse.bass as bass
import numpy as np
from concourse import mybir

F32 = mybir.dt.float32
F32R = mybir.dt.float32r
BF16 = mybir.dt.bfloat16
F16 = mybir.dt.float16
I16 = mybir.dt.int16
I32 = mybir.dt.int32
ALU = mybir.AluOpType
ACT = mybir.ActivationFunctionType

P = 128
N = 512
D = 768
E = 8704
NB = N // P
KB = D // P
HW = D // 2
HEADS0 = 8
HEADS1 = 4
REL3 = 3
REL4 = 4
CH = E // P
NEG = -1.0e30
EPS_SOFTMAX = 1e-16
EPS_NORM = 1e-5
SLOPE = 0.2

GROUPS = [(0, 24), (24, 48), (48, CH)]
PACK = 2.0 ** -12
SHIFT = -0.375
ROUND = 1.5 * 2.0 ** 23
PAIRS = [(1, 0, 1, 0, 1), (1, 2, 3, 2, 3), (0, 0, 1, 4, 5)]
SLOT3 = 4
TOTAL = 7
BIG = 4096.0


def early_loads(nc, ctx):
    early = ctx.enter_context(nc.sbuf_tensor("early", [P, NB * D + 8 * HW], F32))
    raw_in = [ctx.enter_context(nc.semaphore(f"raw_in{p}")) for p in range(3)]
    res_in = ctx.enter_context(nc.semaphore("res_in"))
    return early, raw_in, res_in


def split_early(early):
    acc = early[:, 0:NB * D].rearrange("p (m f) -> p m f", m=NB)
    w_raw = early[:, NB * D:NB * D + 6 * HW].rearrange("p (t a f) -> p t a f", t=3, a=2)
    hv = early[:, NB * D + 6 * HW:NB * D + 8 * HW].rearrange("p (a f) -> p a f", a=2)
    return acc, w_raw, hv


def count_edges(nc, shared, x, weights, edges, counts, masks, flag):
    with ExitStack() as ctx:
        def sb(name, shape, dt):
            return ctx.enter_context(nc.sbuf_tensor(name, shape, dt))

        def sem(name):
            return ctx.enter_context(nc.semaphore(name))

        most_chunks = max(hi - lo for lo, hi in GROUPS)
        edge_i = sb("edge_i", [P, 4, CH], I32)
        edge_f = sb("edge_f", [P, 4, CH], F32)
        first = sb("first", [P, CH], F32)
        weight = sb("weight", [P, len(PAIRS), CH], F32)
        node_i = sb("node_i", [P, N], I32)
        node_f = sb("node_f", [P, N], F16)
        src_hot = sb("src_hot", [P, CH, N], BF16)
        early, raw_in, res_in = shared
        dst_hot = early[:].bitcast(BF16).rearrange("p (c n) -> p c n", n=N)
        assert dst_hot.shape[1] >= most_chunks
        packed = sb("packed", [P, 2, NB, N], F32)
        whole = sb("whole", [P, 2, NB, N], F32)
        sum_a = sb("sum_a", [P, 2, NB, N], F32)
        sum_b = sb("sum_b", [P, 2, NB, N], F32)
        total = sb("total", [P, NB, N], F32)
        rel_c = sb("rel_c", [P, NB, N], F32)
        out16 = sb("out16", [P, 4, NB, N], I16)
        most = sb("most", [P, 1], F32)
        most_row = sb("most_row", [1, 1], F32)
        flag_i = sb("flag_i", [1, 1], I32)
        ident_f = sb("ident_f", [P, P], F32)
        ident_b = sb("ident_b", [P, P], BF16)
        has_edge = src_hot[:, 0:4 * NB]
        mask = src_hot[:, 4 * NB:8 * NB]
        ps = ctx.enter_context(nc.psum_tensor("count_ps", [P, 2, NB, N], F32))

        def turned_tile(t, m):
            return ps[:, (t + 1) % 2, m].bitcast(BF16)[:, 0:N]

        edges_in = sem("edges_in")
        setup = sem("setup")
        iota_done = sem("iota_done")
        ident_done = sem("ident_done")
        hot_ready = sem("hot_ready")
        hot_used = sem("hot_used")
        tile_read = sem("tile_read")
        rounded = sem("rounded")
        summed = sem("summed")
        unpacked = sem("unpacked")
        scaled = sem("scaled")
        total_done = sem("total_done")
        out16_ready = sem("out16_ready")
        pairs_stored = sem("pairs_stored")
        stored = sem("stored")
        last_whole = sem("last_whole")
        last_part = sem("last_part")
        last_b = sem("last_b")
        last_a = sem("last_a")
        c_part = sem("c_part")
        c_ready = sem("c_ready")
        has_ready = sem("has_ready")
        turned = sem("turned")
        mask_act = sem("mask_act")
        mask_dve = sem("mask_dve")
        most_ready = sem("most_ready")
        flag_ready = sem("flag_ready")

        spans = [(CH * pair + lo, CH * pair + hi) for pair in range(len(PAIRS)) for lo, hi in GROUPS]
        per_pair = len(GROUPS)
        last = len(spans) - 1
        block = ctx.enter_context(nc.Block())

        @block.sync
        def _(sp):
            sp.dma_start(edge_i[:], edges).then_inc(edges_in, 16)
            order = [(PAIRS[0][4], 1), (PAIRS[0][3], 0), (PAIRS[1][4], 1), (PAIRS[1][3], 0), (TOTAL, 3),
                     (PAIRS[2][4], 1), (PAIRS[2][3], 0), (SLOT3 + 2, 2)]
            for done, (slot, half) in enumerate(order):
                if done == 5:
                    acc, w_raw, _ = split_early(early)
                    sp.wait_ge(hot_used, spans[last][1])
                    sp.dma_start(acc, x).then_inc(res_in, 16)
                    for p in range(3):
                        sp.dma_start(w_raw[:, p], weights[0, p]).then_inc(raw_in[p], 16)
                sp.wait_ge(out16_ready, done + 1)
                sp.dma_start(counts[slot], out16[:, half]).then_inc(pairs_stored if done < 4 else stored, 16)
            for r, (ready, value) in enumerate(((mask_act, NB), (mask_dve, NB), (mask_act, 2 * NB), (mask_dve, 2 * NB))):
                sp.wait_ge(ready, value)
                sp.dma_start(masks[r], mask[:, r * NB:(r + 1) * NB]).then_inc(stored, 16)
            sp.wait_ge(flag_ready, 1)
            sp.dma_start(flag, flag_i[:]).then_inc(stored, 16)
            sp.wait_ge(pairs_stored, 16 * 4)
            sp.wait_ge(stored, 16 * (len(order) - 4 + 5))

        @block.gpsimd
        def _(pool):
            nc.gpsimd.iota(node_i[:], pattern=[[1, N]], base=0, channel_multiplier=0).then_inc(iota_done, 1)
            nc.gpsimd.memset(ident_f[:], 0.0).then_inc(summed, 1)
            pool.wait_ge(summed, 1)
            nc.gpsimd.affine_select(out=ident_f[:], in_=ident_f[:], compare_op=ALU.not_equal, fill=1.0, base=0,
                                    pattern=[[-1, P]], channel_multiplier=1).then_inc(ident_done, 1)
            steps = 1
            for group in range(last):
                pair, g = divmod(group, per_pair)
                slot = group % 2
                pool.wait_ge(rounded, group + 1)
                if g == 0:
                    if pair == 2:
                        pool.wait_ge(total_done, 1)
                    nc.gpsimd.tensor_tensor(sum_a[:, pair % 2], packed[:, slot], sum_b[:, pair % 2],
                                            ALU.subtract).then_inc(unpacked, 1)
                else:
                    nc.gpsimd.tensor_tensor(packed[:, slot], packed[:, slot], whole[:, slot], ALU.subtract).then_inc(summed, 1)
                    pool.wait_ge(unpacked, group)
                    nc.gpsimd.tensor_tensor(sum_b[:, pair % 2], sum_b[:, pair % 2], whole[:, slot], ALU.add).then_inc(summed, 1)
                    steps += 2
                    pool.wait_ge(summed, steps)
                    nc.gpsimd.tensor_tensor(sum_a[:, pair % 2], sum_a[:, pair % 2], packed[:, slot],
                                            ALU.add).then_inc(unpacked, 1)
                if g == per_pair - 1:
                    pool.wait_ge(scaled, pair + 1)
                    if pair == 0:
                        nc.gpsimd.tensor_tensor(total[:], sum_a[:, 0], sum_b[:, 0], ALU.add).then_inc(total_done, 1)
                    else:
                        pool.wait_ge(total_done, 1)
                        nc.gpsimd.tensor_tensor(total[:], total[:], sum_a[:, 1], ALU.add).then_inc(summed, 1)
                        steps += 1
                        pool.wait_ge(summed, steps)
                        nc.gpsimd.tensor_tensor(total[:], total[:], sum_b[:, 1], ALU.add).then_inc(total_done, 1)
            pool.wait_ge(total_done, 2)
            for m in range(NB):
                pool.wait_ge(last_b, m + 1)
                nc.gpsimd.tensor_tensor(rel_c[:, m], total[:, m], sum_b[:, 0, m], ALU.subtract).then_inc(c_part, 1)
            for m in range(NB):
                pool.wait_ge(c_part, m + 1)
                pool.wait_ge(scaled, 2 + m + 1)
                nc.gpsimd.tensor_tensor(rel_c[:, m], rel_c[:, m], sum_a[:, 0, m], ALU.subtract).then_inc(c_ready, 1)

        @block.scalar
        def _(act):
            def copy(dst, src, bias=0.0, scale=1.0):
                return nc.scalar.activation(dst, src, ACT.Copy, bias=bias, scale=scale)

            to_count = dict(scale=1.0 / PACK, bias=-SHIFT * per_pair / PACK)
            for group, (_, end) in enumerate(spans):
                act.wait_ge(hot_used, end)
                if group >= 2:
                    act.wait_ge(unpacked, group - 1)
                for m in range(NB):
                    copy(packed[:, group % 2, m], ps[:, group % 2, m], bias=SHIFT).then_inc(tile_read, 1)
                pair = group // per_pair - 1
                if pair >= 0 and group % per_pair == 0:
                    act.wait_ge(unpacked, group)
                    copy(sum_a[:, pair], sum_a[:, pair], **to_count).then_inc(scaled, 1)
                    if pair:
                        act.wait_ge(pairs_stored, 32)
                    copy(out16[:, 1], sum_b[:, pair]).then_inc(out16_ready, 1)
                    act.wait_ge(scaled, pair + 1)
                    copy(out16[:, 0], sum_a[:, pair]).then_inc(out16_ready, 1)
                if group == last - 1:
                    act.wait_ge(total_done, 2)
                    copy(out16[:, 3], total[:]).then_inc(out16_ready, 1)
            for m in range(NB):
                act.wait_ge(turned, m + 1)
                copy(mask[:, m], turned_tile(0, m), scale=-NEG, bias=NEG).then_inc(mask_act, 1)
            act.wait_ge(pairs_stored, 64)
            for m in range(NB):
                act.wait_ge(last_a, m + 1)
                copy(sum_a[:, 0, m], sum_a[:, 0, m], **to_count).then_inc(scaled, 1)
            act.wait_ge(last_b, NB)
            copy(out16[:, 1], sum_b[:, 0]).then_inc(out16_ready, 1)
            act.wait_ge(scaled, 2 + NB)
            copy(out16[:, 0], sum_a[:, 0]).then_inc(out16_ready, 1)
            for m in range(NB):
                act.wait_ge(turned, NB + m + 1)
                copy(mask[:, 2 * NB + m], turned_tile(1, m), scale=-NEG, bias=NEG).then_inc(mask_act, 1)
            act.wait_ge(c_ready, NB)
            copy(out16[:, 2], rel_c[:]).then_inc(out16_ready, 1)

        @block.vector
        def _(dve):
            n = [0]

            def step(ins):
                n[0] += 1
                ins.then_inc(setup, 1)
                dve.wait_ge(setup, n[0])

            dve.wait_ge(ident_done, 1)
            nc.vector.tensor_copy(ident_b[:], ident_f[:]).then_inc(ident_done, 1)
            dve.wait_ge(iota_done, 1)
            step(nc.vector.tensor_copy(node_f[:], node_i[:]))
            dve.wait_ge(edges_in, 16)
            step(nc.vector.tensor_copy(edge_f[:], edge_i[:]))
            for pair, (kinds, type_a, type_b, _, _) in enumerate(PAIRS):
                kind = edge_f[:, 2 + kinds, :]
                step(nc.vector.tensor_scalar(first[:], kind, float(type_a), PACK, ALU.is_equal, ALU.mult))
                step(nc.vector.scalar_tensor_tensor(weight[:, pair, :], kind, float(type_b), first[:],
                                                    ALU.is_equal, ALU.add))

            def one_hot(pair, c, slot):
                if pair == 0:
                    nc.vector.tensor_scalar(src_hot[:, bass.ds(c, 1)], node_f[:], edge_f[:, 0, bass.ds(c, 1)], None, ALU.is_equal)
                nc.vector.tensor_scalar(dst_hot[:, bass.ds(slot, 1)], node_f[:], edge_f[:, 1, bass.ds(c, 1)],
                                        weight[:, pair, bass.ds(c, 1)], ALU.is_equal, ALU.mult).then_inc(hot_ready, 1)

            def round_group(group):
                pair, g = divmod(group, per_pair)
                dve.wait_ge(tile_read, NB * (group + 1))
                if g == 0 and pair == 2:
                    dve.wait_ge(total_done, 1)
                    dve.wait_ge(out16_ready, 2)
                nc.vector.tensor_scalar(sum_b[:, pair % 2] if g == 0 else whole[:, group % 2], packed[:, group % 2],
                                        ROUND, -ROUND, ALU.add, ALU.add).then_inc(rounded, 1)

            for group, (begin, end) in enumerate(spans):
                pair = group // per_pair
                lo = begin - CH * pair
                with dve.Fori(0, (end - begin) // 2) as i:
                    for half in range(2):
                        if group:
                            dve.wait_ge(hot_used, i * 2 + (spans[group - 1][0] + half + 1))
                        one_hot(pair, i * 2 + (lo + half), i * 2 + half)
                if group:
                    round_group(group - 1)
            dve.wait_ge(hot_used, spans[last][0])
            dve.wait_ge(total_done, 2)
            for m in range(NB):
                nc.vector.tensor_scalar(has_edge[:, m], total[:, m], 1.0, None, ALU.min).then_inc(has_ready, 1)
            nc.vector.tensor_reduce(most[:], total[:], mybir.AxisListType.XY, ALU.max).then_inc(most_ready, 1)
            slot = last % 2
            for m in range(NB):
                dve.wait_ge(tile_read, NB * last + m + 1)
                nc.vector.tensor_scalar(whole[:, slot, m], packed[:, slot, m], ROUND, -ROUND, ALU.add, ALU.add).then_inc(last_whole, 1)
            dve.wait_ge(unpacked, last)
            for m in range(NB):
                dve.wait_ge(last_whole, m + 1)
                nc.vector.tensor_tensor(packed[:, slot, m], packed[:, slot, m], whole[:, slot, m], ALU.subtract).then_inc(last_part, 1)
            for m in range(NB):
                dve.wait_ge(last_part, m + 1)
                nc.vector.tensor_tensor(sum_a[:, 0, m], sum_a[:, 0, m], packed[:, slot, m], ALU.add).then_inc(last_a, 1)
            for m in range(NB):
                nc.vector.tensor_tensor(sum_b[:, 0, m], sum_b[:, 0, m], whole[:, slot, m], ALU.add).then_inc(last_b, 1)
            for m in range(NB):
                dve.wait_ge(last_b, m + 1)
                nc.vector.tensor_scalar(has_edge[:, NB + m], sum_b[:, 0, m], 1.0, None, ALU.min).then_inc(has_ready, 1)
            for m in range(NB):
                dve.wait_ge(scaled, 2 + m + 1)
                nc.vector.tensor_scalar(has_edge[:, 2 * NB + m], sum_a[:, 0, m], 1.0, None, ALU.min).then_inc(has_ready, 1)
            for m in range(NB):
                dve.wait_ge(c_ready, m + 1)
                nc.vector.tensor_scalar(has_edge[:, 3 * NB + m], rel_c[:, m], 1.0, None, ALU.min).then_inc(has_ready, 1)
            for t, row in ((2, 1), (3, 3)):
                for m in range(NB):
                    dve.wait_ge(turned, NB * t + m + 1)
                    nc.vector.tensor_scalar(mask[:, NB * row + m], turned_tile(t, m), 1.0, -NEG,
                                            ALU.subtract, ALU.mult).then_inc(mask_dve, 1)
            dve.wait_ge(turned, 4 * NB + 1)
            step(nc.vector.tensor_reduce(most_row[:], ps[0:1, 1, 0, 0:P], mybir.AxisListType.X, ALU.max))
            nc.vector.tensor_scalar(flag_i[:], most_row[:], BIG, None, ALU.is_ge).then_inc(flag_ready, 1)

        @block.tensor
        def _(pe):
            for group, (begin, end) in enumerate(spans):
                bank = group % 2
                lo = begin % CH
                if group >= 2:
                    pe.wait_ge(tile_read, NB * (group - 1))

                def chunk(index, start, stop):
                    pe.wait_ge(hot_ready, index + (begin + 1))
                    for m in range(NB):
                        mm = nc.tensor.matmul(ps[:, bank, m], src_hot[:, bass.ds(index + lo, 1), m * P:(m + 1) * P],
                                              dst_hot[:, bass.ds(index, 1)], start=start, stop=stop, skip_group_check=True)
                    mm.then_inc(hot_used, 1)

                chunk(0, True, False)
                with pe.Fori(0, (end - begin - 2) // 2) as i:
                    chunk(i * 2 + 1, False, False)
                    chunk(i * 2 + 2, False, False)
                chunk(end - begin - 1, False, True)
            pe.wait_ge(ident_done, 2)
            for t in range(4):
                for m in range(NB):
                    if t == 0:
                        pe.wait_ge(tile_read, NB * last)
                    elif t == 1:
                        pe.wait_ge(tile_read, NB * (last + 1))
                    else:
                        pe.wait_ge(mask_act, NB * (t - 2) + m + 1)
                    pe.wait_ge(has_ready, NB * (t + 1))
                    for s in range(NB):
                        mm = nc.tensor.transpose(turned_tile(t, m)[:, s * P:(s + 1) * P],
                                                 has_edge[:, NB * t + s, m * P:(m + 1) * P], ident_b[:])
                    mm.then_inc(turned, 1)
            pe.wait_ge(most_ready, 1)
            pe.wait_ge(mask_dve, 1)
            nc.tensor.transpose(ps[0:1, 1, 0, 0:P], most[:], ident_f[:]).then_inc(turned, 1)


WEIGHT_BLOCKS = 2 * HEADS0 + 2 * REL3 + 3 * (REL4 + 1) + 2
B_ROW_AT = (1, 2, 5, 7)
SD_AT = (1, 2, 4, 5)
HEAD_STEPS = 17
W_AT = 84
PIECES = [(0, slice(0, P)), (1, slice(0, 64)), (1, slice(64, P)), (2, slice(0, P)),
          (3, slice(0, P)), (4, slice(0, 64)), (4, slice(64, P)), (5, slice(0, P))]


def tile_at(h, s):
    return W_AT + 12 * h + s + 2 * max(h - 1, 0) + (2 if h and s > 5 else 0)


def result_at(h, c):
    return (tile_at(h + 1, 5) if h + 1 < HEADS1 else tile_at(h, 11)) + 1 + c


def relational_items():
    items = []
    for h in range(HEADS1):
        for s in range(REL3 * NB):
            items.append((h, s, None))
            if h and s == 5:
                items += [(h - 1, None, 0), (h - 1, None, 1)]
    return items + [(HEADS1 - 1, None, 0), (HEADS1 - 1, None, 1)]


def graph_layers(nc, shared, x, weights, attn0, attn1, attn2, bias_cols, bias_rows, counts, masks, flag, kept, out):
    PASSES = 2 * WEIGHT_BLOCKS
    with ExitStack() as ctx:
        def sb(name, shape, dt):
            return ctx.enter_context(nc.sbuf_tensor(name, shape, dt))

        def sem(name):
            return ctx.enter_context(nc.semaphore(name))

        cols_x = sb("cols_x", [P, 2, KB, N], F32R)
        wide = [sb(f"wide{i}", [P, 2, KB * N], F32R) for i in range(3)]
        prob = sb("prob", [P, 2, NB, N], F32R)
        w_pair = sb("w_pair", [P, 2, 2, KB, HW], F32R)
        early, raw_in, res_in = shared
        acc, w_raw, hv = split_early(early)
        multi = sb("multi", [P, NB * D], F32)
        mask = sb("edge_mask", [P, NB, N], BF16)
        xt = sb("xt", [P, 2, N], F32)
        yt = sb("yt", [P, 2, N], F32)
        v_bc = sb("v_bc", [P, N], F32)
        r_den = sb("r_den", [P, N], F32)
        q_rows = sb("q_rows", [4, N], F32R)
        ident = sb("ident", [P, P], F32)
        ones = sb("ones", [P, P], F32R)
        pick = sb("pick", [4, 2, P], F32R)
        b_cols = sb("b_cols", [P, HEADS0 * KB + KB], F32)
        al_part = sb("al_part", [P, 8, NB], F32)
        al = sb("al", [P, 2, 2, NB], F32)
        al_half = sb("al_half", [P, 2, REL3, 2, NB], F32)
        al1 = sb("al1", [P, 2, REL3, HEADS1, NB], F32)
        kc = sb("kc", [P, HEADS1, NB, 2], F32)
        ks = sb("ks", [P, 2, 2, NB], F32)
        ks1 = sb("ks1", [P, 2, REL3, HEADS1, NB], F32)
        mx = sb("mx", [P, NB], F32)
        mx1 = sb("mx1", [P, REL3, HEADS1, NB], F32)
        uv = sb("uv", [P, 2, NB], F32)
        uv1 = sb("uv1", [P, 2, REL3, HEADS1, NB], F32)
        uvc = sb("uvc", [P, REL3, HEADS1, NB, 4], F32)
        zc = sb("zc", [P, 2, NB], F32)
        bn = sb("bn", [P, NB, 2, 6], F32)
        stat = sb("stat", [P, NB, 2], F32)
        sd = sb("sd", [P, 2, NB], F32)
        waited = sb("waited", [P, 1], F32)
        flag_sb = sb("flag_sb", [1, 1], I32)
        rows = [wide[i][:].rearrange("p a (m f) -> p a m f", m=NB) for i in range(3)]
        cols_y = [wide[i][:].rearrange("p a (k n) -> p a k n", k=KB) for i in (2, 1)]
        prob_sets = [prob, cols_x]
        count16 = [multi[:, 1024 * r:1024 * (r + 1)].bitcast(I16).rearrange("p (m n) -> p m n", m=NB) for r in range(3)]
        vec = multi[:, 1024:1024 + 2 * D].rearrange("p (a f) -> p a f", a=2)
        vec4 = multi[:].rearrange("p (a f) -> p a f", a=NB)
        resid = multi[:].rearrange("p (m f) -> p m f", m=NB)
        scale_bc = multi[:, 1024:].rearrange("p (r n) -> p r n", r=REL4)
        y_tiles = [yt[:, 0], yt[:, 1], multi[:, 2560:2560 + N]]
        acc_flat = acc.rearrange("p m f -> p (m f)")
        uv_sets1 = [(acc_flat[:, 1024 * i:1024 * i + N], acc_flat[:, 1024 * i + N:1024 * (i + 1)]) for i in range(2)]
        uv_sets2 = [(r_den[:], v_bc[:]), tuple(mask[:, 2 * i:2 * i + 2, :].rearrange("p m n -> p (m n)").bitcast(F32) for i in range(2))]
        row_sets = [q_rows[0:2, :], prob[0:2, 0, 0, :]]
        y_ring = [yt[:, 0], yt[:, 1], hv.rearrange("p a n -> p (a n)")[:, 0:N]]
        query_products = [v_bc[:, 0:HW], r_den[:, 0:HW]]
        cnt16 = mask[:].bitcast(I16)
        ones_f = xt[:, 0, 0:P]
        pick_f = yt[0:4, :, 0:P]
        yt_row = yt[:].rearrange("p a n -> p (a n)")[:, 0:D]
        b_row = yt[:].rearrange("p a n -> p (a n)")[:, 0:D]
        xt_row = xt[:].rearrange("p a n -> p (a n)")[:, 0:D]
        ps = ctx.enter_context(nc.psum_tensor("ps", [P, 8, N], F32))

        consts = sem("consts")
        w_high = sem("w_high")
        w_low = sem("w_low")
        prod_done = sem("prod_done")
        tile_copied = sem("tile_copied")
        rows_ready = sem("rows_ready")
        rows_split = sem("rows_split")
        acc_added = sem("acc_added")
        agg_done = sem("agg_done")
        agg_read = sem("agg_read")
        misc_done = sem("misc_done")
        kc_ready = sem("kc_ready")
        uv_ready = sem("uv_ready")
        q_ready = sem("q_ready")
        vb_ready = sem("vb_ready")
        rd_done = sem("rd_done")
        max_done = sem("max_done")
        b_used = sem("b_used")
        diag_added = sem("diag_added")
        out_done = sem("out_done")
        den_read = sem("den_read")
        x_pre = sem("x_pre")
        x_exp = sem("x_exp")
        x_mid = sem("x_mid")
        x_hi = sem("x_hi")
        x_lo = sem("x_lo")
        rows_low = sem("rows_low")
        multiplied = sem("multiplied")
        query_summed = sem("query_summed")
        p_used = sem("p_used")
        row_done = sem("row_done")
        row_read = sem("row_read")
        turn_done = sem("turn_done")
        turn_hi = sem("turn_hi")
        turn_lo = sem("turn_lo")
        cnt_hi = sem("cnt_hi")
        cnt_lo = sem("cnt_lo")
        edge_done = sem("edge_done")
        y_done = sem("y_done")
        y_hi = sem("y_hi")
        y_lo = sem("y_lo")
        scale_ready = sem("scale_ready")
        var_ready = sem("var_ready")
        sd_ready = sem("sd_ready")
        acc_ready = sem("acc_ready")
        step = sem("step")
        vec_in = sem("vec_in")
        cnt_in = sem("cnt_in")
        mask_in = sem("mask_in")
        b_in = sem("b_in")
        small_in = sem("small_in")
        kept_out = sem("kept_out")

        block = ctx.enter_context(nc.Block())

        @block.sync
        def _(sp):
            with sp.Fori(1, PASSES) as j:
                for p in range(3):
                    sp.wait_ge(w_low, j * 3 + (p - 2))
                    sp.dma_start(w_raw[:, p], weights[bass.ds(j, 1), p]).then_inc(raw_in[p], 16)

        @block.gpsimd
        def _(pool):
            nc.gpsimd.memset(ident[:], 0.0).then_inc(consts, 1)
            nc.gpsimd.memset(ones_f, 1.0).then_inc(consts, 1)
            pool.wait_ge(consts, 2)
            nc.gpsimd.affine_select(out=ident[:], in_=ident[:], compare_op=ALU.not_equal, fill=1.0, base=0,
                                    pattern=[[-1, P]], channel_multiplier=1).then_inc(consts, 1)

            def low_of(dst, whole, high):
                return nc.gpsimd.tensor_tensor(dst, whole, high.bitcast(F32), ALU.subtract)

            def weights_low(slot, count):
                for p in range(3):
                    pool.wait_ge(w_high, count + (p + 1))
                    low_of(w_pair[:, slot, 1, 2 * p:2 * p + 2, :], w_raw[:, p],
                           w_pair[:, slot, 0, 2 * p:2 * p + 2, :]).then_inc(w_low, 1)

            def relation_low(first_tile, first_pass, queries):
                for r in range(REL3):
                    for u in range(8):
                        n, m = u // 4, u % 4
                        part = slice(n * HW, (n + 1) * HW)
                        pool.wait_ge(tile_copied, first_tile + 8 * r + u + 1)
                        low_of(rows[r][:, 1, m, part], hv[:, m % 2], rows[r][:, 0, m, part]).then_inc(rows_low, 1)
                        for v in range(2 if queries else 0):
                            t = 8 * r + u
                            if t:
                                pool.wait_ge(query_summed, 2 * t + v - 1)
                            nc.gpsimd.tensor_tensor(query_products[v], hv[:, m % 2], vec4[:, 2 + v, part],
                                                    ALU.mult).then_inc(multiplied, 1)
                        if m == 3:
                            weights_low(n, 3 * (first_pass + 2 * r + n))

            with pool.Fori(0, 17) as i:
                for slot in range(2):
                    weights_low(slot, i * 6 + 3 * slot)
            pool.wait_ge(vec_in, 176)
            relation_low(64, 34, True)
            items = relational_items()
            for i, (h, s, c) in enumerate(items):
                pool.wait_ge(x_hi, W_AT + i + 1)
                if c is not None or (i and items[i - 1][2] is not None):
                    pool.wait_ge(x_lo, W_AT + i)
                if c is None:
                    low_of(prob[:, 1, s % 4, :], y_ring[i % 3], prob[:, 0, s % 4, :]).then_inc(x_lo, 1)
                else:
                    f, part = PIECES[2 * h + c]
                    low_of(cols_x[part, 1, f, :], y_ring[i % 3][part], cols_x[part, 0, f, :]).then_inc(x_lo, 1)
            relation_low(88, 40, False)
            for t in range(REL3 * NB):
                r, s = t // NB, t % NB
                pool.wait_ge(x_hi, 140 + t + 1)
                low_of(prob_sets[r % 2][:, 1, s, :], y_ring[t % 3], prob_sets[r % 2][:, 0, s, :]).then_inc(x_lo, 1)
            with pool.Fori(23, PASSES // 2) as i:
                for slot in range(2):
                    weights_low(slot, i * 6 + 3 * slot)

        @block.tensor
        def _(pe):
            def product(j, m, left, free, value):
                pe.wait_ge(free, value)
                for k in range(KB):
                    if m == 0 and k % 2 == 0:
                        pe.wait_ge(w_low, j * 3 + (k // 2 + 1))
                    for a, b in ((0, 0), (0, 1), (1, 0)):
                        mm = nc.tensor.matmul(ps[:, m, 0:HW], left[:, a, k, m * P:(m + 1) * P], w_pair[:, slot_of[0], b, k, :],
                                              start=(k == 0 and a + b == 0), stop=(k == KB - 1 and a == 1))
                mm.then_inc(prod_done, 1)

            slot_of = [0]

            def turn_small(table, width):
                for m in range(NB):
                    mm = nc.tensor.transpose(ps[0:width, 6, m * P:(m + 1) * P], table[:, m, :], ident[:])
                mm.then_inc(misc_done, 1)

            def turn_source(h=0, into=0):
                for m in range(NB):
                    mm = nc.tensor.transpose(ps[0:2, 6 - 2 * into, m * P:(m + 1) * P], kc[:, h, m, :], ident[:])
                mm.then_inc(misc_done, 1)

            def spread_source(into=0):
                nc.tensor.matmul(ps[:, 7 - 2 * into, :], ones[0:2, :], row_sets[into], start=True, stop=True).then_inc(misc_done, 1)

            def spread_uv():
                nc.tensor.matmul(ps[:, 7, :], pick[:, 0, :], q_rows[:], start=True, stop=True)
                nc.tensor.matmul(ps[:, 6, :], pick[:, 1, :], q_rows[:], start=True, stop=True).then_inc(misc_done, 1)

            def turn(count):
                for f in range(KB):
                    if f >= 2:
                        pe.wait_ge(turn_lo, count + f - 1)
                    for m in range(NB):
                        mm = nc.tensor.transpose(ps[:, 4 + f % 2, m * P:(m + 1) * P], acc[:, m, f * P:(f + 1) * P], ident[:])
                    mm.then_inc(turn_done, 1)

            pe.wait_ge(consts, 5)
            pe.wait_ge(res_in, 16)
            turn(0)
            pe.wait_ge(small_in, 32)
            many = pe.value_load(flag_sb[0:1, 0:1], min_val=0, max_val=1)

            def head(h, parity, j_rows, j_out, with_next, with_last):
                if with_next:
                    for u in range(8):
                        n, m = u // 4, u % 4
                        slot_of[0] = n
                        if n == 0:
                            if with_last:
                                pe.wait_ge(acc_added, h * 8 + (m - 3))
                            product(j_rows, m, cols_x, tile_copied, h * 8 + (4 + m + 1))
                        else:
                            product(j_rows + 1, m, cols_x, tile_copied, h * 8 + (8 + m + 1))
                        if u == 0:
                            pe.wait_ge(kc_ready, h + 1)
                            if with_last:
                                pe.wait_ge(rd_done, h)
                            turn_source()
                        elif u == 1:
                            pe.wait_ge(q_ready, h * 2 + 1)
                            if with_last:
                                pe.wait_ge(x_pre, h * 10)
                            spread_source()
                        elif u == 4:
                            pe.wait_ge(uv_ready, h + 1)
                            turn_small(uvc[:, 0, 0], 4)
                        elif u == 6:
                            pe.wait_ge(q_ready, h * 2 + 2)
                            spread_uv()
                if with_last:
                    out_product(h - 1, j_out, tile_copied if with_next else None, None if with_next else h)
                pe.wait_ge(x_lo, h * 10 + 4)
                pe.wait_ge(vb_ready, h + 1)
                for s in range(NB):
                    for a in range(2):
                        mm = nc.tensor.matmul(ps[:, 6, :], ones[:], prob[:, a, s, :], start=(s + a == 0), stop=(s + a == NB))
                mm.then_inc(misc_done, 1)
                pe.wait_ge(rows_ready, h * 8 + 8)
                for f in range(KB):
                    if with_last or f >= 2:
                        pe.wait_ge(agg_read, h * 6 + (f - 1))
                    for s in range(NB):
                        for a, b in ((0, 0), (0, 1), (1, 0)):
                            mm = nc.tensor.matmul(ps[:, 4 + f % 2, :], rows[parity][:, a, s, f * P:(f + 1) * P], prob[:, b, s, :],
                                                  start=(s + a + b == 0), stop=(s == NB - 1 and a == 1))
                    mm.then_inc(agg_done, 1)

            def out_product(x_head, j, before, small_of=None):
                pe.wait_ge(x_lo, x_head * 10 + 10)
                for u in range(8):
                    n, m = u // 4, u % 4
                    slot_of[0] = n
                    if n == 0 and before is tile_copied:
                        product(j, m, cols_y[0], tile_copied, x_head * 8 + (16 + 4 + m + 1))
                    else:
                        product(j + n, m, cols_y[0], acc_added, x_head * 8 + (4 + m + 1 if n == 0 else 8 + m + 1))
                    if small_of is not None:
                        h = small_of
                        if u == 0:
                            pe.wait_ge(kc_ready, h + 1)
                            pe.wait_ge(rd_done, h)
                            turn_source()
                        elif u == 1:
                            pe.wait_ge(q_ready, h * 2 + 1)
                            spread_source()
                        elif u == 3:
                            pe.wait_ge(uv_ready, h + 1)
                            turn_small(uvc[:, 0, 0], 4)
                            pe.wait_ge(q_ready, h * 2 + 2)
                            spread_uv()

            pe.wait_ge(turn_lo, KB)
            for u in range(8):
                slot_of[0] = u // 4
                if u < 4:
                    product(0, u % 4, cols_x, turn_lo, KB)
                else:
                    product(1, u % 4, cols_x, tile_copied, u % 4 + 1)
            head(0, 0, 2, None, True, False)
            with pe.Fori(0, 3) as i:
                for odd in range(2):
                    h = i * 2 + (1 + odd)
                    head(h, 1 - odd, h * 4, h * 4 + 2, True, True)
            head(7, 1, None, 28, False, True)
            out_product(7, 30, acc_added)

            pe.wait_ge(kc_ready, 9)
            turn_source()
            pe.wait_ge(q_ready, 17)
            spread_source()
            pe.wait_ge(uv_ready, 9)
            turn_small(uvc[:, 0, 0], 4)
            pe.wait_ge(q_ready, 18)
            spread_uv()

            def row_sums(source, weights_of, first_sem, first_value, units):
                for m in range(NB):
                    for s in range(NB):
                        for a in range(2):
                            mm = nc.tensor.matmul(ps[:, 5, 2 * m:2 * m + 2], weights_of[:, a, s, m * P:(m + 1) * P], ones[:, 0:2],
                                                  start=(s + a == 0), stop=(s + a == NB))
                mm.then_inc(misc_done, 1)
                for u in range(8):
                    n, m = u // 4, u % 4
                    if n == 0:
                        pe.wait_ge(first_sem, first_value + m)
                    else:
                        pe.wait_ge(row_read, units + m + 1)
                    for s in range(NB):
                        for a, b in ((0, 0), (0, 1), (1, 0)):
                            mm = nc.tensor.matmul(ps[:, m, 0:HW], weights_of[:, a, s, m * P:(m + 1) * P],
                                                  source[:, b, s, n * HW:(n + 1) * HW],
                                                  start=(s + a + b == 0), stop=(s == NB - 1 and a == 1))
                    mm.then_inc(row_done, 1)

            pe.wait_ge(x_lo, 84)
            pe.wait_ge(rows_split, NB)
            row_sums(rows[0], prob, acc_added, 69, 0)
            pe.wait_ge(acc_ready, 1)
            turn(KB)

            def max_round(kc_count, q_count, part):
                if part == 0:
                    pe.wait_ge(kc_ready, kc_count)
                    turn_source()
                else:
                    pe.wait_ge(q_ready, q_count)
                    spread_source()

            pe.wait_ge(turn_lo, 2 * KB)
            for r in range(REL3):
                for u in range(8):
                    n, m = u // 4, u % 4
                    slot_of[0] = n
                    if r == 0 and n == 0:
                        product(32, m, cols_x, row_read, 4 + m + 1)
                    else:
                        product(32 + 2 * r + n, m, cols_x, tile_copied, 64 + 8 * r + 4 * n - 4 + m + 1)
                    if r:
                        max_round(9 + 4 * (r - 1) + u // 2 + 1, 18 + 4 * (r - 1) + u // 2 + 1, u % 2)
            pe.wait_ge(kc_ready, 21)
            turn_source(0, 0)
            turn_source(1, 1)
            for h in range(HEADS1):
                pe.wait_ge(q_ready, 27 + h)
                if h >= 2:
                    pe.wait_ge(max_done, 18 + h - 2)
                spread_source(h % 2)
                if h < 2:
                    turn_source(h + 2, h % 2)
            def turn_uv(g):
                turn_small(uvc[:, g % REL3, g // REL3], 4)

            pe.wait_ge(uv_ready, 10)
            for g in range(2):
                if g:
                    pe.wait_ge(vb_ready, 9 + g)
                turn_uv(g)
                pe.wait_ge(q_ready, 31 + g)
                spread_uv()
            pe.wait_ge(tile_copied, 88)
            pe.wait_ge(rows_low, 24)
            rounds = REL3 * HEADS1
            for g in range(rounds):
                h, r = g // REL3, g % REL3
                if r == 0 and h >= 2:
                    pe.wait_ge(agg_read, 48 + 2 * (h - 1))
                    pe.wait_ge(rd_done, 8 + h - 1)
                chunk0 = (0, 1, 3, 4)[h]
                for s in range(NB):
                    if s == 1 and g + 2 < rounds:
                        pe.wait_ge(vb_ready, 11 + g)
                        turn_uv(g + 2)
                    if s == 3 and g + 2 < rounds:
                        pe.wait_ge(q_ready, 33 + g)
                        spread_uv()
                    pe.wait_ge(x_lo, tile_at(h, r * NB + s) + 1)
                    begin, end = r == 0 and s == 0, r == REL3 - 1 and s == NB - 1
                    for a in range(2):
                        nc.tensor.matmul(ps[:, 4 + h % 2, :], ones[:], prob[:, a, s, :], start=(begin and a == 0), stop=(end and a == 1))
                    for c in range(2):
                        f = chunk0 + c
                        for a, b in ((0, 0), (0, 1), (1, 0)):
                            mm = nc.tensor.matmul(ps[:, 2 * (h % 2) + c, :], rows[r][:, a, s, f * P:(f + 1) * P], prob[:, b, s, :],
                                                  start=(begin and a + b == 0), stop=(end and a == 1))
                    mm.then_inc(p_used, 1)

            pe.wait_ge(x_lo, 140)
            for r in range(REL3):
                for u in range(8):
                    n, m = u // 4, u % 4
                    slot_of[0] = n
                    if r == 0 and n == 0:
                        product(38, m, cols_x, agg_read, 56)
                    else:
                        product(38 + 2 * r + n, m, cols_x, tile_copied, 88 + 8 * r + 4 * n - 4 + m + 1)
                    if r and u < 2:
                        max_round(21 + r, 42 + r, u)
            for part in range(2):
                max_round(24, 45, part)

            pe.wait_ge(uv_ready, 11)
            for r in range(REL3):
                if r:
                    pe.wait_ge(vb_ready, 21 + r)
                turn_small(uvc[:, r, 0], 4)
                pe.wait_ge(q_ready, 46 + r)
                spread_uv()
            pe.wait_ge(x_lo, 144)
            pe.wait_ge(rows_low, 48)
            row_sums(rows[0], prob_sets[0], tile_copied, 109, 8)
            pe.wait_ge(x_lo, 148)
            pe.wait_ge(den_read, 2)
            row_sums(rows[1], prob_sets[1], row_read, 13, 16)
            pe.wait_ge(x_lo, 152)
            pe.wait_ge(den_read, 3)
            row_sums(rows[2], prob_sets[0], row_read, 21, 24)

            def edge_sums(number, cnt):
                pe.wait_ge(cnt_lo, cnt)
                for f in range(KB):
                    t = number * KB + f
                    if t >= 2:
                        pe.wait_ge(y_done, t - 1)
                    bank = ps[:, 4 + f % 2, :]
                    nc.tensor.matmul(bank, rows[0][:, 0, 0, f * P:(f + 1) * P], prob[:, 0, 0, :], start=True, stop=False)
                    with pe.If(many > 0):
                        for s in range(NB):
                            for a in range(2):
                                nc.tensor.matmul(bank, rows[0][:, a, s, f * P:(f + 1) * P], prob[:, 1, s, :], start=False, stop=False)
                    for s in range(NB):
                        for a in range(2):
                            if s + a:
                                mm = nc.tensor.matmul(bank, rows[0][:, a, s, f * P:(f + 1) * P], prob[:, 0, s, :],
                                                      start=False, stop=(s + a == NB))
                    mm.then_inc(edge_done, 1)

            def degrees(spread_only):
                for s in range(NB):
                    for a in range(2):
                        mm = nc.tensor.matmul(ps[:, 6, :], ones[:], prob[:, a, s, :], start=(s + a == 0), stop=(s + a == NB))
                if not spread_only:
                    for m in range(NB):
                        for s in range(NB):
                            for a in range(2):
                                mm = nc.tensor.matmul(ps[:, 7, 2 * m:2 * m + 2], prob[:, a, s, m * P:(m + 1) * P], ones[:, 0:2],
                                                      start=(s + a == 0), stop=(s + a == NB))
                mm.then_inc(misc_done, 1)

            def layer_product(j, left, added):
                for u in range(8):
                    n, m = u // 4, u % 4
                    slot_of[0] = n
                    product(j + n, m, left, acc_added, added + 4 * n - 4 + m + 1)

            added = 72
            pe.wait_ge(row_read, 32)
            for layer in range(3):
                for r in range(REL4):
                    if layer == 0:
                        pe.wait_ge(cnt_lo, r + 1)
                        if r:
                            pe.wait_ge(scale_ready, r)
                        degrees(True)
                    pe.wait_ge(rows_split, NB * (2 + layer))
                    edge_sums(4 * layer + r, 4 * layer + r + 1)
                    if r == 0:
                        pe.wait_ge(acc_ready, 2)
                        if layer:
                            pe.wait_ge(acc_added, added)
                        pe.wait_ge(y_done, KB * (4 * layer + 1))
                        turn(KB * (2 + layer))
                        pe.wait_ge(turn_lo, KB * (3 + layer))
                        layer_product(44 + 10 * layer, cols_x, added)
                    else:
                        pe.wait_ge(y_lo, KB * (4 * layer + r))
                        layer_product(44 + 10 * layer + 2 * r, cols_y[(r - 1) % 2], added)
                    added += 8
                pe.wait_ge(y_lo, KB * (4 * layer + 4))
                if layer == 2:
                    pe.wait_ge(cnt_lo, 13)
                    pe.wait_ge(scale_ready, REL4)
                    degrees(False)
                layer_product(52 + 10 * layer, cols_y[1], added)
                added += 8
            for layer in range(2):
                pe.wait_ge(rows_split, NB * (5 + layer))
                edge_sums(12 + layer, 13)
                pe.wait_ge(y_lo, KB * (13 + layer))
                layer_product(74 + 2 * layer, cols_y[0], added)
                added += 8

        @block.scalar
        def _(act):
            def copy(dst, src):
                return nc.scalar.activation(dst, src, ACT.Copy)

            def split_high(j, slot, wait=True):
                for p in range(3):
                    act.wait_ge(raw_in[p], j * 16 + 16)
                    if p == 0 and wait:
                        act.wait_ge(prod_done, j * 4 - 4)
                    copy(w_pair[:, slot, 0, 2 * p:2 * p + 2, :], w_raw[:, p]).then_inc(w_high, 1)

            def copy_tile(j, m, n, q, dst, first=False, lows=None):
                act.wait_ge(prod_done, j * 4 + (m + 1))
                if not first:
                    act.wait_ge(rows_ready, q - 1)
                if lows is not None and lows > 1:
                    act.wait_ge(rows_low, lows - 1)
                copy(hv[:, m % 2], ps[:, m, 0:HW])
                copy(dst[:, 0, m, n * HW:(n + 1) * HW], ps[:, m, 0:HW]).then_inc(tile_copied, 1)

            def copy_rows(count, width):
                act.wait_ge(misc_done, count)
                copy(q_rows[0:width, :], ps[0:width, 6, :]).then_inc(q_ready, 1)

            def copy_v(count):
                act.wait_ge(misc_done, count)
                copy(v_bc[:], ps[:, 6, :]).then_inc(vb_ready, 1)

            def copy_uv(count, target):
                act.wait_ge(misc_done, count)
                copy(target[0], ps[:, 7, :])
                copy(target[1], ps[:, 6, :]).then_inc(vb_ready, 1)

            def exponential(w, slot, bias):
                act.wait_ge(x_pre, w + 1)
                nc.scalar.activation(xt[:, slot], xt[:, slot], ACT.Exp, bias=bias).then_inc(x_exp, 1)

            def elu_exponential(w, slot, y, bias, part=slice(0, P)):
                act.wait_ge(x_pre, w + 1)
                nc.scalar.activation(xt[part, slot], xt[part, slot], ACT.Exp)
                nc.scalar.activation(y[part], y[part], ACT.Identity, bias=bias).then_inc(x_exp, 1)

            def high(w, y, dst, part=slice(0, P)):
                act.wait_ge(x_mid, w + 1)
                copy(dst, y[part]).then_inc(x_hi, 1)

            def turn(count, relu=False):
                for f in range(KB):
                    act.wait_ge(turn_done, count + f + 1)
                    nc.scalar.activation(cols_x[:, 0, f, :], ps[:, 4 + f % 2, :], ACT.Relu if relu else ACT.Copy).then_inc(turn_hi, 1)

            act.dma_start(b_cols[:], bias_cols).then_inc(small_in, 16)
            act.dma_start(flag_sb[:], flag).then_inc(small_in, 16)
            act.dma_start(vec, attn0[0:1].partition_broadcast(P)).then_inc(vec_in, 16)
            act.dma_start(count16[0], counts[TOTAL]).then_inc(cnt_in, 16)
            act.dma_start(mask[:], masks[0]).then_inc(mask_in, 16)
            split_high(0, 0, wait=False)
            turn(0)
            split_high(1, 1, wait=False)

            def head(h, parity, j_rows, j_out, with_next, with_last):
                if with_next:
                    for u in range(8):
                        n, m = u // 4, u % 4
                        copy_tile(j_rows + n, m, n, h * 8 + (8 + u), rows[1 - parity])
                        if u == 0:
                            copy_rows(h * 5 + 1, 2)
                        elif u == 3:
                            split_high(j_rows + 2, 0)
                        elif u == 4:
                            copy_rows(h * 5 + 3, 4)
                        elif u == 6:
                            copy_v(h * 5 + 4)
                    split_high(j_rows + 3, 1)
                    act.wait_ge(rows_ready, h * 8 + 16)
                    act.dma_start(vec, attn0[bass.ds(h + 2, 1)].partition_broadcast(P)).then_inc(vec_in, 16)
                else:
                    copy_rows(h * 5 + 1, 2)
                    copy_rows(h * 5 + 3, 4)
                    copy_v(h * 5 + 4)
                for s in range(NB + 1):
                    if s < NB:
                        exponential(h * 10 + s, s % 2, ks[:, parity, 1, s:s + 1])
                    if s >= 1:
                        high(h * 10 + (s - 1), y_tiles[(s - 1) % 2], prob[:, 0, s - 1, :])
                    if s == 3 and with_last:
                        split_high(j_out + 2, 0)
                if with_last:
                    split_high(j_out + 3, 1)
                for f in range(KB + 1):
                    if f < KB:
                        elu_exponential(h * 10 + (4 + f), f % 2, y_tiles[f % 3], b_cols[:, bass.ds(h * KB + f, 1)])
                    if f >= 1:
                        high(h * 10 + (4 + f - 1), y_tiles[(f - 1) % 3], cols_y[0][:, 0, f - 1, :])

            for u in range(8):
                copy_tile(u // 4, u % 4, u // 4, u, rows[0], first=u < 2)
                if u == 3:
                    split_high(2, 0)
            split_high(3, 1)
            act.wait_ge(rows_ready, 8)
            act.dma_start(vec, attn0[1:2].partition_broadcast(P)).then_inc(vec_in, 16)
            head(0, 0, 2, None, True, False)
            with act.Fori(0, 3) as i:
                for odd in range(2):
                    h = i * 2 + (1 + odd)
                    head(h, 1 - odd, h * 4, h * 4 + 2, True, True)
            head(7, 1, None, 28, False, True)
            split_high(32, 0)
            split_high(33, 1)

            copy_rows(41, 2)
            copy_rows(43, 4)
            copy_v(44)
            for s in range(NB + 1):
                if s < NB:
                    exponential(80 + s, s % 2, ks[:, 0, 1, s:s + 1])
                if s >= 1:
                    high(80 + s - 1, y_tiles[(s - 1) % 2], prob[:, 0, s - 1, :])

            def norm(layer):
                act.wait_ge(var_ready, layer + 1)
                nc.scalar.activation(sd[:, 0], stat[:, :, 1], ACT.Sqrt).then_inc(sd_ready, 1)

            def keep(layer):
                act.wait_ge(acc_ready, layer + 1)
                act.dma_start(kept, acc).then_inc(kept_out, 16)

            act.wait_ge(x_lo, 84)
            act.dma_start(b_row, bias_rows[0:1].partition_broadcast(P)).then_inc(b_in, 16)
            act.dma_start(resid, x).then_inc(res_in, 16)
            norm(0)
            act.dma_start(vec4, attn1[1:2].partition_broadcast(P)).then_inc(vec_in, 16)
            keep(0)
            turn(KB)
            act.wait_ge(kept_out, 16)

            act.dma_start(acc, attn1[0:1].partition_broadcast(P)).then_inc(vec_in, 16)
            act.dma_start(mask[:], masks[1]).then_inc(mask_in, 16)

            def sum_queries(t):
                r, n, m = t // 8, t % 8 // 4, t % 4
                for v in range(2):
                    act.wait_ge(multiplied, 2 * t + v + 1)
                    nc.scalar.activation(query_products[v], query_products[v], ACT.Copy,
                                         accum_out=al_half[:, n, r, v, m:m + 1]).then_inc(query_summed, 1)

            for r in range(REL3):
                for u in range(8):
                    n, m = u // 4, u % 4
                    if 8 * r + u >= 2:
                        sum_queries(8 * r + u - 2)
                    copy_tile(32 + 2 * r + n, m, n, 64 + 8 * r + u, rows[r], lows=8 * r + u)
                    if m == 3:
                        split_high(34 + 2 * r + n, n)
                    if r and u % 2 == 0:
                        copy_rows(45 + 8 * (r - 1) + u + 1, 2)
                if r:
                    act.wait_ge(max_done, 9 + 4 * r)
                    act.dma_start(mask[:], masks[1 + r]).then_inc(mask_in, 16)
            for t in (22, 23):
                sum_queries(t)
            act.wait_ge(rows_ready, 88)
            for r in range(REL3):
                act.dma_start(count16[r], counts[SLOT3 + r]).then_inc(cnt_in, 16)
            for h, turned in enumerate((62, 63, 65, 67)):
                act.wait_ge(misc_done, turned)
                copy(row_sets[h % 2], ps[0:2, 6 - 2 * (h % 2), :]).then_inc(q_ready, 1)
            copy_rows(70, 4)
            copy_uv(71, uv_sets1[0])
            items = relational_items()

            def exp_item(i):
                if i < len(items):
                    h, s, c = items[i]
                    if c is None:
                        exponential(W_AT + i, i % 2, ks1[:, 1, s // 4, h, s % 4:s % 4 + 1])
                    else:
                        f, part = PIECES[2 * h + c]
                        elu_exponential(W_AT + i, i % 2, y_ring[i % 3], b_cols[part, HEADS0 * KB + f:HEADS0 * KB + f + 1], part)

            def high_item(i):
                if i >= 1:
                    h, s, c = items[i - 1]
                    if c is None:
                        tile = 12 * h + s
                        if tile >= NB:
                            act.wait_ge(p_used, tile - NB + 1)
                        high(W_AT + i - 1, y_ring[(i - 1) % 3], prob[:, 0, s % 4, :])
                        g = tile // 4 + 1
                        if g < REL3 * HEADS1 and s % 4 == 0:
                            copy_rows(70 + 2 * g, 4)
                        elif g < REL3 * HEADS1 and s % 4 == 1:
                            copy_uv(71 + 2 * g, uv_sets1[g % 2])
                    else:
                        f, part = PIECES[2 * h + c]
                        high(W_AT + i - 1, y_ring[(i - 1) % 3], cols_x[part, 0, f, :], part)

            for i in range(len(items) + 1):
                result_tile = i < len(items) and items[i][2] is not None
                for stage in (high_item, exp_item) if result_tile else (exp_item, high_item):
                    stage(i)

            act.dma_start(acc[:, 0:2], attn2.partition_broadcast(P)).then_inc(vec_in, 16)
            act.dma_start(mask[:], masks[1]).then_inc(mask_in, 16)
            for r in range(REL3):
                for u in range(8):
                    n, m = u // 4, u % 4
                    copy_tile(38 + 2 * r + n, m, n, 88 + 8 * r + u, rows[r], lows=24 + 8 * r + u)
                    if m == 3:
                        split_high(40 + 2 * r + n, n)
                    if r and u == 0:
                        copy_rows(93 + 2 * r - 1, 2)
                    if r and u == 7:
                        act.wait_ge(max_done, 21 + r)
                        act.dma_start(mask[:], masks[1 + r]).then_inc(mask_in, 16)
            copy_rows(98, 2)
            for r in range(2):
                copy_rows(100 + 2 * r, 4)
                copy_uv(101 + 2 * r, uv_sets2[r])
            copy_rows(104, 4)
            for r in range(REL3):
                if r == 1:
                    act.wait_ge(x_mid, 144)
                    copy_uv(105, uv_sets2[0])
                if r == 2:
                    act.wait_ge(row_done, 16)
                for s in range(NB + 1):
                    if s < NB:
                        exponential(140 + 4 * r + s, s % 2, ks1[:, 1, r, 0, s:s + 1])
                    if s >= 1:
                        high(140 + 4 * r + s - 1, y_ring[(4 * r + s - 1) % 3], prob_sets[r % 2][:, 0, s - 1, :])
            act.wait_ge(x_lo, 152)
            act.dma_start(b_row, bias_rows[1:2].partition_broadcast(P)).then_inc(b_in, 16)
            act.dma_start(resid, kept).then_inc(res_in, 16)
            act.dma_start(cnt16, counts[0]).then_inc(cnt_in, 16)
            norm(1)

            def count_high(number, after):
                act.wait_ge(cnt_in, 16 * (4 + number))
                if number > 1:
                    act.wait_ge(edge_done, KB * (number - 1))
                else:
                    act.wait_ge(row_done, 32)
                copy(prob[:, 0], cnt16).then_inc(cnt_hi, 1)
                if after is not None:
                    act.wait_ge(cnt_lo, number)
                    act.dma_start(cnt16, after).then_inc(cnt_in, 16)

            def edge_high(number, dst):
                for f in range(KB):
                    t = number * KB + f
                    act.wait_ge(y_done, t + 1)
                    copy(dst[:, 0, f, :], xt[:, f % 2]).then_inc(y_hi, 1)

            for layer in range(3):
                j = 44 + 10 * layer
                if layer == 0:
                    count_high(1, counts[1])
                    keep(1)
                act.wait_ge(b_used, 2 + layer)
                act.dma_start(b_row, bias_rows[2 + layer:3 + layer].partition_broadcast(P)).then_inc(b_in, 16)
                for r in range(REL4):
                    edge_high(4 * layer + r, cols_y[r % 2])
                    if r == 0:
                        turn(KB * (2 + layer), relu=layer > 0)
                    if r + 1 < REL4:
                        count_high(4 * layer + r + 2, counts[TOTAL if layer == 2 and r == 2 else (r + 2) % REL4])
                    elif layer == 2:
                        act.wait_ge(y_lo, KB * 12)
                        act.wait_ge(kept_out, 32)
                        act.dma_start(resid, kept).then_inc(res_in, 16)
                        act.wait_ge(diag_added, 1)
                        count_high(13, None)
                    else:
                        count_high(4 * layer + 5, counts[1])
                    for n in range(2):
                        split_high(j + 2 * r + n + 2, n)
                if layer == 2:
                    act.wait_ge(misc_done, 113)
                    nc.scalar.activation(v_bc[:], ps[:, 6, :], ACT.Sqrt)
                    nc.scalar.activation(zc[:, 0], ps[:, 7, 0:2 * NB:2], ACT.Sqrt).then_inc(sd_ready, 1)
                for n in range(2):
                    split_high(j + 10 + n, n)
            norm(2)
            keep(2)
            for layer in range(2):
                act.wait_ge(b_used, 5 + layer)
                act.dma_start(b_row, bias_rows[5 + layer:6 + layer].partition_broadcast(P)).then_inc(b_in, 16)
                edge_high(12 + layer, cols_y[0])
                if layer == 0:
                    act.wait_ge(kept_out, 48)
                    act.dma_start(resid, kept).then_inc(res_in, 16)
                    for n in range(2):
                        split_high(76 + n, n)
            norm(3)
            act.wait_ge(acc_ready, 4)
            act.dma_start(out, acc).then_inc(out_done, 16)
            act.wait_ge(out_done, 16)

        @block.vector
        def _(dve):
            base, local = [0], [0]

            def mark(ins):
                local[0] += 1
                ins.then_inc(step, 1)

            def wait_steps():
                dve.wait_ge(step, base[0] + local[0])

            def wait_all_but_one():
                dve.wait_ge(step, base[0] + (local[0] - 1))

            def sub(dst, a, b):
                return nc.vector.tensor_tensor(dst, a, b, ALU.subtract)

            def add(dst, a, b):
                return nc.vector.tensor_tensor(dst, a, b, ALU.add)

            def copy(dst, src):
                return nc.vector.tensor_copy(dst, src)

            def dot(scratch, a, b, start, total):
                return nc.vector.tensor_tensor_reduce(out=scratch, in0=a, in1=b, scale=1.0, scalar=start,
                                                      op0=ALU.mult, op1=ALU.add, accum_out=total)

            def f32(ap):
                return ap.bitcast(F32)

            def turn(count, relu=False):
                for f in range(KB):
                    dve.wait_ge(turn_hi, count + f + 1)
                    if relu:
                        ins = nc.vector.scalar_tensor_tensor(cols_x[:, 1, f, :], ps[:, 4 + f % 2, :], 0.0, f32(cols_x[:, 0, f, :]),
                                                             ALU.max, ALU.subtract)
                    else:
                        ins = sub(cols_x[:, 1, f, :], ps[:, 4 + f % 2, :], f32(cols_x[:, 0, f, :]))
                    ins.then_inc(turn_lo, 1)

            def split_tile(q, m, n, dst, dots):
                dve.wait_ge(tile_copied, q + 1)
                if not (isinstance(q, int) and q == 0):
                    dve.wait_ge(rows_ready, q)
                tile = hv[:, m % 2]
                part = slice(n * HW, (n + 1) * HW)
                if dst is not None:
                    sub(dst[:, 1, m, part], tile, f32(dst[:, 0, m, part]))
                for v, (vector, total) in enumerate(dots):
                    if v >= 2:
                        wait_all_but_one()
                    if n == 0:
                        ins = dot(yt[:, v % 2, 0:HW], tile, vector[:, part], 0.0, al_part[:, v, m:m + 1])
                    else:
                        ins = dot(yt[:, v % 2, 0:HW], tile, vector[:, part], al_part[:, v, m:m + 1], total[:, m:m + 1])
                    ins.then_inc(rows_ready, 1) if v == len(dots) - 1 else mark(ins)

            def source_columns(term, scaled=None, h=0):
                high, low_part = kc[:, h, :, 0], kc[:, h, :, 1]
                mark(nc.vector.tensor_copy(high.bitcast(F32R), term))
                if scaled is not None:
                    nc.vector.tensor_scalar(scaled[0], term, 1.0 - SLOPE, None, ALU.mult)
                    nc.vector.tensor_scalar(scaled[1], term, SLOPE, None, ALU.mult)
                wait_steps()
                sub(low_part, term, high).then_inc(kc_ready, 1)

            def maxima(misc, total, done, tiles=None, bank=7):
                if tiles is not None:
                    dve.wait_ge(x_lo, tiles)
                dve.wait_ge(misc_done, misc)
                nc.vector.memset(waited[:], 0.0)
                for m in range(NB):
                    ins = nc.vector.tensor_tensor_reduce(out=(xt, yt)[m // 2][:, m % 2], in0=ps[:, bank, :], in1=mask[:, m, :], scale=1.0,
                                                         scalar=-3.0e38, op0=ALU.add, op1=ALU.max, accum_out=total[:, m:m + 1])
                ins.then_inc(max_done, 1)
                dve.wait_ge(max_done, done)

            def leaky(z):
                wait_steps()
                mark(nc.vector.scalar_tensor_tensor(z, z, SLOPE, z, ALU.mult, ALU.max))
                wait_steps()

            def u_and_v(target, largest, u, v, parts):
                mark(sub(u, target, largest))
                mark(nc.vector.scalar_tensor_tensor(v, target, SLOPE, largest, ALU.mult, ALU.subtract))
                wait_steps()
                mark(nc.vector.tensor_copy(parts[0].bitcast(F32R), u))
                mark(nc.vector.tensor_copy(parts[2].bitcast(F32R), v))
                wait_steps()
                mark(sub(parts[1], u, parts[0]))
                return sub(parts[3], v, parts[2])

            def exponent(w, slot, source, u, v, first=False):
                if not first:
                    dve.wait_ge(x_mid, w - 1)
                nc.vector.scalar_tensor_tensor(xt[:, slot], u, source, v, ALU.add, ALU.max).then_inc(x_pre, 1)

            def weigh(w, slot, y, count, before=None):
                dve.wait_ge(x_exp, w + 1)
                if before is not None:
                    dve.wait_ge(x_lo, before)
                nc.vector.scalar_tensor_tensor(y, xt[:, slot], 1.0, count, ALU.min, ALU.mult).then_inc(x_mid, 1)

            def low(w, y, dst, high, part=slice(0, P)):
                dve.wait_ge(x_hi, w + 1)
                sub(dst, y[part], f32(high)).then_inc(x_lo, 1)

            def elu_start(w, read, slot, y, bank, bias, before, part=slice(0, P)):
                dve.wait_ge(x_lo, before)
                nc.vector.tensor_tensor(y[part], bank[part], r_den[part], ALU.mult).then_inc(agg_read, 1)
                dve.wait_ge(agg_read, read + 1)
                nc.vector.tensor_scalar(xt[part, slot], y[part], bias, 0.0, ALU.add, ALU.min).then_inc(x_pre, 1)

            def elu_end(w, slot, y, part=slice(0, P)):
                dve.wait_ge(x_exp, w + 1)
                nc.vector.scalar_tensor_tensor(y[part], xt[part, slot], -1.0, y[part],
                                               ALU.add, ALU.max).then_inc(x_mid, 1)

            def denominators(bank):
                mark(nc.vector.tensor_scalar(r_den[:], bank, EPS_SOFTMAX, None, ALU.add))
                wait_steps()
                nc.vector.reciprocal(r_den[:], r_den[:]).then_inc(rd_done, 1)

            dve.wait_ge(consts, 3)
            nc.vector.memset(pick_f, 0.0).then_inc(consts, 1)
            dve.wait_ge(consts, 4)
            mark(nc.vector.memset(pick_f[0:2, 0, :], 1.0))
            wait_steps()
            mark(nc.vector.tensor_scalar(pick_f[:, 1, :], pick_f[:, 0, :], -1.0, 1.0, ALU.mult, ALU.add))
            wait_steps()
            mark(copy(ones[:], ones_f))
            copy(pick[:], pick_f).then_inc(consts, 1)
            turn(0)
            nc.vector.memset(acc, 0.0).then_inc(acc_added, 8)
            dve.wait_ge(small_in, 32)
            dve.wait_ge(mask_in, 16)
            dve.wait_ge(cnt_in, 16)

            def rows_tile(x_head, parity, u):
                split_tile(x_head * 8 + u, u % 4, u // 4, rows[parity],
                           [(vec[:, v], al[:, parity, v]) for v in range(2)])

            def product_tile(j, u, into_first=False):
                n, m = u // 4, u % 4
                part = slice(n * HW, (n + 1) * HW)
                dve.wait_ge(prod_done, j * 4 + (u + 1))
                if into_first:
                    copy(acc[:, m, part], ps[:, m, 0:HW]).then_inc(acc_added, 1)
                else:
                    add(acc[:, m, part], acc[:, m, part], ps[:, m, 0:HW]).then_inc(acc_added, 1)

            def prob_slot(h, parity, s, with_last=True):
                if s < NB:
                    exponent(h * 10 + s, s % 2, ks[:, parity, 0, s:s + 1], ps[:, 7, :], v_bc[:], first=not with_last and s < 2)
                if 1 <= s <= NB:
                    weigh(h * 10 + (s - 1), (s - 1) % 2, y_tiles[(s - 1) % 2], count16[0][:, s - 1, :],
                          before=None if not with_last and s <= 2 else h * 10 + (s - 2))
                if s >= 2:
                    low(h * 10 + (s - 2), y_tiles[s % 2], prob[:, 1, s - 2, :], prob[:, 0, s - 2, :])

            def small_uv(h, parity, first=False):
                target = al[:, parity, 1]
                maxima(h * 5 + 2, mx, h + 1, None if first else h * 10)
                mark(add(mx[:], mx[:], target))
                leaky(mx[:])
                u_and_v(target, mx[:], uv[:, 0], uv[:, 1], [uvc[:, 0, 0, :, i] for i in range(4)]).then_inc(uv_ready, 1)

            def head(h, parity, j_rows, j_out, with_next, with_last):
                if with_next:
                    dve.wait_ge(vec_in, h * 16 + 32)
                    if with_last:
                        dve.wait_ge(x_lo, h * 10)
                    for u in range(8):
                        rows_tile(h + 1, 1 - parity, u)
                        if u == 2:
                            dve.wait_ge(rows_ready, h * 8 + 11)
                            small_uv(h, parity, first=not with_last)
                    dve.wait_ge(rows_ready, h * 8 + 16)
                    source_columns(al[:, 1 - parity, 0], (ks[:, 1 - parity, 0], ks[:, 1 - parity, 1]))
                else:
                    small_uv(h, parity)
                dve.wait_ge(misc_done, h * 5 + 4)
                dve.wait_ge(vb_ready, h + 1)
                for u in range(8):
                    if with_last:
                        product_tile(j_out, u)
                    if u < NB + 2:
                        prob_slot(h, parity, u, with_last)
                dve.wait_ge(misc_done, h * 5 + 5)
                denominators(ps[:, 6, :])
                dve.wait_ge(rd_done, h + 1)
                for s in range(KB + 2):
                    if s < KB:
                        dve.wait_ge(agg_done, h * 6 + (s + 1))
                        elu_start(h * 10 + (4 + s), h * 6 + s, s % 2, y_tiles[s % 3], ps[:, 4 + s % 2, :],
                                  b_cols[:, bass.ds(h * KB + s, 1)], h * 10 + (4 + max(s - 2, 0)))
                    if 1 <= s <= KB:
                        elu_end(h * 10 + (4 + s - 1), (s - 1) % 2, y_tiles[(s - 1) % 3])
                    if s >= 2:
                        low(h * 10 + (4 + s - 2), y_tiles[(s - 2) % 3], cols_y[0][:, 1, s - 2, :], cols_y[0][:, 0, s - 2, :])

            dve.wait_ge(vec_in, 16)
            for u in range(8):
                rows_tile(0, 0, u)
            dve.wait_ge(rows_ready, 8)
            source_columns(al[:, 0, 0], (ks[:, 0, 0], ks[:, 0, 1]))
            head(0, 0, 2, None, True, False)
            base[0], local[0] = local[0], 0
            first_steps = base[0]
            with dve.Fori(0, 3) as i:
                for odd in range(2):
                    base[0], local[0] = i * (2 * HEAD_STEPS) + (first_steps + odd * HEAD_STEPS), 0
                    h = i * 2 + (1 + odd)
                    head(h, 1 - odd, h * 4, h * 4 + 2, True, True)
                    assert local[0] == HEAD_STEPS, local
            base[0], local[0] = first_steps + 6 * HEAD_STEPS, 0
            head(7, 1, None, 28, False, True)

            def split_row(m, relu=False, scaled=False):
                if relu:
                    mark(nc.vector.tensor_scalar(rows[0][:, 0, m, :], acc[:, m, :], 0.0, None, ALU.max))
                elif scaled:
                    mark(nc.vector.tensor_scalar(rows[0][:, 0, m, :], acc[:, m, :], zc[:, 1, m:m + 1], None, ALU.mult))
                else:
                    mark(copy(rows[0][:, 0, m, :], acc[:, m, :]))
                wait_steps()
                high = f32(rows[0][:, 0, m, :])
                if relu or scaled:
                    ins = nc.vector.scalar_tensor_tensor(rows[0][:, 1, m, :], acc[:, m, :], 0.0 if relu else zc[:, 1, m:m + 1], high,
                                                         ALU.max if relu else ALU.mult, ALU.subtract)
                else:
                    ins = sub(rows[0][:, 1, m, :], acc[:, m, :], high)
                ins.then_inc(rows_split, 1)

            dve.wait_ge(vec_in, 144)
            dve.wait_ge(x_lo, 80)
            for u in range(8):
                product_tile(30, u)
                if u >= NB:
                    m = u - NB
                    dve.wait_ge(acc_added, 64 + u + 1)
                    wait_steps()
                    for v in range(2):
                        mark(dot((xt_row, yt_row)[v], acc[:, m, :], vec[:, v], 0.0, al[:, 0, v, m:m + 1]))
                    split_row(m)
            wait_steps()
            source_columns(al[:, 0, 0], (ks[:, 0, 0], ks[:, 0, 1]))
            small_uv(8, 0)
            dve.wait_ge(misc_done, 44)
            dve.wait_ge(vb_ready, 9)
            for s in range(NB + 2):
                prob_slot(8, 0, s)

            def read_denominators(misc, first):
                dve.wait_ge(misc_done, misc)
                bank = ps[:, 5, 0:2 * NB:2]
                if first:
                    copy(zc[:, 0], bank).then_inc(den_read, 1)
                else:
                    add(zc[:, 0], zc[:, 0], bank).then_inc(den_read, 1)

            def read_rows(done, first):
                for u in range(8):
                    n, m = u // 4, u % 4
                    part = slice(n * HW, (n + 1) * HW)
                    dve.wait_ge(row_done, done + u + 1)
                    if first:
                        copy(acc[:, m, part], ps[:, m, 0:HW]).then_inc(row_read, 1)
                    else:
                        add(acc[:, m, part], acc[:, m, part], ps[:, m, 0:HW]).then_inc(row_read, 1)

            def add_bias_to_residual(layer):
                dve.wait_ge(res_in, 16 * (2 + layer))
                dve.wait_ge(b_in, 16 * B_ROW_AT[layer])
                for m in range(NB):
                    ins = add(resid[:, m, :], resid[:, m, :], b_row)
                    ins.then_inc(b_used, 1) if m == NB - 1 else mark(ins)
                dve.wait_ge(b_used, B_ROW_AT[layer])

            def invert_denominators(reads):
                dve.wait_ge(den_read, reads)
                mark(nc.vector.tensor_scalar(zc[:, 0], zc[:, 0], EPS_SOFTMAX, None, ALU.add))
                wait_steps()
                mark(nc.vector.reciprocal(zc[:, 1], zc[:, 0]))
                wait_steps()

            def norm(layer, tile):
                for u in range(8):
                    n, m = u // 4, u % 4
                    tile(u)
                    mark(nc.vector.bn_stats(bn[:, m, n], acc[:, m, n * HW:(n + 1) * HW]))
                    if n == 1:
                        wait_steps()
                        mark(nc.vector.bn_aggr(stat[:, m, :], bn[:, m].rearrange("p n s -> p (n s)")))
                wait_steps()
                nc.vector.tensor_scalar(stat[:, :, 1], stat[:, :, 1], EPS_NORM, None, ALU.add).then_inc(var_ready, 1)
                dve.wait_ge(sd_ready, SD_AT[layer])
                mark(nc.vector.reciprocal(sd[:, 1], sd[:, 0]))
                wait_steps()
                for m in range(NB):
                    ins = nc.vector.tensor_scalar(acc[:, m, :], acc[:, m, :], stat[:, m, 0:1], sd[:, 1, m:m + 1],
                                                  ALU.subtract, ALU.mult)
                ins.then_inc(acc_ready, 1)

            def attention_rows(u):
                n, m = u // 4, u % 4
                part = slice(n * HW, (n + 1) * HW)
                dve.wait_ge(row_done, u + 1)
                nc.vector.scalar_tensor_tensor(acc[:, m, part], ps[:, m, 0:HW], zc[:, 1, m:m + 1], resid[:, m, part],
                                               ALU.mult, ALU.add).then_inc(row_read, 1)
                dve.wait_ge(row_read, u + 1)

            def relation_rows(u):
                n, m = u // 4, u % 4
                part = slice(n * HW, (n + 1) * HW)
                dve.wait_ge(row_done, 24 + u + 1)
                add(acc[:, m, part], acc[:, m, part], ps[:, m, 0:HW]).then_inc(row_read, 1)
                dve.wait_ge(row_read, 24 + u + 1)
                mark(nc.vector.scalar_tensor_tensor(acc[:, m, part], acc[:, m, part], zc[:, 1, m:m + 1], resid[:, m, part],
                                                    ALU.mult, ALU.add))
                wait_steps()

            read_denominators(45, True)
            dve.wait_ge(x_lo, 84)
            add_bias_to_residual(0)
            invert_denominators(1)
            norm(0, attention_rows)
            dve.wait_ge(acc_ready, 1)
            turn(KB)

            def relation_uv(heads):
                span = slice(0, heads)
                z, target = mx1[:, :, span], al1[:, 1, :, span]
                mark(add(z, z, target))
                leaky(z)
                mark(nc.vector.tensor_tensor(mx1[:, 0, span], mx1[:, 0, span], mx1[:, 1, span], ALU.max))
                wait_steps()
                mark(nc.vector.tensor_tensor(mx1[:, 0, span], mx1[:, 0, span], mx1[:, 2, span], ALU.max))
                wait_steps()
                for r in range(REL3):
                    ins = u_and_v(target[:, r], mx1[:, 0, span], uv1[:, 0, r, span], uv1[:, 1, r, span],
                                  [uvc[:, r, span, :, i] for i in range(4)])
                    ins.then_inc(uv_ready, 1) if r == REL3 - 1 else mark(ins)

            def scale_sources(r, heads):
                span = slice(0, heads)
                for i, by in enumerate((1.0 - SLOPE, SLOPE)):
                    nc.vector.tensor_scalar(ks1[:, i, r, span], al1[:, 0, r, span], by, None, ALU.mult)

            dve.wait_ge(vec_in, 176)
            for r in range(REL3):
                for u in range(8):
                    if r and u % 2 == 0:
                        if u == 0:
                            dve.wait_ge(mask_in, 16 * (1 + r))
                        source_columns(al1[:, 0, r - 1, u // 2])
                    split_tile(64 + 8 * r + u, u % 4, u // 4, None,
                               [((acc if v < 4 else vec4)[:, v % 4], al1[:, v // 4, r, v % 4]) for v in range(6)])
                    if r and u % 2 == 1:
                        dve.wait_ge(rows_ready, 64 + 8 * r + u + 1)
                        maxima(45 + 8 * (r - 1) + u + 1, mx1[:, r - 1, u // 2], 9 + 4 * (r - 1) + u // 2 + 1, 84)
                dve.wait_ge(rows_ready, 72 + 8 * r)
                scale_sources(r, HEADS1)
            dve.wait_ge(mask_in, 64)
            for h in range(HEADS1):
                source_columns(al1[:, 0, 2, h], h=h)
            for h, spread in enumerate((64, 66, 68, 69)):
                maxima(spread, mx1[:, 2, h], 18 + h, 84, bank=7 - 2 * (h % 2))
            dve.wait_ge(query_summed, 48)
            mark(nc.vector.tensor_tensor(al1[:, 1, :, 2:4], al_half[:, 0], al_half[:, 1], ALU.add))
            wait_steps()
            relation_uv(HEADS1)
            dve.wait_ge(cnt_in, 64)
            items = relational_items()
            dve.wait_ge(rows_low, 24)

            def start(i):
                h, s, c = items[i]
                if c is None:
                    if s % 4 == 0:
                        dve.wait_ge(vb_ready, 10 + 3 * h + s // 4)
                    exponent(W_AT + i, i % 2, ks1[:, 0, s // 4, h, s % 4:s % 4 + 1], *uv_sets1[(3 * h + s // 4) % 2])
                else:
                    if c == 0:
                        dve.wait_ge(p_used, 12 * (h + 1))
                        denominators(ps[:, 4 + h % 2, :])
                        dve.wait_ge(rd_done, 8 + h + 1)
                    f, part = PIECES[2 * h + c]
                    elu_start(W_AT + i, 48 + 2 * h + c, i % 2, y_ring[i % 3], ps[:, 2 * (h % 2) + c, :],
                              b_cols[part, HEADS0 * KB + f:HEADS0 * KB + f + 1], W_AT + i - 2, part)

            def middle(i):
                h, s, c = items[i]
                if c is None:
                    weigh(W_AT + i, i % 2, y_ring[i % 3], count16[s // 4][:, s % 4, :], before=W_AT + i - 2)
                else:
                    elu_end(W_AT + i, i % 2, y_ring[i % 3], PIECES[2 * h + c][1])

            for i in range(len(items) + 1):
                result_tile = i < len(items) and items[i][2] is not None
                if i < len(items) and not result_tile:
                    start(i)
                if i >= 1:
                    middle(i - 1)
                if result_tile:
                    start(i)

            dve.wait_ge(vec_in, 192)
            for r in range(REL3):
                for u in range(8):
                    if r and u == 0:
                        dve.wait_ge(mask_in, 16 * (4 + r))
                        source_columns(al1[:, 0, r - 1, 0])
                    split_tile(88 + 8 * r + u, u % 4, u // 4, None, [(acc[:, v], al1[:, v, r, 0]) for v in range(2)])
                    if r and u == 1:
                        dve.wait_ge(rows_ready, 88 + 8 * r + u + 1)
                        maxima(94 + 2 * (r - 1) + 1, mx1[:, r - 1, 0], 21 + r, 140)
                dve.wait_ge(rows_ready, 96 + 8 * r)
                scale_sources(r, 1)
            dve.wait_ge(mask_in, 16 * 7)
            source_columns(al1[:, 0, 2, 0])
            maxima(99, mx1[:, 2, 0], 24, 140)
            relation_uv(1)
            dve.wait_ge(rows_low, 48)
            for r in range(REL3):
                dve.wait_ge(vb_ready, 22 + r)
                w0 = 140 + 4 * r
                for s in range(NB + 1):
                    if s < NB:
                        exponent(w0 + s, s % 2, ks1[:, 0, r, 0, s:s + 1], *uv_sets2[r % 2])
                    if 1 <= s <= NB:
                        weigh(w0 + s - 1, (s - 1) % 2, y_ring[(4 * r + s - 1) % 3], count16[r][:, s - 1, :], before=w0 + s - 3)
                if r:
                    read_denominators((106, 107)[r - 1], r == 1)
                    if r == 2:
                        dve.wait_ge(row_read, 16)
                    read_rows(8 * r, r == 1)
            dve.wait_ge(row_read, 24)
            add_bias_to_residual(1)
            read_denominators(108, False)
            invert_denominators(4)
            norm(1, relation_rows)
            dve.wait_ge(acc_ready, 2)
            for m in range(NB):
                split_row(m)

            def count_low(number):
                dve.wait_ge(cnt_hi, number)
                sub(prob[:, 1], cnt16, f32(prob[:, 0])).then_inc(cnt_lo, 1)

            def edge_tiles(number, scale, dst):
                for f in range(KB + 1):
                    t = number * KB + f
                    if f < KB:
                        dve.wait_ge(edge_done, t + 1)
                        if t >= 2:
                            dve.wait_ge(y_lo, t - 1)
                        nc.vector.tensor_tensor(xt[:, f % 2], ps[:, 4 + f % 2, :], scale, ALU.mult).then_inc(y_done, 1)
                    if f >= 1:
                        dve.wait_ge(y_hi, t)
                        sub(dst[:, 1, f - 1, :], xt[:, (f - 1) % 2], f32(dst[:, 0, f - 1, :])).then_inc(y_lo, 1)

            def add_bias(count):
                dve.wait_ge(b_in, 16 * count)
                for m in range(NB):
                    ins = add(acc[:, m, :], acc[:, m, :], b_row)
                    ins.then_inc(b_used, 1) if m == NB - 1 else mark(ins)
                dve.wait_ge(b_used, count)

            added = 72
            for layer in range(3):
                for r in range(REL4):
                    number = 4 * layer + r
                    if number == 0:
                        count_low(1)
                    if layer == 0:
                        dve.wait_ge(misc_done, 108 + r + 1)
                        mark(nc.vector.tensor_scalar(scale_bc[:, r], ps[:, 6, :], 1.0, None, ALU.max))
                        wait_steps()
                        nc.vector.reciprocal(scale_bc[:, r], scale_bc[:, r]).then_inc(scale_ready, 1)
                        dve.wait_ge(scale_ready, r + 1)
                    edge_tiles(number, scale_bc[:, r], cols_y[r % 2])
                    if r == 0:
                        turn(KB * (2 + layer), relu=layer > 0)
                        if layer == 0:
                            dve.wait_ge(kept_out, 32)
                    if number + 1 < 3 * REL4:
                        count_low(number + 2)
                    else:
                        dve.wait_ge(cnt_in, 16 * 17)
                        for m in range(NB):
                            ins = add(cnt16[:, m, m * P:(m + 1) * P], cnt16[:, m, m * P:(m + 1) * P], ident[:])
                        ins.then_inc(diag_added, 1)
                        count_low(13)
                    for u in range(8):
                        if r:
                            dve.wait_ge(acc_added, added)
                        product_tile(44 + 10 * layer + 2 * r, u, into_first=r == 0)
                    added += 8
                dve.wait_ge(acc_added, added)
                if layer < 2:
                    add_bias(3 + layer)
                    for u in range(8):
                        product_tile(52 + 10 * layer, u)
                        if u >= NB:
                            dve.wait_ge(acc_added, added + u + 1)
                            split_row(u - NB, relu=True)
                else:
                    dve.wait_ge(sd_ready, 3)
                    mark(nc.vector.reciprocal(zc[:, 1], zc[:, 0]))
                    nc.vector.reciprocal(v_bc[:], v_bc[:]).then_inc(scale_ready, 1)
                    add_bias_to_residual(2)
                    for m in range(NB):
                        mark(add(acc[:, m, :], acc[:, m, :], resid[:, m, :]))
                    wait_steps()

                    def last_product(u):
                        product_tile(72, u)
                        dve.wait_ge(acc_added, added + u + 1)

                    norm(2, last_product)
                    dve.wait_ge(acc_ready, 3)
                added += 8

            def gcn_tile(u, onto):
                n, m = u // 4, u % 4
                part = slice(n * HW, (n + 1) * HW)
                dve.wait_ge(prod_done, 76 * 4 + (u + 1))
                add(acc[:, m, part], ps[:, m, 0:HW], onto[:, m, part]).then_inc(acc_added, 1)
                dve.wait_ge(acc_added, added + u + 1)

            dve.wait_ge(scale_ready, 5)
            for m in range(NB):
                split_row(m, scaled=True)
            edge_tiles(12, v_bc[:], cols_y[0])
            dve.wait_ge(kept_out, 48)
            dve.wait_ge(b_in, 16 * 6)
            for u in range(8):
                n, m = u // 4, u % 4
                part = slice(n * HW, (n + 1) * HW)
                dve.wait_ge(prod_done, 74 * 4 + (u + 1))
                add(acc[:, m, part], ps[:, m, 0:HW], b_row[:, part]).then_inc(acc_added, 1)
                if n == 1:
                    dve.wait_ge(acc_added, added + u + 1)
                    ins = nc.vector.tensor_scalar(acc[:, m, :], acc[:, m, :], 0.0, zc[:, 1, m:m + 1], ALU.max, ALU.mult)
                    if u == 7:
                        ins.then_inc(b_used, 1)
                        dve.wait_ge(b_used, 6)
                    else:
                        mark(ins)
                        wait_steps()
                    split_row(m)
            added += 8
            edge_tiles(13, v_bc[:], cols_y[0])
            add_bias_to_residual(3)
            norm(3, lambda u: gcn_tile(u, resid))


def kernel(**inputs):
    import concourse.bacc as bacc
    from concourse.bass_utils import run_bass_kernel_spmd

    a = {name: np.ascontiguousarray(value) for name, value in inputs.items()}
    blocks = {}
    first0 = a["L0_gnn_W1"].reshape(D, HEADS0, D)
    second0 = a["L0_gnn_W2"].reshape(HEADS0, D, D)
    order = [first0[:, 0], first0[:, 1]]
    for h in range(HEADS0 - 2):
        order += [first0[:, h + 2], second0[h]]
    order += [second0[6], second0[7], *a["L1_gnn_W1"], *a["L1_gnn_W2"]]
    for i in "123":
        order += [a["L2_gnn_root" + i], *a["L2_gnn_W" + i]]
    order += [a["L3_gnn_W1"], a["L3_gnn_W2"]]
    weights = np.stack(order).reshape(WEIGHT_BLOCKS, 3, 2, P, 2, HW).transpose(0, 4, 1, 3, 2, 5)
    arrays = {
        "edges": np.stack([a["src"], a["dst"], a["edge_type_3"], a["edge_type_4"]]).reshape(4, P, CH).transpose(1, 0, 2),
        "x_rows": a["x"].reshape(NB, P, D).transpose(1, 0, 2),
        "weights": weights.reshape(2 * WEIGHT_BLOCKS, 3, P, 2 * HW),
        "attn0": np.stack([np.concatenate([a["L0_gnn_a_src1"], a["L0_gnn_a_src2"]]),
                           np.concatenate([a["L0_gnn_a_dst1"], a["L0_gnn_a_dst2"]])], 1),
        "attn1": np.stack([a["L1_gnn_k1"].T, a["L1_gnn_q1"].T]),
        "attn2": np.stack([a["L1_gnn_k2"].T, a["L1_gnn_q2"].T], 1),
        "bias_cols": np.concatenate([a["L0_gnn_b1"], a["L1_gnn_b1"]]).reshape(HEADS0 * KB + KB, P).T,
        "bias_rows": np.stack([a[n] for n in ("L0_gnn_b2", "L1_gnn_b2", "L2_gnn_b1", "L2_gnn_b2", "L2_gnn_b3",
                                              "L3_gnn_b1", "L3_gnn_b2")]),
    }
    arrays = {name: np.ascontiguousarray(value) for name, value in arrays.items()}

    nc = bacc.Bacc("TRN2", target_bir_lowering=False, num_devices=1)
    dram = {name: nc.dram_tensor(name, v.shape, mybir.dt.from_np(v.dtype), kind="ExternalInput").ap()
            for name, v in arrays.items()}
    out = nc.dram_tensor("out", [P, NB, D], F32, kind="ExternalOutput").ap()
    counts = nc.dram_tensor("counts", [8, P, NB, N], I16).ap()
    masks = nc.dram_tensor("masks", [4, P, NB, N], BF16).ap()
    flag = nc.dram_tensor("flag", [1, 1], I32).ap()
    kept = nc.dram_tensor("kept", [P, NB, D], F32).ap()
    with ExitStack() as ctx:
        shared = early_loads(nc, ctx)
        count_edges(nc, shared, dram["x_rows"], dram["weights"], dram["edges"], counts, masks, flag)
        graph_layers(nc, shared, dram["x_rows"], dram["weights"], dram["attn0"], dram["attn1"], dram["attn2"],
                     dram["bias_cols"], dram["bias_rows"], counts, masks, flag, kept, out)
    got = run_bass_kernel_spmd(nc, [arrays], core_ids=[0]).results[0]["out"]
    return got.reshape(P, NB, D).transpose(1, 0, 2).reshape(N, D)
```
